# Optimizing a Trainium2 kernel written in Bass

```python
import numpy as np
import jax
import jax.numpy as jnp

def _softmax(x, axis=-1):
    return jax.nn.softmax(x, axis=axis)

def _gelu(x):
    return jax.nn.gelu(x, approximate=True)

def _silu(x):
    return jax.nn.silu(x)

def _sigmoid(x):
    return jax.nn.sigmoid(x)

def _layernorm(x, axis=-1, eps=1e-05):
    m = jnp.mean(x, axis=axis, keepdims=True)
    v = jnp.var(x, axis=axis, keepdims=True)
    return (x - m) / jnp.sqrt(v + eps)

def _scatter_add(tgt, idx, src, axis=0):
    return tgt.at[idx].add(src)

def _segment_sum(src, seg, n):
    return jax.ops.segment_sum(src, seg, n)
kernel_name = 'mk_gnn_preln_d4_gnn_r8_c24543'

def setup_inputs(seed: int=0):
    np.random.seed(seed)
    _w = jnp.asarray

    def _rec_inputs():
        import jax
        import jax.numpy as jnp
        _gk = jax.random.key(seed)
        x = -0.000202 + 1 * jax.random.normal(jax.random.fold_in(_gk, 1), (6250, 64), jnp.float32)
        src = jax.random.randint(jax.random.fold_in(_gk, 2), (200000,), 0, 6250, jnp.int32)
        dst = jnp.minimum((6250 * jax.random.uniform(jax.random.fold_in(_gk, 3), (200000,)) ** 2.0).astype(jnp.int32), 49999)
        _o = jnp.argsort(dst, stable=True)
        src = src[_o]
        dst = dst[_o]
        edge_attr_32 = -5.3897e-05 + 0.999841 * jax.random.normal(jax.random.fold_in(_gk, 12), (200000, 32), jnp.float32)
        edge_weight = jax.random.uniform(jax.random.fold_in(_gk, 15), (200000,), jnp.float32, 0.0, 0.999998)
        return (x, src, dst, edge_attr_32, edge_weight)
    x, src, dst, edge_attr_32, edge_weight = _rec_inputs()

    def _L0_gnn_setup():
        import jax, jax.numpy as jnp
        import numpy as np
        N_NODES = 12500
        N_EDGES = 200000
        D_IN = 64
        D_OUT = 64
        D_HID = 64

        def _init_linear(key, fan_in, fan_out):
            kw, kb = jax.random.split(key)
            bound = 1.0 / np.sqrt(fan_in)
            w = jax.random.uniform(kw, (fan_in, fan_out), jnp.float32, -bound, bound)
            b = jax.random.uniform(kb, (fan_out,), jnp.float32, -bound, bound)
            return (w, b)
        key = jax.random.key(seed)
        ks = jax.random.split(key, 10)
        x = jax.random.normal(ks[0], (N_NODES, D_IN), jnp.float32)
        edge_index = jax.random.randint(ks[1], (2, N_EDGES), 0, N_NODES, jnp.int64)
        pw1, pb1 = _init_linear(ks[2], D_IN, D_HID)
        pw2, pb2 = _init_linear(ks[3], D_HID, D_OUT)
        fw1, fb1 = _init_linear(ks[4], D_IN, D_HID)
        fw2, fb2 = _init_linear(ks[5], D_HID, D_OUT)
        cw1, cb1 = _init_linear(ks[6], 2 * D_IN, D_HID)
        cw2, cb2 = _init_linear(ks[7], D_HID, 1)
        ow1, ob1 = _init_linear(ks[8], D_OUT, D_HID)
        ow2, ob2 = _init_linear(ks[9], D_HID, D_OUT)
        return {'x': x, 'edge_index': edge_index, 'pw1': pw1, 'pb1': pb1, 'pw2': pw2, 'pb2': pb2, 'fw1': fw1, 'fb1': fb1, 'fw2': fw2, 'fb2': fb2, 'cw1': cw1, 'cb1': cb1, 'cw2': cw2, 'cb2': cb2, 'ow1': ow1, 'ob1': ob1, 'ow2': ow2, 'ob2': ob2}
    _L0_gnn_all = _L0_gnn_setup()
    _L0_gnn_in = {k: v for k, v in _L0_gnn_all.items() if k in ('pw1', 'pb1', 'pw2', 'pb2', 'fw1', 'fb1', 'fw2', 'fb2', 'cw1', 'cb1', 'cw2', 'cb2', 'ow1', 'ob1', 'ow2', 'ob2')}
    del _L0_gnn_all

    def _L1_gnn_setup():
        import jax, jax.numpy as jnp
        import numpy as np
        N_NODES = 6250
        N_EDGES = 100000
        D_NODE = 64
        D_EDGE = 32
        H_MSG = (2 * D_NODE + D_EDGE) // 2
        H_CMB = 3 * D_NODE // 2

        def _gelu(x):
            return jax.nn.gelu(x, approximate=False)
        key = jax.random.key(seed)
        ks = jax.random.split(key, 11)

        def lin(k, fan_in, fan_out):
            bound = 1.0 / np.sqrt(fan_in)
            k1, k2 = jax.random.split(k)
            W = jax.random.uniform(k1, (fan_in, fan_out), jnp.float32, -bound, bound)
            b = jax.random.uniform(k2, (fan_out,), jnp.float32, -bound, bound)
            return (W, b)
        node_vectors = jax.random.normal(ks[0], (N_NODES, D_NODE), jnp.float32)
        edge_vectors = jax.random.normal(ks[1], (N_EDGES, D_EDGE), jnp.float32)
        edge_indices = jax.random.randint(ks[2], (N_EDGES, 2), 0, N_NODES, jnp.int64 if jax.config.jax_enable_x64 else jnp.int32)
        W_m1, b_m1 = lin(ks[3], 2 * D_NODE + D_EDGE, H_MSG)
        W_m2, b_m2 = lin(ks[4], H_MSG, D_NODE)
        W_c1, b_c1 = lin(ks[5], 2 * D_NODE, H_CMB)
        W_c2, b_c2 = lin(ks[6], H_CMB, D_NODE)
        return {'node_vectors': node_vectors, 'edge_vectors': edge_vectors, 'edge_indices': edge_indices, 'W_m1': W_m1, 'b_m1': b_m1, 'W_m2': W_m2, 'b_m2': b_m2, 'W_c1': W_c1, 'b_c1': b_c1, 'W_c2': W_c2, 'b_c2': b_c2}
    _L1_gnn_all = _L1_gnn_setup()
    _L1_gnn_in = {k: v for k, v in _L1_gnn_all.items() if k in ('W_m1', 'b_m1', 'W_m2', 'b_m2', 'W_c1', 'b_c1', 'W_c2', 'b_c2')}
    del _L1_gnn_all

    def _L2_gnn_setup():
        import jax, jax.numpy as jnp
        import numpy as np
        EPS = 1e-05

        def gcn_conv(x, W, b, src, dst, ew, num_nodes):
            deg = jax.ops.segment_sum(ew, dst, num_segments=num_nodes) + 1.0
            dinv = jax.lax.rsqrt(deg)
            norm = dinv[src] * ew * dinv[dst]
            h = x @ W
            msg = norm[:, None] * h[src]
            agg = jax.ops.segment_sum(msg, dst, num_segments=num_nodes)
            agg = agg + h * (1.0 / deg)[:, None]
            return agg + b

        def batchnorm(h, gamma, beta):
            mean = jnp.mean(h, axis=0)
            var = jnp.mean(jnp.square(h - mean), axis=0)
            return (h - mean) * jax.lax.rsqrt(var + EPS) * gamma + beta
        key = jax.random.key(seed)
        ks = jax.random.split(key, 8)
        N, E, F = (6250, 100000, 64)
        x = jax.random.normal(ks[0], (N, F), dtype=jnp.float32)
        edge_index = jax.random.randint(ks[1], (2, E), 0, N, dtype=jnp.int64)
        edge_weight = jax.random.uniform(ks[2], (E,), dtype=jnp.float32)
        s = 1.0 / np.sqrt(F)
        W1 = jax.random.uniform(ks[3], (F, F), jnp.float32, -s, s)
        b1 = jnp.zeros((F,), jnp.float32)
        W2 = jax.random.uniform(ks[4], (F, F), jnp.float32, -s, s)
        b2 = jnp.zeros((F,), jnp.float32)
        gamma1 = jnp.ones((F,), jnp.float32)
        beta1 = jnp.zeros((F,), jnp.float32)
        gamma2 = jnp.ones((F,), jnp.float32)
        beta2 = jnp.zeros((F,), jnp.float32)
        return {'x': x, 'edge_index': edge_index, 'edge_weight': edge_weight, 'W1': W1, 'b1': b1, 'gamma1': gamma1, 'beta1': beta1, 'W2': W2, 'b2': b2, 'gamma2': gamma2, 'beta2': beta2}
    _L2_gnn_all = _L2_gnn_setup()
    _L2_gnn_in = {k: v for k, v in _L2_gnn_all.items() if k in ('W1', 'b1', 'gamma1', 'beta1', 'W2', 'b2', 'gamma2', 'beta2')}
    del _L2_gnn_all

    def _L3_gnn_setup():
        import jax, jax.numpy as jnp
        import numpy as np
        N_NODES = 12500
        N_EDGES = 200000
        D = 64

        def _ngcf_conv(x, W1, W2, src, dst, n_nodes):
            ones = jnp.ones(src.shape[0], dtype=x.dtype)
            deg_out = jnp.clip(jax.ops.segment_sum(ones, src, num_segments=n_nodes), 1.0)
            deg_in = jnp.clip(jax.ops.segment_sum(ones, dst, num_segments=n_nodes), 1.0)
            norm = jax.lax.rsqrt(deg_out[src] * deg_in[dst])
            h_src = x[src]
            h_dst = x[dst]
            msg = (h_src @ W1 + h_src * h_dst @ W2) * norm[:, None]
            agg = jax.ops.segment_sum(msg, dst, num_segments=n_nodes)
            return x @ W1 + agg
        key = jax.random.key(seed)
        ks = jax.random.split(key, 8)
        s = 1.0 / np.sqrt(D)
        return {'x': jax.random.normal(ks[0], (N_NODES, D), dtype=jnp.float32), 'edge_src': jax.random.randint(ks[1], (N_EDGES,), 0, N_NODES, dtype=jnp.int32), 'edge_dst': jax.random.randint(ks[2], (N_EDGES,), 0, N_NODES, dtype=jnp.int32), 'W1_1': jax.random.normal(ks[3], (D, D), dtype=jnp.float32) * s, 'W2_1': jax.random.normal(ks[4], (D, D), dtype=jnp.float32) * s, 'W1_2': jax.random.normal(ks[5], (D, D), dtype=jnp.float32) * s, 'W2_2': jax.random.normal(ks[6], (D, D), dtype=jnp.float32) * s}
    _L3_gnn_all = _L3_gnn_setup()
    _L3_gnn_in = {k: v for k, v in _L3_gnn_all.items() if k in ('W1_1', 'W2_1', 'W1_2', 'W2_2')}
    del _L3_gnn_all
    return {'x': x, 'src': src, 'dst': dst, 'edge_attr_32': edge_attr_32, 'edge_weight': edge_weight, 'L0_gnn_pw1': _L0_gnn_in['pw1'], 'L0_gnn_pb1': _L0_gnn_in['pb1'], 'L0_gnn_pw2': _L0_gnn_in['pw2'], 'L0_gnn_pb2': _L0_gnn_in['pb2'], 'L0_gnn_fw1': _L0_gnn_in['fw1'], 'L0_gnn_fb1': _L0_gnn_in['fb1'], 'L0_gnn_fw2': _L0_gnn_in['fw2'], 'L0_gnn_fb2': _L0_gnn_in['fb2'], 'L0_gnn_cw1': _L0_gnn_in['cw1'], 'L0_gnn_cb1': _L0_gnn_in['cb1'], 'L0_gnn_cw2': _L0_gnn_in['cw2'], 'L0_gnn_cb2': _L0_gnn_in['cb2'], 'L0_gnn_ow1': _L0_gnn_in['ow1'], 'L0_gnn_ob1': _L0_gnn_in['ob1'], 'L0_gnn_ow2': _L0_gnn_in['ow2'], 'L0_gnn_ob2': _L0_gnn_in['ob2'], 'L1_gnn_W_m1': _L1_gnn_in['W_m1'], 'L1_gnn_b_m1': _L1_gnn_in['b_m1'], 'L1_gnn_W_m2': _L1_gnn_in['W_m2'], 'L1_gnn_b_m2': _L1_gnn_in['b_m2'], 'L1_gnn_W_c1': _L1_gnn_in['W_c1'], 'L1_gnn_b_c1': _L1_gnn_in['b_c1'], 'L1_gnn_W_c2': _L1_gnn_in['W_c2'], 'L1_gnn_b_c2': _L1_gnn_in['b_c2'], 'L2_gnn_W1': _L2_gnn_in['W1'], 'L2_gnn_b1': _L2_gnn_in['b1'], 'L2_gnn_gamma1': _L2_gnn_in['gamma1'], 'L2_gnn_beta1': _L2_gnn_in['beta1'], 'L2_gnn_W2': _L2_gnn_in['W2'], 'L2_gnn_b2': _L2_gnn_in['b2'], 'L2_gnn_gamma2': _L2_gnn_in['gamma2'], 'L2_gnn_beta2': _L2_gnn_in['beta2'], 'L3_gnn_W1_1': _L3_gnn_in['W1_1'], 'L3_gnn_W2_1': _L3_gnn_in['W2_1'], 'L3_gnn_W1_2': _L3_gnn_in['W1_2'], 'L3_gnn_W2_2': _L3_gnn_in['W2_2']}

def reference(x, src, dst, edge_attr_32, edge_weight, L0_gnn_pw1, L0_gnn_pb1, L0_gnn_pw2, L0_gnn_pb2, L0_gnn_fw1, L0_gnn_fb1, L0_gnn_fw2, L0_gnn_fb2, L0_gnn_cw1, L0_gnn_cb1, L0_gnn_cw2, L0_gnn_cb2, L0_gnn_ow1, L0_gnn_ob1, L0_gnn_ow2, L0_gnn_ob2, L1_gnn_W_m1, L1_gnn_b_m1, L1_gnn_W_m2, L1_gnn_b_m2, L1_gnn_W_c1, L1_gnn_b_c1, L1_gnn_W_c2, L1_gnn_b_c2, L2_gnn_W1, L2_gnn_b1, L2_gnn_gamma1, L2_gnn_beta1, L2_gnn_W2, L2_gnn_b2, L2_gnn_gamma2, L2_gnn_beta2, L3_gnn_W1_1, L3_gnn_W2_1, L3_gnn_W1_2, L3_gnn_W2_2):
    import jax
    import jax.numpy as jnp

    def _L0_gnn_ref(x, edge_index, pw1, pb1, pw2, pb2, fw1, fb1, fw2, fb2, cw1, cb1, cw2, cb2, ow1, ob1, ow2, ob2):
        import jax, jax.numpy as jnp
        import numpy as np
        N_NODES = 12500
        N_EDGES = 200000
        D_IN = 64
        D_OUT = 64
        D_HID = 64

        def _init_linear(key, fan_in, fan_out):
            kw, kb = jax.random.split(key)
            bound = 1.0 / np.sqrt(fan_in)
            w = jax.random.uniform(kw, (fan_in, fan_out), jnp.float32, -bound, bound)
            b = jax.random.uniform(kb, (fan_out,), jnp.float32, -bound, bound)
            return (w, b)
        num_nodes = x.shape[0]
        phases = jnp.tanh(x @ pw1 + pb1) @ pw2 + pb2
        freqs = jax.nn.relu(x @ fw1 + fb1) @ fw2 + fb2
        src = edge_index[0]
        tgt = edge_index[1]
        ef = jnp.concatenate([x[tgt], x[src]], axis=-1)
        k = jax.nn.sigmoid(jax.nn.relu(ef @ cw1 + cb1) @ cw2 + cb2)
        msg = k * jnp.sin(phases[src] - phases[tgt])
        agg = jax.ops.segment_sum(msg, tgt, num_segments=num_nodes)
        phase_derivatives = freqs + agg
        out = jax.nn.relu(phase_derivatives @ ow1 + ob1) @ ow2 + ob2
        return out

    def _L1_gnn_ref(node_vectors, edge_vectors, edge_indices, W_m1, b_m1, W_m2, b_m2, W_c1, b_c1, W_c2, b_c2):
        import jax, jax.numpy as jnp
        import numpy as np
        N_NODES = 6250
        N_EDGES = 100000
        D_NODE = 64
        D_EDGE = 32
        H_MSG = (2 * D_NODE + D_EDGE) // 2
        H_CMB = 3 * D_NODE // 2

        def _gelu(x):
            return jax.nn.gelu(x, approximate=False)
        node_i = node_vectors[edge_indices[:, 0]]
        node_j = node_vectors[edge_indices[:, 1]]
        msg_input = jnp.concatenate([node_i, node_j, edge_vectors], axis=1)
        h = _gelu(msg_input @ W_m1 + b_m1)
        messages = _gelu(h @ W_m2 + b_m2)
        boxes = jax.ops.segment_sum(messages, edge_indices[:, 1], num_segments=node_vectors.shape[0])
        pairs = jnp.concatenate([node_vectors, boxes], axis=1)
        c = _gelu(pairs @ W_c1 + b_c1)
        combined = _gelu(c @ W_c2 + b_c2)
        return node_vectors + combined

    def _L2_gnn_ref(x, edge_index, edge_weight, W1, b1, gamma1, beta1, W2, b2, gamma2, beta2):
        import jax, jax.numpy as jnp
        import numpy as np
        EPS = 1e-05

        def gcn_conv(x, W, b, src, dst, ew, num_nodes):
            deg = jax.ops.segment_sum(ew, dst, num_segments=num_nodes) + 1.0
            dinv = jax.lax.rsqrt(deg)
            norm = dinv[src] * ew * dinv[dst]
            h = x @ W
            msg = norm[:, None] * h[src]
            agg = jax.ops.segment_sum(msg, dst, num_segments=num_nodes)
            agg = agg + h * (1.0 / deg)[:, None]
            return agg + b

        def batchnorm(h, gamma, beta):
            mean = jnp.mean(h, axis=0)
            var = jnp.mean(jnp.square(h - mean), axis=0)
            return (h - mean) * jax.lax.rsqrt(var + EPS) * gamma + beta
        N = x.shape[0]
        src, dst = (edge_index[0], edge_index[1])
        identity = x
        out = gcn_conv(x, W1, b1, src, dst, edge_weight, N)
        out = jax.nn.relu(batchnorm(out, gamma1, beta1))
        out = gcn_conv(out, W2, b2, src, dst, edge_weight, N)
        out = batchnorm(out, gamma2, beta2)
        out = out + identity
        return jax.nn.relu(out)

    def _L3_gnn_ref(x, edge_src, edge_dst, W1_1, W2_1, W1_2, W2_2):
        import jax, jax.numpy as jnp
        import numpy as np
        N_NODES = 12500
        N_EDGES = 200000
        D = 64

        def _ngcf_conv(x, W1, W2, src, dst, n_nodes):
            ones = jnp.ones(src.shape[0], dtype=x.dtype)
            deg_out = jnp.clip(jax.ops.segment_sum(ones, src, num_segments=n_nodes), 1.0)
            deg_in = jnp.clip(jax.ops.segment_sum(ones, dst, num_segments=n_nodes), 1.0)
            norm = jax.lax.rsqrt(deg_out[src] * deg_in[dst])
            h_src = x[src]
            h_dst = x[dst]
            msg = (h_src @ W1 + h_src * h_dst @ W2) * norm[:, None]
            agg = jax.ops.segment_sum(msg, dst, num_segments=n_nodes)
            return x @ W1 + agg
        n = x.shape[0]
        h = _ngcf_conv(x, W1_1, W2_1, edge_src, edge_dst, n)
        h = jax.nn.relu(h)
        h = _ngcf_conv(h, W1_2, W2_2, edge_src, edge_dst, n)
        return h
    edge_index = jnp.stack([src, dst])
    edge_index_t = jnp.stack([src, dst], axis=1)
    h = jnp.maximum(_layernorm(x, axis=-1), 0.0)
    x = x + _L0_gnn_ref(h, edge_index, L0_gnn_pw1, L0_gnn_pb1, L0_gnn_pw2, L0_gnn_pb2, L0_gnn_fw1, L0_gnn_fb1, L0_gnn_fw2, L0_gnn_fb2, L0_gnn_cw1, L0_gnn_cb1, L0_gnn_cw2, L0_gnn_cb2, L0_gnn_ow1, L0_gnn_ob1, L0_gnn_ow2, L0_gnn_ob2)
    h = jnp.maximum(_layernorm(x, axis=-1), 0.0)
    x = x + _L1_gnn_ref(h, edge_attr_32, edge_index_t, L1_gnn_W_m1, L1_gnn_b_m1, L1_gnn_W_m2, L1_gnn_b_m2, L1_gnn_W_c1, L1_gnn_b_c1, L1_gnn_W_c2, L1_gnn_b_c2)
    h = jnp.maximum(_layernorm(x, axis=-1), 0.0)
    x = x + _L2_gnn_ref(h, edge_index, edge_weight, L2_gnn_W1, L2_gnn_b1, L2_gnn_gamma1, L2_gnn_beta1, L2_gnn_W2, L2_gnn_b2, L2_gnn_gamma2, L2_gnn_beta2)
    h = jnp.maximum(_layernorm(x, axis=-1), 0.0)
    x = x + _L3_gnn_ref(h, src, dst, L3_gnn_W1_1, L3_gnn_W2_1, L3_gnn_W1_2, L3_gnn_W2_2)
    return x

_drawn_inputs = setup_inputs


def setup_inputs(seed=0):
    import zlib

    import numpy as np

    out = dict(_drawn_inputs(seed))
    spreads = {'L2_gnn_b1': (0.0, 2.0),
     'L2_gnn_gamma1': (1.0, 0.2),
     'L2_gnn_beta1': (0.0, 0.295),
     'L2_gnn_b2': (0.0, 2.0),
     'L2_gnn_gamma2': (1.0, 0.2),
     'L2_gnn_beta2': (0.0, 0.377)}
    factors = {'edge_attr_32': 6.773,
     'L0_gnn_pb1': 4.002,
     'L0_gnn_pb2': 64.0,
     'L0_gnn_fb1': 8.0,
     'L0_gnn_fb2': 4.019,
     'L0_gnn_cb1': 8.0,
     'L1_gnn_b_m1': 2.984,
     'L1_gnn_b_c1': 8.0,
     'L1_gnn_b_c2': 3.57}
    for name, (base, spread) in spreads.items():
        noise = np.random.default_rng([zlib.crc32(name.encode()), seed]).standard_normal(out[name].shape)
        drawn = base * np.exp(spread * noise) if base else spread * noise
        out[name] = jnp.asarray(drawn.astype(out[name].dtype))
    for name, factor in factors.items():
        out[name] = (out[name] * factor).astype(out[name].dtype)
    return out
```

```python
from contextlib import ExitStack

import concourse.bass as bass
from concourse import mybir

F32 = mybir.dt.float32
I32 = mybir.dt.int32
BF16 = mybir.dt.bfloat16
ALU = mybir.AluOpType
ACT = mybir.ActivationFunctionType
AX = mybir.AxisListType.X

P = 128
N = 6250
E = 200000
D = 64
DE = 32
NT = -(-N // P)
NP = NT * P
WIN = 64
NW = NP + WIN
J = 4
GE = J * P
U = 4
NG = -(-E // (GE * U)) * U
EP = NG * GE
TURNS = NG // U
HM = 80
HC = 96
CH = 512
NCH = -(-NP // CH)
AHEAD = 4
EPS = 1e-5
PI = 3.141592653589793
TWO_PI_HI = 6.28125
TWO_PI_LO = 2.0 * PI - TWO_PI_HI
ROUND_MAGIC = 12582912.0
PI_BELOW = 3.1415925
NO_TARGET = 1 << 20


def chunk(c):
    return c * CH, min(CH, NP - c * CH)


def ds(start, size):
    return bass.ds(start, size)


def bc(ap, shape):
    return ap.to_broadcast(shape)


class Memory:

    def __init__(self, nc, ctx):
        def sb(name, shape, dt=F32):
            return ctx.enter_context(nc.sbuf_tensor(name, shape, dt))

        self.big = sb("node_arrays", [P, 6 * NW])
        r = [self.big[:, k * NW:(k + 1) * NW] for k in range(6)]
        self.A, self.B, self.C, self.D, self.E, self.F = r
        self.DE = self.big[:, 3 * NW:5 * NW]
        self.x = sb("x_nodes", [P, NT, D])
        self.src = sb("src_ids", [P, (NG + U) * J], I32)
        self.ew = sb("edge_weights", [P, NG * J])
        self.dstrel = sb("target_in_window", [P, NG, J])
        self.nodeid = sb("window_node_ids", [WIN, NG])
        self.base_i = sb("window_base", [1, NG], I32)
        self.edw = sb("degree_rows", [P, 2, J, P])
        self.onehot = sb("onehot", [P, 2, J, WIN])
        self.hi1 = sb("onehot_src_tile", [P, 2, J, WIN], BF16)
        self.lo1 = sb("onehot_src_row", [P, 2, J, P], BF16)
        self.idx = sb("gather_ids", [P, U, J], I32)
        self.ident = sb("identity", [P, P])
        self.iota = sb("iota_free", [P, P])
        self.iotap = sb("iota_partition", [P, 1])
        self.stat = sb("node_stats", [P, 4, NT])
        self.col = sb("channel_stats", [P, 16])
        self.kgate = sb("gates", [P, 2, J])
        self.zsum = sb("gate_inputs", [P, 2, J])
        self.ps = [ctx.enter_context(nc.psum_tensor(f"bank{k}", [P, CH], F32)) for k in range(8)]

        self.H = self.F[:, 0:NT * D].rearrange("p (t f) -> p t f", f=D)
        self.TAB = self.F[:, NW // 2:NW // 2 + NT * D].rearrange("p (t f) -> p t f", f=D)
        self.hilo = self.F[:, NW // 2:NW // 2 + NG * J * 2 // 2]

    def carve(self, region, sizes):
        out, at = [], 0
        for parts, *shape in sizes:
            n = 1
            for s in shape:
                n *= s
            piece = region[0:parts, at:at + n]
            if len(shape) == 2:
                piece = piece.rearrange("p (a b) -> p a b", b=shape[1])
            elif len(shape) == 3:
                piece = piece.rearrange("p (a b c) -> p a b c", b=shape[1], c=shape[2])
            out.append(piece)
            at += n
        assert at <= NW, at
        return out


class Chain:

    def __init__(self, eng, sem):
        self.eng, self.sem, self.n = eng, sem, 0

    def __call__(self, ins):
        self.n += 1
        ins.then_inc(self.sem, 1)
        self.eng.wait_ge(self.sem, self.n)


class Stage:

    def __init__(self, nc, name):
        self.nc, self.name, self.all, self.kept = nc, name, [], []
        self.ctx = ExitStack()

    def sem(self, name):
        s = self.ctx.enter_context(self.nc.semaphore(f"{self.name}_{name}"))
        self.all.append(s)
        return s

    def keep(self, sems):
        self.all += sems
        self.kept = sems
        return sems

    def close(self):
        kept = sorted(s.num for s in self.kept)
        if kept:
            self.nc.gpsimd.dma_reset(range(kept[0], kept[-1] + 1))
        for s in self.all:
            self.nc.gpsimd.sem_clear(s)
        self.nc.all_engine_barrier()
        self.ctx.close()


def rows_of(table, cols):
    return table[0:NP, cols[0]:cols[1]].rearrange("(t p) f -> p t f", p=P)




def setup(nc, m, w, ins, dr):
    st = Stage(nc, "setup")
    loads, consts, idz, mins, sent, back, dve, loaded_bases, rounds_ready = (
        st.sem(n) for n in ("loads", "consts", "ident_zero", "mins", "sent", "back", "dve", "bases", "rounds"))
    rows_in, zero_out = st.sem("rows_in"), st.sem("zero_out")
    per = NG // 98
    rows = m.A[0:98, 0:per * GE].bitcast(I32).rearrange("p (c e) -> p c e", e=GE)
    inside = m.B[0:98, 0:per * GE].rearrange("p (c e) -> p c e", e=GE)
    least, most, reach = m.C[0:98, 0:per], m.C[0:98, 8:8 + per], m.C[0:98, 16:16 + per]
    least_i = m.C[0:98, 24:24 + per].bitcast(I32)
    reach_row = m.C[0:1, 512:512 + NG]
    far = m.C[0:1, 1024:1028]
    far_i = m.C[0:1, 1032:1034].bitcast(I32)
    n_loads = len(ins["loads"]) + 3
    with nc.Block() as block:
        @block.sync
        def _(sp):
            sp.dma_start(rows, ins["dst_rows"].rearrange("(p c) e -> p c e", c=per)).then_inc(rows_in, 16)
            sp.dma_start(m.x[:], ins["x"].rearrange("(t p) f -> p t f", p=P)).then_inc(loads, 16)
            sp.dma_start(m.src[:, 0:NG * J], ins["src_t"]).then_inc(loads, 16)
            sp.dma_start(m.ew[:], ins["ew_t"]).then_inc(loads, 16)
            for to, what in ins["loads"]:
                sp.dma_start(to, what).then_inc(loads, 16)
            sp.wait_ge(mins, 1)
            sp.dma_start(dr["base_f"].rearrange("a (p c) -> (a p) c", c=per), least).then_inc(sent, 16)
            sp.dma_start(dr["base_i"].rearrange("a (p c) -> (a p) c", c=per), least_i).then_inc(sent, 16)
            sp.dma_start(dr["reach"].rearrange("a (p c) -> (a p) c", c=per), reach).then_inc(sent, 16)
            sp.wait_ge(sent, 48)
            sp.dma_start(reach_row, dr["reach"]).then_inc(back, 16)
            sp.wait_ge(consts, 3)
            for t, width in ((dr["tgt0"], D), (dr["tgt1"], HM)):
                sp.dma_start(t[NP:NW, :], m.E[0:WIN, 0:width]).then_inc(zero_out, 16)
            sp.wait_ge(zero_out, 32)
            sp.wait_ge(loads, 16 * n_loads)

        @block.gpsimd
        def _(pool):
            nc.gpsimd.memset(m.ident[:], 0.0).then_inc(idz, 1)
            nc.gpsimd.iota(m.iota[:], [[1, P]], base=0, channel_multiplier=0,
                           allow_small_or_imprecise_dtypes=True).then_inc(consts, 1)
            nc.gpsimd.iota(m.iotap[:], [[1, 1]], base=0, channel_multiplier=1,
                           allow_small_or_imprecise_dtypes=True).then_inc(consts, 1)
            pool.wait_ge(idz, 1)
            nc.gpsimd.affine_select(out=m.ident[:], in_=m.ident[:], compare_op=ALU.not_equal, fill=1.0,
                                    base=0, pattern=[[-1, P]], channel_multiplier=1).then_inc(idz, 1)
            pool.wait_ge(idz, 2)

        @block.vector
        def _(v):
            step = Chain(v, dve)
            nc.vector.memset(m.E[0:WIN, 0:P], 0.0).then_inc(consts, 1)
            step(nc.vector.memset(m.src[:, NG * J:], 0))
            step(nc.vector.memset(m.edw[:], 1.0))
            v.wait_ge(rows_in, 16)
            step(nc.vector.tensor_reduce(out=least, in_=rows, axis=AX, op=ALU.min))
            step(nc.vector.scalar_tensor_tensor(out=inside, in0=rows, scalar=float(N), in1=rows,
                                                op0=ALU.is_lt, op1=ALU.mult))
            step(nc.vector.tensor_reduce(out=most, in_=inside, axis=AX, op=ALU.max))
            step(nc.vector.tensor_scalar(least, least, float(N), None, ALU.min))
            step(nc.vector.tensor_copy(least_i, least))
            nc.vector.scalar_tensor_tensor(out=reach, in0=least, scalar=-1.0, in1=most,
                                           op0=ALU.mult, op1=ALU.add).then_inc(mins, 1)
            v.wait_ge(back, 16)
            step(nc.vector.tensor_reduce(out=far[:, 0:1], in_=reach_row, axis=AX, op=ALU.max))
            step(nc.vector.tensor_scalar(far[:, 1:2], far[:, 0:1], 0.0, None, ALU.max))
            step(nc.vector.tensor_copy(far_i[:, 0:1], far[:, 1:2]))
            step(nc.vector.tensor_single_scalar(far_i[:, 1:2], far_i[:, 0:1], WIN.bit_length() - 1,
                                                op=ALU.arith_shift_right))
            step(nc.vector.tensor_copy(far[:, 2:3], far_i[:, 1:2]))
            step(nc.vector.tensor_scalar(far[:, 3:4], far[:, 2:3], 1.0, None, ALU.add))
            step(nc.vector.tensor_copy(m.rounds[:], far[:, 3:4]))
    st.close()
    with nc.Block() as block:
        @block.vector
        def _(v):
            pass
    return nc.values_load(m.rounds[0:1, 0:1], min_val=1, max_val=-(-N // WIN))




class Nodes:

    def __init__(self, nc, m, st, scratch):
        self.nc, self.m, self.scratch = nc, m, scratch
        self.chain, self.var, self.std, self.h = (st.sem(n) for n in ("ln_dve", "ln_var", "ln_std", "ln_h"))
        self.turned, self.stored = st.sem("h_turned"), st.sem("hT_stored")

    def vector(self, v):
        nc, m = self.nc, self.m
        step = Chain(v, self.chain)
        mean, var, std, rstd = (m.stat[:, k, :] for k in range(4))
        scr = self.scratch[:, 0:NT * D].rearrange("p (t f) -> p t f", f=D)
        wide = [P, NT, D]
        step(nc.vector.tensor_reduce(out=mean, in_=m.x[:], axis=AX, op=ALU.add))
        step(nc.vector.tensor_scalar(mean, mean, 1.0 / D, None, ALU.mult))
        step(nc.vector.tensor_tensor(m.H, m.x[:], bc(mean.unsqueeze(2), wide), ALU.subtract))
        step(nc.vector.tensor_tensor(scr, m.H, m.H, ALU.mult))
        step(nc.vector.tensor_reduce(out=var, in_=scr, axis=AX, op=ALU.add))
        nc.vector.tensor_scalar(var, var, 1.0 / D, EPS, ALU.mult, ALU.add).then_inc(self.var, 1)
        v.wait_ge(self.std, 1)
        step(nc.vector.reciprocal(rstd, std))
        nc.vector.scalar_tensor_tensor(out=m.H, in0=m.H, scalar=0.0, in1=bc(rstd.unsqueeze(2), wide),
                                       op0=ALU.max, op1=ALU.mult).then_inc(self.h, 1)

    def scalar(self, act):
        nc, m = self.nc, self.m
        act.wait_ge(self.var, 1)
        nc.scalar.activation(m.stat[:, 2, :], m.stat[:, 1, :], ACT.Sqrt).then_inc(self.std, 1)
        for c in range(NCH):
            lo, n = chunk(c)
            act.wait_ge(self.turned, c + 1)
            nc.scalar.copy(m.A[0:D, lo:lo + n], m.ps[c % 2][0:D, 0:n]).then_inc(self.stored, 1)

    def tensor(self, pe):
        nc, m = self.nc, self.m
        pe.wait_ge(self.h, 1)
        for c in range(NCH):
            lo, n = chunk(c)
            if c >= 2:
                pe.wait_ge(self.stored, c - 1)
            for j in range(n // P):
                last = nc.tensor.transpose(m.ps[c % 2][0:D, j * P:(j + 1) * P], m.H[:, lo // P + j, :], m.ident[:])
            last.then_inc(self.turned, 1)


def reduced_sine(nc, step, x, k):
    step(nc.vector.tensor_scalar(k, x, 1.0 / (2.0 * PI), ROUND_MAGIC, ALU.mult, ALU.add))
    step(nc.vector.tensor_scalar(k, k, -ROUND_MAGIC, None, ALU.add))
    step(nc.vector.scalar_tensor_tensor(out=x, in0=k, scalar=-TWO_PI_HI, in1=x, op0=ALU.mult, op1=ALU.add))
    step(nc.vector.scalar_tensor_tensor(out=x, in0=k, scalar=-TWO_PI_LO, in1=x, op0=ALU.mult, op1=ALU.add))
    return nc.vector.tensor_scalar(x, x, PI_BELOW, -PI_BELOW, ALU.min, ALU.max)


def load_windows(nc, m, sp, ins, dr, sem, n_sem):
    sp.dma_start(m.dstrel[:].bitcast(I32), ins["dst_t"].rearrange("p (g j) -> p g j", j=J)).then_inc(sem, 16)
    sp.dma_start(m.D[:, 0:NG], bc(dr["base_f"], [P, NG])).then_inc(sem, 16)
    sp.dma_start(m.base_i[:], dr["base_i"]).then_inc(sem, 16)


def finish_windows(nc, m, v, step, sem):
    v.wait_ge(sem, 48)
    step(nc.vector.tensor_copy(m.dstrel[:], m.dstrel[:].bitcast(I32)))
    step(nc.vector.tensor_tensor(m.dstrel[:], m.dstrel[:], bc(m.D[:, 0:NG].unsqueeze(2), [P, NG, J]), ALU.subtract))
    step(nc.vector.tensor_scalar(m.nodeid[:], m.D[0:WIN, 0:NG], m.iotap[0:WIN, :], None, ALU.add))


def first_windows(nc, m, ins, dr, name, zero):
    st = Stage(nc, name + "_win")
    landed, dve = st.sem("landed"), st.sem("dve")
    with nc.Block() as block:
        @block.sync
        def _(sp):
            load_windows(nc, m, sp, ins, dr, landed, 3)
            sp.wait_ge(landed, 48)

        @block.vector
        def _(v):
            step = Chain(v, dve)
            for z in zero:
                step(nc.vector.memset(z, 0.0))
            finish_windows(nc, m, v, step, landed)
    st.close()


def edge_rounds(nc, m, rounds, name, one_round):
    with nc.Fori(0, rounds) as _r:
        st = Stage(nc, name)
        one_round(st)
        st.close()
        st = Stage(nc, name + "_shift")
        dve = st.sem("dve")
        with nc.Block() as block:
            @block.vector
            def _(v):
                step = Chain(v, dve)
                step(nc.vector.tensor_scalar(m.dstrel[:], m.dstrel[:], float(-WIN), None, ALU.add))
                step(nc.vector.tensor_scalar(m.nodeid[:], m.nodeid[:], float(WIN), None, ALU.add))
                step(nc.vector.tensor_scalar(m.base_i[:], m.base_i[:], float(WIN), float(N), ALU.add, ALU.min))
        st.close()


class Ring:

    def __init__(self, st, name):
        self.s = st.sem(name)

    def start(self, eng):
        eng.sem_inc(self.s, AHEAD)

    def done(self, eng, g, back=0):
        eng.wait_ge(self.s, g + (1 + AHEAD - back))

    def inc(self, ins):
        ins.then_inc(self.s, 1)


def gather_program(nc, m, pool, rows, table, idx_set, seg, gathered, turns):
    with pool.Fori(0, TURNS) as i:
        for u in range(U):
            g = i * U + u
            pool.wait_ge(idx_set, g + 1)
            seg.done(pool, g, U)
            pool.sem_inc(turns, 1)
            for j in range(J):
                nc.gpsimd.indirect_dma_start(
                    rows[:, u * J + j, :], None, table,
                    bass.IndirectOffsetOnAxis(ap=m.idx[:, u, j:j + 1], axis=0)).then_inc(gathered[u], 16)


def first_ids(nc, m, act, idx_set):
    for u in range(U):
        nc.scalar.copy(m.idx[:, u, :], m.src[:, u * J:(u + 1) * J]).then_inc(idx_set, 1)


def next_ids(nc, m, act, i, u, gathered, idx_set):
    act.wait_ge(gathered[u], i * (16 * J) + 16 * J)
    nc.scalar.copy(m.idx[:, u, :], m.src[:, ds(i * (U * J) + (U + u) * J, J)]).then_inc(idx_set, 1)


def window_base(m, eng, g):
    return eng.value_load(m.base_i[0:1, ds(g, 1)], min_val=0, max_val=NP)




def layer0_nodes(nc, m, w, dr):
    st = Stage(nc, "l0n")
    ln = Nodes(nc, m, st, m.D)
    up, upd, ph, phd, nm, nmd = (st.sem(n) for n in ("up", "up_read", "ph", "ph_read", "nm", "nm_read"))
    dve, args, trig, out, dved = (st.sem(n) for n in ("dve", "args", "trig", "out", "dve_done"))
    T1, PHT, PHN, AB = m.B, m.C, m.D, m.E
    phn3 = PHN[:, 0:NP].rearrange("p (t f) -> p t f", f=P)
    ab3 = AB[:, 0:NP].rearrange("p (t f) -> p t f", f=P)
    with nc.Block() as block:
        @block.vector
        def _(v):
            ln.vector(v)
            for c in range(NCH):
                lo, n = chunk(c)
                k = n // P
                v.wait_ge(ph, c + 1)
                nc.vector.tensor_scalar(PHT[:, lo:lo + n], m.ps[4 + c % 2][:, 0:n], w["b_ph"][:], None,
                                        ALU.add).then_inc(phd, 1)
                v.wait_ge(nm, 2 * c + 1)
                nc.vector.tensor_tensor(phn3[:, lo // P:lo // P + k, :],
                                        m.ps[6][:, 0:n].rearrange("p (t f) -> p t f", f=P),
                                        bc(w["row_ph"][:].unsqueeze(1), [P, k, P]), ALU.add).then_inc(nmd, 1)
                v.wait_ge(nm, 2 * c + 2)
                nc.vector.tensor_tensor(ab3[:, lo // P:lo // P + k, :],
                                        m.ps[7][:, 0:n].rearrange("p (t f) -> p t f", f=P),
                                        bc(w["row_ab"][:].unsqueeze(1), [P, k, P]), ALU.add).then_inc(nmd, 1)
            v.wait_ge(phd, NCH)
            v.wait_ge(nmd, 2 * NCH)
            step = Chain(v, dve)
            reduced_sine(nc, step, PHN[:, 0:NP], m.F[:, 0:NP]).then_inc(args, 1)
            v.wait_ge(args, 1)
            reduced_sine(nc, step, PHT[:, 0:NP], m.F[:, 0:NP]).then_inc(args, 1)

        @block.scalar
        def _(act):
            ln.scalar(act)
            for c in range(NCH):
                lo, n = chunk(c)
                act.wait_ge(up, c + 1)
                nc.scalar.activation(T1[0:D, lo:lo + n], m.ps[2 + c % 2][0:D, 0:n], ACT.Tanh,
                                     bias=w["b_pf"][0:D, :]).then_inc(upd, 1)
                nc.scalar.activation(T1[D:P, lo:lo + n], m.ps[2 + c % 2][D:P, 0:n], ACT.Relu,
                                     bias=w["b_pf"][D:P, :]).then_inc(upd, 1)
            act.wait_ge(args, 1)
            nc.scalar.activation(PHN[:, 0:NP], PHN[:, 0:NP], ACT.Sin).then_inc(trig, 1)
            act.wait_ge(args, 2)
            nc.scalar.activation(PHT[:, 0:NP], PHT[:, 0:NP], ACT.Sin).then_inc(trig, 1)

        @block.tensor
        def _(pe):
            ln.tensor(pe)
            for c in range(NCH):
                lo, n = chunk(c)
                pe.wait_ge(ln.stored, c + 1)
                if c >= 2:
                    pe.wait_ge(upd, 2 * (c - 1))
                nc.tensor.matmul(m.ps[2 + c % 2][:, 0:n], w["w_pf"][:], m.A[0:D, lo:lo + n],
                                 start=True, stop=True).then_inc(up, 1)
                pe.wait_ge(upd, 2 * (c + 1))
                if c >= 2:
                    pe.wait_ge(phd, c - 1)
                nc.tensor.matmul(m.ps[4 + c % 2][:, 0:n], w["w_pp"][:], T1[0:D, lo:lo + n],
                                 start=True, stop=True).then_inc(ph, 1)
                if c >= 1:
                    pe.wait_ge(nmd, 2 * c - 1)
                for j in range(n // P):
                    last = nc.tensor.matmul(m.ps[6][:, j * P:(j + 1) * P], T1[0:D, lo + j * P:lo + (j + 1) * P],
                                            w["w_pp"][:], start=True, stop=True)
                last.then_inc(nm, 1)
                if c >= 1:
                    pe.wait_ge(nmd, 2 * c)
                for j in range(n // P):
                    last = nc.tensor.matmul(m.ps[7][:, j * P:(j + 1) * P], m.A[0:D, lo + j * P:lo + (j + 1) * P],
                                            w["w_ba"][:], start=True, stop=True)
                last.then_inc(nm, 1)

        @block.sync
        def _(sp):
            sp.wait_ge(nmd, 2 * NCH)
            sp.dma_start(rows_of(dr["tab0"], (2 * D, 3 * D)), ab3[:, :, 0:D]).then_inc(out, 16)
            sp.dma_start(rows_of(dr["tgt0"], (0, D)), ab3[:, :, D:P]).then_inc(out, 16)
            sp.wait_ge(trig, 1)
            sp.dma_start(rows_of(dr["tab0"], (0, 2 * D)), phn3).then_inc(out, 16)
            sp.wait_ge(out, 48)
    st.close()


def layer0_edges(nc, m, w, ins, dr, rounds):
    RW = 3 * D
    rows, trow, ot, win, relu = m.carve(m.D, [(P, U * J, RW), (WIN, 2, GE), (WIN, 2, GE), (WIN, 2, D), (P, J, D)])
    trow = trow.bitcast(I32)
    table = dr["tab0"]

    def one_round(st):
        gathered = st.keep(m.gathered)
        trow_in = [st.sem(f"targets_in{b}") for b in range(2)]
        win_in = [st.sem(f"window_in{b}") for b in range(2)]
        idx_set, dve, turns = st.sem("ids_set"), st.sem("dve"), st.sem("gather_turns")
        ot_set, z_set, zs_set, k_set, ok_set, seg, added = (
            Ring(st, n) for n in ("expander", "gate_psum", "gate_sum", "gate", "onehot", "segments", "added"))

        def landed(eng, sems, i, u):
            eng.wait_ge(sems[u % 2], i * 32 + 16 * (u // 2 + 1))

        with nc.Block() as block:
            @block.sync
            def _(sp):
                with sp.Fori(0, TURNS) as i:
                    for u in range(U):
                        g, b = i * U + u, u % 2
                        ot_set.done(sp, g, 2)
                        sp.dma_start(trow[:, b, :], bc(ins["dst_rows"][ds(g, 1), :], [WIN, GE])).then_inc(trow_in[b], 16)
                        z_set.done(sp, g, 2)
                        base = window_base(m, sp, g)
                        sp.dma_start(win[:, b, :], dr["tgt0"][ds(base, WIN), :]).then_inc(win_in[b], 16)

            @block.gpsimd
            def _(pool):
                gather_program(nc, m, pool, rows, table, idx_set, seg, gathered, turns)

            @block.scalar
            def _(act):
                k_set.start(act)
                first_ids(nc, m, act, idx_set)
                with act.Fori(0, TURNS) as i:
                    for u in range(U):
                        g, b = i * U + u, u % 2
                        next_ids(nc, m, act, i, u, gathered, idx_set)
                        zs_set.done(act, g)
                        k_set.inc(nc.scalar.activation(m.kgate[:, b, :], m.zsum[:, b, :], ACT.Sigmoid,
                                                       bias=w["cb2"][:]))

            @block.tensor
            def _(pe):
                z_set.start(pe)
                seg.start(pe)
                with pe.Fori(0, TURNS) as i:
                    for u in range(U):
                        g, b = i * U + u, u % 2
                        z = m.ps[b]
                        ot_set.done(pe, g)
                        landed(pe, win_in, i, u)
                        zs_set.done(pe, g, 2)
                        pe.wait_ge(gathered[u], i * (16 * J) + 16 * J)
                        for j in range(J):
                            nc.tensor.matmul(z[:, j * D:(j + 1) * D], ot[:, b, j * P:(j + 1) * P], win[:, b, :],
                                             start=True, stop=False)
                            last = nc.tensor.matmul(z[:, j * D:(j + 1) * D], m.ident[:],
                                                    rows[:, u * J + j, 2 * D:3 * D], start=False, stop=True)
                        z_set.inc(last)
                        ok_set.done(pe, g)
                        added.done(pe, g, 2)
                        for j in range(J):
                            last = nc.tensor.matmul(m.ps[2 + b][:, 0:WIN], rows[:, u * J + j, 0:2 * D],
                                                    m.onehot[:, b, j, :], start=(j == 0), stop=(j == J - 1))
                        seg.inc(last)

            @block.vector
            def _(v):
                for r in (ot_set, zs_set, ok_set, added):
                    r.start(v)
                with v.Fori(0, TURNS) as i:
                    for u in range(U):
                        g, b = i * U + u, u % 2
                        base = window_base(m, v, g)
                        landed(v, trow_in, i, u)
                        z_set.done(v, g, 2)
                        ot_set.inc(nc.vector.tensor_scalar(ot[:, b, :], trow[:, b, :], m.nodeid[:, ds(g, 1)],
                                                           None, ALU.is_equal))
                        z_set.done(v, g)
                        nc.vector.scalar_tensor_tensor(
                            out=relu, in0=m.ps[b][:, 0:J * D].rearrange("p (j f) -> p j f", f=D), scalar=0.0,
                            in1=bc(w["row_cw2"][:].unsqueeze(1), [P, J, D]), op0=ALU.max, op1=ALU.mult).then_inc(dve, 1)
                        v.wait_ge(dve, g + 1)
                        zs_set.inc(nc.vector.tensor_reduce(out=m.zsum[:, b, :], in_=relu, axis=AX, op=ALU.add))
                        k_set.done(v, g)
                        for j in range(J):
                            last = nc.vector.tensor_scalar(m.onehot[:, b, j, :], m.iota[:, 0:WIN],
                                                           m.dstrel[:, ds(g, 1), j], m.kgate[:, b, j:j + 1],
                                                           ALU.is_equal, ALU.mult)
                        ok_set.inc(last)
                        seg.done(v, g)
                        added.done(v, g, 1)
                        added.inc(nc.vector.tensor_tensor(m.E[:, ds(base, WIN)], m.E[:, ds(base, WIN)],
                                                          m.ps[2 + b][:, 0:WIN], ALU.add))

    edge_rounds(nc, m, rounds, "l0e", one_round)


def layer0_out(nc, m, w):
    st = Stage(nc, "l0o")
    mul, fr, frd, o1, o1d, o2, o2d, dve = (
        st.sem(n) for n in ("mul", "freq", "freq_read", "o1", "o1_read", "o2", "o2_read", "dve"))
    O1 = m.D
    with nc.Block() as block:
        @block.vector
        def _(v):
            nc.vector.tensor_tensor(m.E[:, 0:NP], m.E[:, 0:NP], m.C[:, 0:NP], ALU.mult).then_inc(mul, 1)
            for c in range(NCH):
                lo, n = chunk(c)
                t, k = lo // P, n // P
                v.wait_ge(o2, c + 1)
                nc.vector.tensor_tensor(m.H[:, t:t + k, :], m.ps[4 + c % 2][:, 0:k * D].rearrange("p (t f) -> p t f", f=D),
                                        bc(w["row_ob2"][:].unsqueeze(1), [P, k, D]), ALU.add).then_inc(o2d, 1)
            v.wait_ge(o2d, NCH)
            nc.vector.tensor_tensor(m.x[:], m.x[:], m.H, ALU.add).then_inc(dve, 1)
            v.wait_ge(dve, 1)

        @block.scalar
        def _(act):
            for c in range(NCH):
                lo, n = chunk(c)
                act.wait_ge(fr, c + 1)
                nc.scalar.activation(m.A[0:D, lo:lo + n], m.ps[c % 2][0:D, 0:n], ACT.Identity,
                                     bias=w["fb2"][:]).then_inc(frd, 1)
                act.wait_ge(o1, c + 1)
                nc.scalar.activation(O1[0:D, lo:lo + n], m.ps[2 + c % 2][0:D, 0:n], ACT.Relu,
                                     bias=w["ob1"][:]).then_inc(o1d, 1)

        @block.tensor
        def _(pe):
            for c in range(NCH):
                lo, n = chunk(c)
                if c >= 2:
                    pe.wait_ge(frd, c - 1)
                nc.tensor.matmul(m.ps[c % 2][0:D, 0:n], w["fw2"][D:P, :], m.B[D:P, lo:lo + n],
                                 start=True, stop=True).then_inc(fr, 1)
                pe.wait_ge(mul, 1)
                if c >= 2:
                    pe.wait_ge(o1d, c - 1)
                nc.tensor.matmul(m.ps[2 + c % 2][0:D, 0:n], w["ow1s"][:], m.E[:, lo:lo + n], start=True, stop=False)
                pe.wait_ge(frd, c + 1)
                nc.tensor.matmul(m.ps[2 + c % 2][0:D, 0:n], w["ow1s"][0:D, :], m.A[0:D, lo:lo + n],
                                 start=False, stop=True).then_inc(o1, 1)
                pe.wait_ge(o1d, c + 1)
                if c >= 2:
                    pe.wait_ge(o2d, c - 1)
                for j in range(n // P):
                    last = nc.tensor.matmul(m.ps[4 + c % 2][:, j * D:(j + 1) * D], O1[0:D, lo + j * P:lo + (j + 1) * P],
                                            w["ow2"][:], start=True, stop=True)
                last.then_inc(o2, 1)
    st.close()




def layer1_nodes(nc, m, w, dr):
    st = Stage(nc, "l1n")
    ln = Nodes(nc, m, st, m.D)
    tb, tbd, out, dve = (st.sem(n) for n in ("tab", "tab_read", "out", "dve"))
    tab = m.DE[:, 0:NT * 2 * HM].rearrange("p (t f) -> p t f", f=2 * HM)
    per = 3
    cuts = [(t, min(per, NT - t)) for t in range(0, NT, per)]
    with nc.Block() as block:
        @block.vector
        def _(v):
            ln.vector(v)
            for c, (t, k) in enumerate(cuts):
                v.wait_ge(tb, c + 1)
                nc.vector.tensor_tensor(tab[:, t:t + k, :],
                                        m.ps[2 + c % 2][:, 0:k * 2 * HM].rearrange("p (t f) -> p t f", f=2 * HM),
                                        bc(w["row_m1"][:].unsqueeze(1), [P, k, 2 * HM]), ALU.add).then_inc(tbd, 1)

        @block.scalar
        def _(act):
            ln.scalar(act)

        @block.tensor
        def _(pe):
            ln.tensor(pe)
            pe.wait_ge(ln.stored, NCH)
            for c, (t, k) in enumerate(cuts):
                if c >= 2:
                    pe.wait_ge(tbd, c - 1)
                for j in range(k):
                    last = nc.tensor.matmul(m.ps[2 + c % 2][:, j * 2 * HM:(j + 1) * 2 * HM],
                                            m.A[0:D, (t + j) * P:(t + j + 1) * P], w["w_m1"][:], start=True, stop=True)
                last.then_inc(tb, 1)

        @block.sync
        def _(sp):
            sp.wait_ge(tbd, len(cuts))
            sp.dma_start(rows_of(dr["tab1"], (0, HM)), tab[:, :, 0:HM]).then_inc(out, 16)
            sp.dma_start(rows_of(dr["tgt1"], (0, HM)), tab[:, :, HM:2 * HM]).then_inc(out, 16)
            sp.wait_ge(out, 32)
    st.close()


def source_digits(nc, m):
    st = Stage(nc, "dig")
    dve = st.sem("dve")
    with nc.Block() as block:
        @block.vector
        def _(v):
            step = Chain(v, dve)
            step(nc.vector.memset(m.edw[:], 1.0))
            step(nc.vector.memset(m.m1[:], 1.0))
    st.close()


def layer1_edges(nc, m, w, ins, dr, rounds):
    rows, trow, ot, win, ea = m.carve(m.D, [(P, U * J, HM), (WIN, 2, GE), (WIN, 2, GE), (WIN, 2, HM), (DE, 2, GE)])
    trow = trow.bitcast(I32)
    m1, msg, hist = m.m1, m.msg, m.hist

    def one_round(st):
        gathered = st.keep(m.gathered)
        trow_in = [st.sem(f"targets_in{b}") for b in range(2)]
        win_in = [st.sem(f"window_in{b}") for b in range(2)]
        ea_in = [st.sem(f"edge_features_in{b}") for b in range(2)]
        idx_set, dve, turns = st.sem("ids_set"), st.sem("dve"), st.sem("gather_turns")
        ot_set, pre, g1, msgp, g2, oh, seg, added = (
            Ring(st, n) for n in ("expander", "pre", "gelu1", "msg_psum", "gelu2", "onehots", "segments", "added"))

        def landed(eng, sems, i, u):
            eng.wait_ge(sems[u % 2], i * 32 + 16 * (u // 2 + 1))

        with nc.Block() as block:
            @block.sync
            def _(sp):
                with sp.Fori(0, TURNS) as i:
                    for u in range(U):
                        g, b = i * U + u, u % 2
                        ot_set.done(sp, g, 2)
                        sp.dma_start(trow[:, b, :], bc(ins["dst_rows"][ds(g, 1), :], [WIN, GE])).then_inc(trow_in[b], 16)
                        pre.done(sp, g, 2)
                        base = window_base(m, sp, g)
                        sp.dma_start(win[:, b, :], dr["tgt1"][ds(base, WIN), :]).then_inc(win_in[b], 16)
                        sp.dma_start(ea[:, b, :], ins["ea_T"][:, ds(i * (U * GE) + u * GE, GE)]).then_inc(ea_in[b], 16)

            @block.gpsimd
            def _(pool):
                gather_program(nc, m, pool, rows, dr["tab1"], idx_set, seg, gathered, turns)

            @block.scalar
            def _(act):
                g1.start(act)
                g2.start(act)
                first_ids(nc, m, act, idx_set)
                with act.Fori(0, TURNS) as i:
                    for u in range(U):
                        g, b = i * U + u, u % 2
                        next_ids(nc, m, act, i, u, gathered, idx_set)
                        pre.done(act, g)
                        msgp.done(act, g, 2)
                        g1.inc(nc.scalar.activation(m1[0:HM, b, :], m.ps[b][0:HM, :], ACT.Gelu))
                        msgp.done(act, g)
                        seg.done(act, g, 2)
                        g2.inc(nc.scalar.activation(msg[:, b, :, :], m.ps[2 + b][:, 0:J * D].rearrange(
                            "p (j f) -> p j f", f=D), ACT.Gelu))

            @block.tensor
            def _(pe):
                for r in (pre, msgp, seg):
                    r.start(pe)
                with pe.Fori(0, TURNS) as i:
                    for u in range(U):
                        g, b = i * U + u, u % 2
                        z = m.ps[b][0:HM, :]
                        g1.done(pe, g, 2)
                        landed(pe, ea_in, i, u)
                        nc.tensor.matmul(z, w["w_e"][:], ea[:, b, :], start=True, stop=False)
                        ot_set.done(pe, g)
                        landed(pe, win_in, i, u)
                        nc.tensor.matmul(z, win[:, b, :], ot[:, b, :], start=False, stop=False)
                        pe.wait_ge(gathered[u], i * (16 * J) + 16 * J)
                        for j in range(J):
                            last = nc.tensor.matmul(z[:, j * P:(j + 1) * P], rows[:, u * J + j, :], m.ident[:],
                                                    start=False, stop=(j == J - 1))
                        pre.inc(last)
                        g1.done(pe, g)
                        g2.done(pe, g, 2)
                        for j in range(J):
                            last = nc.tensor.matmul(m.ps[2 + b][:, j * D:(j + 1) * D], m1[:, b, j * P:(j + 1) * P],
                                                    w["w_m2"][:], start=True, stop=True)
                        msgp.inc(last)
                        oh.done(pe, g)
                        added.done(pe, g, 2)
                        for j in range(J):
                            nc.tensor.matmul(m.ps[6 + b][:, 0:WIN], m.edw[:, b, j, :], m.onehot[:, b, j, :],
                                             start=(j == 0), stop=(j == J - 1))
                        for j in range(J):
                            nc.tensor.matmul(m.ps[6 + b][0:WIN, P:2 * P], m.hi1[:, b, j, :], m.lo1[:, b, j, :],
                                             start=(j == 0), stop=(j == J - 1))
                        g2.done(pe, g)
                        for j in range(J):
                            last = nc.tensor.matmul(m.ps[4 + b][0:D, 0:WIN], msg[:, b, j, :], m.onehot[:, b, j, :],
                                                    start=(j == 0), stop=(j == J - 1))
                        seg.inc(last)

            @block.vector
            def _(v):
                nc.vector.memset(hist, 0.0).then_inc(dve, 1)
                for r in (ot_set, oh, added):
                    r.start(v)
                v.wait_ge(dve, 1)
                with v.Fori(0, TURNS) as i:
                    for u in range(U):
                        g, b = i * U + u, u % 2
                        base = window_base(m, v, g)
                        landed(v, trow_in, i, u)
                        pre.done(v, g, 2)
                        ot_set.inc(nc.vector.tensor_scalar(ot[:, b, :], trow[:, b, :], m.nodeid[:, ds(g, 1)],
                                                           None, ALU.is_equal))
                        seg.done(v, g, 2)
                        nc.vector.tensor_tensor(m.onehot[:, b], bc(m.iota[:, 0:WIN].unsqueeze(1), [P, J, WIN]),
                                                bc(m.dstrel[:, ds(g, 1), :].rearrange("p a j -> p (a j)").unsqueeze(2),
                                                   [P, J, WIN]), ALU.is_equal)
                        nc.vector.tensor_copy(m.edw[:, b, :, 0:D],
                                              bc(m.ew[:, ds(i * (U * J) + u * J, J)].unsqueeze(2), [P, J, D]))
                        e0 = i * (U * J) + u * J
                        nc.vector.tensor_tensor(m.hi1[:, b], bc(m.iota[:, 0:WIN].unsqueeze(1), [P, J, WIN]),
                                                bc(m.hi[:, ds(e0, J)].unsqueeze(2), [P, J, WIN]), ALU.is_equal)
                        oh.inc(nc.vector.tensor_tensor(m.lo1[:, b], bc(m.iota[:].unsqueeze(1), [P, J, P]),
                                                       bc(m.lo[:, ds(e0, J)].unsqueeze(2), [P, J, P]), ALU.is_equal))
                        seg.done(v, g)
                        added.done(v, g, 1)
                        nc.vector.tensor_tensor(m.B[:, ds(base, WIN)], m.B[:, ds(base, WIN)],
                                                m.ps[6 + b][:, 0:WIN], ALU.add)
                        nc.vector.tensor_tensor(hist, hist, m.ps[6 + b][0:WIN, P:2 * P], ALU.add)
                        added.inc(nc.vector.tensor_tensor(m.E[0:D, ds(base, WIN)], m.E[0:D, ds(base, WIN)],
                                                          m.ps[4 + b][0:D, 0:WIN], ALU.add))

    edge_rounds(nc, m, rounds, "l1e", one_round)


def split_sources(nc, m):
    st = Stage(nc, "split")
    dve = st.sem("dve")
    n = NG * J
    hi_i, lo_i = m.hi_scr, m.lo_scr
    with nc.Block() as block:
        @block.vector
        def _(v):
            step = Chain(v, dve)
            step(nc.vector.memset(m.edw[:], 1.0))
            step(nc.vector.memset(m.m1, 1.0))
            step(nc.vector.tensor_single_scalar(hi_i, m.src[:, 0:n], P.bit_length() - 1, op=ALU.arith_shift_right))
            step(nc.vector.tensor_single_scalar(lo_i, m.src[:, 0:n], P - 1, op=ALU.bitwise_and))
            step(nc.vector.tensor_copy(m.hi, hi_i))
            step(nc.vector.tensor_copy(m.lo, lo_i))
    st.close()


def layer1_out(nc, m, w, dr):
    st = Stage(nc, "l1o")
    c1, c1d, c2, c2d, g, dve, out = (st.sem(n) for n in ("c1", "c1_read", "c2", "c2_read", "gelu", "dve", "out"))
    comb = m.D[:, 0:NT * D].rearrange("p (t f) -> p t f", f=D)
    with nc.Block() as block:
        @block.vector
        def _(v):
            step = Chain(v, dve)
            step(nc.vector.tensor_tensor(m.x[:], m.x[:], m.H, ALU.add))
            for c in range(NCH):
                lo, n = chunk(c)
                t, k = lo // P, n // P
                v.wait_ge(c2, c + 1)
                nc.vector.tensor_tensor(comb[:, t:t + k, :], m.ps[2 + c % 2][:, 0:k * D].rearrange("p (t f) -> p t f", f=D),
                                        bc(w["row_bc2"][:].unsqueeze(1), [P, k, D]), ALU.add).then_inc(c2d, 1)
            v.wait_ge(g, 1)
            step(nc.vector.tensor_tensor(m.x[:], m.x[:], comb, ALU.add))

        @block.scalar
        def _(act):
            for c in range(NCH):
                lo, n = chunk(c)
                act.wait_ge(c1, c + 1)
                nc.scalar.activation(m.C[0:HC, lo:lo + n], m.ps[c % 2][0:HC, 0:n], ACT.Gelu,
                                     bias=w["b_c1"][:]).then_inc(c1d, 1)
            act.wait_ge(c2d, NCH)
            nc.scalar.activation(comb, comb, ACT.Gelu).then_inc(g, 1)

        @block.tensor
        def _(pe):
            for c in range(NCH):
                lo, n = chunk(c)
                if c >= 2:
                    pe.wait_ge(c1d, c - 1)
                nc.tensor.matmul(m.ps[c % 2][0:HC, 0:n], w["w_c1a"][:], m.A[0:D, lo:lo + n], start=True, stop=False)
                nc.tensor.matmul(m.ps[c % 2][0:HC, 0:n], w["w_c1b"][:], m.E[0:D, lo:lo + n],
                                 start=False, stop=True).then_inc(c1, 1)
                pe.wait_ge(c1d, c + 1)
                if c >= 2:
                    pe.wait_ge(c2d, c - 1)
                for j in range(n // P):
                    last = nc.tensor.matmul(m.ps[2 + c % 2][:, j * D:(j + 1) * D], m.C[0:HC, lo + j * P:lo + (j + 1) * P],
                                            w["w_c2"][:], start=True, stop=True)
                last.then_inc(c2, 1)

        @block.sync
        def _(sp):
            sp.dma_start(dr["degout"].rearrange("a (t p) -> (a t) p", p=P), m.hist[0:NT, :]).then_inc(out, 16)
            sp.wait_ge(out, 16)
    st.close()




def sum_sources(nc, m, dr, rounds, name, weighted):
    rows, = m.carve(m.D, [(P, U * J, D)])

    def one_round(st):
        gathered = st.keep(m.gathered)
        idx_set, dve, turns = st.sem("ids_set"), st.sem("dve"), st.sem("gather_turns")
        oh, seg, added = (Ring(st, n) for n in ("onehot", "segments", "added"))
        with nc.Block() as block:
            @block.gpsimd
            def _(pool):
                gather_program(nc, m, pool, rows, dr["tab2"], idx_set, seg, gathered, turns)

            @block.scalar
            def _(act):
                first_ids(nc, m, act, idx_set)
                with act.Fori(0, TURNS) as i:
                    for u in range(U):
                        next_ids(nc, m, act, i, u, gathered, idx_set)

            @block.tensor
            def _(pe):
                seg.start(pe)
                with pe.Fori(0, TURNS) as i:
                    for u in range(U):
                        g, b = i * U + u, u % 2
                        oh.done(pe, g)
                        added.done(pe, g, 2)
                        pe.wait_ge(gathered[u], i * (16 * J) + 16 * J)
                        for j in range(J):
                            last = nc.tensor.matmul(m.ps[b][0:D, 0:WIN], rows[:, u * J + j, :], m.onehot[:, b, j, :],
                                                    start=(j == 0), stop=(j == J - 1))
                        seg.inc(last)

            @block.vector
            def _(v):
                oh.start(v)
                added.start(v)
                with v.Fori(0, TURNS) as i:
                    for u in range(U):
                        g, b = i * U + u, u % 2
                        base = window_base(m, v, g)
                        seg.done(v, g, 2)
                        if weighted:
                            for j in range(J):
                                last = nc.vector.tensor_scalar(
                                    m.onehot[:, b, j, :], m.iota[:, 0:WIN], m.dstrel[:, ds(g, 1), j],
                                    m.ew[:, ds(i * (U * J) + u * J + j, 1)], ALU.is_equal, ALU.mult)
                        else:
                            last = nc.vector.tensor_tensor(
                                m.onehot[:, b], bc(m.iota[:, 0:WIN].unsqueeze(1), [P, J, WIN]),
                                bc(m.dstrel[:, ds(g, 1), :].rearrange("p a j -> p (a j)").unsqueeze(2),
                                   [P, J, WIN]), ALU.is_equal)
                        oh.inc(last)
                        seg.done(v, g)
                        added.done(v, g, 1)
                        added.inc(nc.vector.tensor_tensor(m.E[0:D, ds(base, WIN)], m.E[0:D, ds(base, WIN)],
                                                          m.ps[b][0:D, 0:WIN], ALU.add))

    edge_rounds(nc, m, rounds, name, one_round)


def turn_to_nodes(nc, m, pe, src_region, bank0, turned, stored):
    for c in range(NCH):
        lo, n = chunk(c)
        if c >= 2:
            pe.wait_ge(stored, c - 1)
        for j in range(n // P):
            last = nc.tensor.transpose(m.ps[bank0 + c % 2][:, j * D:(j + 1) * D],
                                       src_region[0:D, lo + j * P:lo + (j + 1) * P], m.ident[0:D, 0:D])
        last.then_inc(turned, 1)




def layer2_in(nc, m, w, dr, conv):
    st = Stage(nc, f"l2n{conv}")
    first = conv == 0
    ln = Nodes(nc, m, st, m.D) if first else None
    dve, rt, dg, us, zt, ztd, zn, znd, out = (
        st.sem(n) for n in ("dve", "root", "deg", "u_set", "zt", "zt_read", "zn", "zn_read", "out"))
    dinv, deg = m.B[0:D, 0:NP], m.B[0:D, 0:NP]
    U_, Z = m.D[0:D, 0:NP], m.C[0:D, 0:NP]
    W_ = w[f"w_g{conv}"]
    with nc.Block() as block:
        @block.vector
        def _(v):
            step = Chain(v, dve)
            if first:
                ln.vector(v)
                nc.vector.tensor_scalar(deg, deg, 1.0, None, ALU.add).then_inc(dg, 1)
                v.wait_ge(rt, 1)
                step(nc.vector.reciprocal(dinv, dinv))
                v.wait_ge(ln.stored, NCH)
            nc.vector.tensor_tensor(U_, m.A[0:D, 0:NP], dinv, ALU.mult).then_inc(us, 1)
            for c in range(NCH):
                lo, n = chunk(c)
                t, k = lo // P, n // P
                v.wait_ge(zn, c + 1)
                nc.vector.tensor_copy(m.TAB[:, t:t + k, :], m.ps[4 + c % 2][:, 0:k * D].rearrange(
                    "p (t f) -> p t f", f=D)).then_inc(znd, 1)

        @block.scalar
        def _(act):
            if first:
                ln.scalar(act)
                act.wait_ge(dg, 1)
                nc.scalar.activation(dinv, deg, ACT.Sqrt).then_inc(rt, 1)
            for c in range(NCH):
                lo, n = chunk(c)
                act.wait_ge(zt, c + 1)
                nc.scalar.copy(Z[:, lo:lo + n], m.ps[2 + c % 2][0:D, 0:n]).then_inc(ztd, 1)

        @block.tensor
        def _(pe):
            if first:
                ln.tensor(pe)
            pe.wait_ge(us, 1)
            for c in range(NCH):
                lo, n = chunk(c)
                if c >= 2:
                    pe.wait_ge(ztd, c - 1)
                nc.tensor.matmul(m.ps[2 + c % 2][0:D, 0:n], W_[:], U_[:, lo:lo + n], start=True, stop=True).then_inc(zt, 1)
                if c >= 2:
                    pe.wait_ge(znd, c - 1)
                for j in range(n // P):
                    last = nc.tensor.matmul(m.ps[4 + c % 2][:, j * D:(j + 1) * D], U_[:, lo + j * P:lo + (j + 1) * P],
                                            W_[:], start=True, stop=True)
                last.then_inc(zn, 1)

        @block.sync
        def _(sp):
            sp.wait_ge(znd, NCH)
            sp.dma_start(rows_of(dr["tab2"], (0, D)), m.TAB).then_inc(out, 16)
            sp.wait_ge(out, 16)
    st.close()


def layer2_out(nc, m, w, conv):
    st = Stage(nc, f"l2o{conv}")
    dve, var, std, done, turned, stored = (st.sem(n) for n in ("dve", "var", "std", "done", "turned", "stored"))
    col = m.col
    Eo = m.E[0:D, 0:NP]
    sq = m.D[0:D, 0:NP]
    mean, v_, sd, scale = (col[0:D, k:k + 1] for k in range(4))
    b, gamma, beta = w[f"b_g{conv}"], w[f"gamma{conv}"], w[f"beta{conv}"]
    with nc.Block() as block:
        @block.vector
        def _(v):
            step = Chain(v, dve)
            step(nc.vector.tensor_tensor(Eo, Eo, m.C[0:D, 0:NP], ALU.add))
            step(nc.vector.tensor_tensor(Eo, Eo, m.B[0:D, 0:NP], ALU.mult))
            step(nc.vector.tensor_scalar(Eo, Eo, b[:], None, ALU.add))
            step(nc.vector.tensor_reduce(out=mean, in_=Eo[:, 0:N], axis=AX, op=ALU.add))
            step(nc.vector.tensor_scalar(mean, mean, 1.0 / N, None, ALU.mult))
            step(nc.vector.tensor_scalar(Eo, Eo, mean, None, ALU.subtract))
            step(nc.vector.tensor_tensor(sq, Eo, Eo, ALU.mult))
            step(nc.vector.tensor_reduce(out=v_, in_=sq[:, 0:N], axis=AX, op=ALU.add))
            nc.vector.tensor_scalar(v_, v_, 1.0 / N, EPS, ALU.mult, ALU.add).then_inc(var, 1)
            v.wait_ge(std, 1)
            step(nc.vector.reciprocal(scale, sd))
            step(nc.vector.tensor_tensor(scale, scale, gamma[:], ALU.mult))
            step(nc.vector.tensor_scalar(m.A[0:D, 0:NP], Eo, scale, beta[:], ALU.mult, ALU.add))
            if conv == 0:
                step(nc.vector.tensor_scalar(m.A[0:D, 0:NP], m.A[0:D, 0:NP], 0.0, None, ALU.max))
            else:
                v.sem_inc(done, 1)
                for c in range(NCH):
                    lo, n = chunk(c)
                    t, k = lo // P, n // P
                    v.wait_ge(turned, c + 1)
                    nc.vector.tensor_tensor(m.H[:, t:t + k, :], m.H[:, t:t + k, :],
                                            m.ps[c % 2][:, 0:k * D].rearrange("p (t f) -> p t f", f=D),
                                            ALU.add).then_inc(stored, 1)
                v.wait_ge(stored, NCH)
                step(nc.vector.scalar_tensor_tensor(out=m.x[:], in0=m.H, scalar=0.0, in1=m.x[:],
                                                    op0=ALU.max, op1=ALU.add))

        @block.scalar
        def _(act):
            act.wait_ge(var, 1)
            nc.scalar.activation(sd, v_, ACT.Sqrt).then_inc(std, 1)

        @block.tensor
        def _(pe):
            if conv == 1:
                pe.wait_ge(done, 1)
                turn_to_nodes(nc, m, pe, m.A, 0, turned, stored)
    st.close()




def layer3_in(nc, m, w, dr, conv):
    st = Stage(nc, f"l3n{conv}")
    first = conv == 0
    ln = Nodes(nc, m, st, m.D) if first else None
    dve, rt, dg, us, turned, stored, out, degs = (
        st.sem(n) for n in ("dve", "root", "deg", "u_set", "turned", "stored", "out", "degs_in"))
    U_ = m.D[0:D, 0:NP]
    both = (m.B[0:D, 0:NP], m.C[0:D, 0:NP])
    with nc.Block() as block:
        @block.vector
        def _(v):
            step = Chain(v, dve)
            if first:
                ln.vector(v)
                v.wait_ge(degs, 32)
                for r in both:
                    nc.vector.tensor_scalar(r, r, 1.0, None, ALU.max).then_inc(dg, 1)
                v.wait_ge(rt, 2)
                for r in both:
                    step(nc.vector.reciprocal(r, r))
                v.wait_ge(ln.stored, NCH)
            nc.vector.tensor_tensor(U_, m.A[0:D, 0:NP], m.B[0:D, 0:NP], ALU.mult).then_inc(us, 1)
            for c in range(NCH):
                lo, n = chunk(c)
                t, k = lo // P, n // P
                v.wait_ge(turned, c + 1)
                nc.vector.tensor_copy(m.TAB[:, t:t + k, :], m.ps[4 + c % 2][:, 0:k * D].rearrange(
                    "p (t f) -> p t f", f=D)).then_inc(stored, 1)

        @block.scalar
        def _(act):
            if first:
                ln.scalar(act)
                act.wait_ge(dg, 2)
                for r in both:
                    nc.scalar.activation(r, r, ACT.Sqrt).then_inc(rt, 1)

        @block.tensor
        def _(pe):
            if first:
                ln.tensor(pe)
            pe.wait_ge(us, 1)
            turn_to_nodes(nc, m, pe, m.D, 4, turned, stored)

        @block.sync
        def _(sp):
            if first:
                sp.dma_start(m.C[0:D, 0:NP], m.B[D:P, 0:NP]).then_inc(degs, 16)
                sp.dma_start(m.B[0:D, 0:NP], bc(dr["degout"], [D, NP])).then_inc(degs, 16)
            sp.wait_ge(stored, NCH)
            sp.dma_start(rows_of(dr["tab2"], (0, D)), m.TAB).then_inc(out, 16)
            sp.wait_ge(out, 16)
    st.close()


def layer3_out(nc, m, w, conv, out_dram):
    st = Stage(nc, f"l3o{conv}")
    dve, ready, pr, prd, out = (st.sem(n) for n in ("dve", "ready", "product", "product_read", "out"))
    A, Eo, M = m.A[0:D, 0:NP], m.E[0:D, 0:NP], m.D[0:D, 0:NP]
    w1, w2 = w[f"w_n1{conv}"], w[f"w_n2{conv}"]
    full = N // P
    with nc.Block() as block:
        @block.vector
        def _(v):
            step = Chain(v, dve)
            step(nc.vector.tensor_tensor(Eo, Eo, m.C[0:D, 0:NP], ALU.mult))
            step(nc.vector.tensor_tensor(M, Eo, A, ALU.mult))
            nc.vector.tensor_tensor(Eo, Eo, A, ALU.add).then_inc(ready, 1)
            if conv == 1:
                for c in range(NCH):
                    lo, n = chunk(c)
                    t, k = lo // P, n // P
                    v.wait_ge(pr, c + 1)
                    nc.vector.tensor_tensor(m.x[:, t:t + k, :], m.x[:, t:t + k, :],
                                            m.ps[c % 2][:, 0:k * D].rearrange("p (t f) -> p t f", f=D),
                                            ALU.add).then_inc(prd, 1)

        @block.scalar
        def _(act):
            if conv == 0:
                for c in range(NCH):
                    lo, n = chunk(c)
                    act.wait_ge(pr, c + 1)
                    nc.scalar.activation(m.A[0:D, lo:lo + n], m.ps[c % 2][0:D, 0:n], ACT.Relu).then_inc(prd, 1)

        @block.tensor
        def _(pe):
            pe.wait_ge(ready, 1)
            for c in range(NCH):
                lo, n = chunk(c)
                if c >= 2:
                    pe.wait_ge(prd, c - 1)
                if conv == 0:
                    nc.tensor.matmul(m.ps[c % 2][0:D, 0:n], w1[:], Eo[:, lo:lo + n], start=True, stop=False)
                    last = nc.tensor.matmul(m.ps[c % 2][0:D, 0:n], w2[:], M[:, lo:lo + n], start=False, stop=True)
                else:
                    for j in range(n // P):
                        at, to = slice(lo + j * P, lo + (j + 1) * P), m.ps[c % 2][:, j * D:(j + 1) * D]
                        nc.tensor.matmul(to, Eo[:, at], w1[:], start=True, stop=False)
                        last = nc.tensor.matmul(to, M[:, at], w2[:], start=False, stop=True)
                last.then_inc(pr, 1)

        @block.sync
        def _(sp):
            if conv == 1:
                sp.wait_ge(prd, NCH)
                store_x(m, sp, out_dram, out)
    st.close()


def store_x(m, sp, out_dram, out):
    full = N // P
    sp.dma_start(out_dram[0:full * P, :].rearrange("(t p) f -> p t f", p=P), m.x[:, 0:full, :]).then_inc(out, 16)
    sp.dma_start(out_dram[full * P:N, :], m.x[0:N - full * P, full, :]).then_inc(out, 16)
    sp.wait_ge(out, 32)




def gnn_kernel(nc, a, out, stop=None):
    with ExitStack() as ctx:
        m = Memory(nc, ctx)
        m.gathered = [ctx.enter_context(nc.semaphore(f"gathered{u}")) for u in range(U)]
        m.rounds = ctx.enter_context(nc.sbuf_tensor("rounds", [1, 1], I32))
        m.hist = ctx.enter_context(nc.sbuf_tensor("source_counts", [WIN, P], F32))[:]
        n = NG * J
        m.hi = m.C[:, 0:n]
        m.lo = m.C[:, n:2 * n]
        m.hi_scr = m.C[:, 2 * n:3 * n].bitcast(I32)
        m.lo_scr = m.C[:, 3 * n:4 * n].bitcast(I32)
        half = m.F[:, NW // 2:NW]
        m.m1 = half[0:HC, 0:2 * GE].rearrange("p (b e) -> p b e", b=2)
        m.msg = half[:, 2 * GE:2 * GE + 2 * J * D].rearrange("p (b j f) -> p b j f", b=2, j=J)

        w, loads = {}, []

        def weight(name, shape, *parts):
            t = ctx.enter_context(nc.sbuf_tensor("w_" + name, shape, F32))
            w[name] = t
            for where, what in parts:
                loads.append((t[where], what))

        def col(ap):
            return ap.rearrange("(a b) -> a b", b=1)

        def row(ap, parts):
            return bc(ap.rearrange("(a b) -> a b", a=1), [parts, ap.shape[0]])

        s = slice
        al, top, bot = s(None), s(0, D), s(D, P)
        left, right = (al, s(0, D)), (al, s(D, P))
        weight("w_pf", [D, P], (left, a["L0_gnn_pw1"]), (right, a["L0_gnn_fw1"]))
        weight("w_pp", [D, P], (left, a["L0_gnn_pw2"]), (right, a["L0_gnn_pw2"]))
        weight("w_ba", [D, P], (left, a["L0_gnn_cw1"][D:2 * D, :]), (right, a["L0_gnn_cw1"][0:D, :]))
        weight("fw2", [P, D], ((bot, al), a["L0_gnn_fw2"]))
        weight("ow1s", [P, D], ((top, al), a["L0_gnn_ow1"]), ((bot, al), a["L0_gnn_ow1"]))
        weight("ow2", [D, D], ((al, al), a["L0_gnn_ow2"]))
        weight("b_pf", [P, 1], ((top, al), col(a["L0_gnn_pb1"])), ((bot, al), col(a["L0_gnn_fb1"])))
        weight("b_ph", [P, 1], ((top, al), col(a["L0_gnn_pb2"])), ((bot, al), col(a["L0_gnn_pb2"])))
        weight("row_ph", [P, P], (left, row(a["L0_gnn_pb2"], P)), (right, row(a["L0_gnn_pb2"], P)))
        weight("row_ab", [P, P], (right, row(a["L0_gnn_cb1"], P)))
        weight("fb2", [D, 1], ((al, al), col(a["L0_gnn_fb2"])))
        weight("ob1", [D, 1], ((al, al), col(a["L0_gnn_ob1"])))
        weight("row_ob2", [P, D], ((al, al), row(a["L0_gnn_ob2"], P)))
        weight("row_cw2", [P, D], ((al, al), bc(a["L0_gnn_cw2"].rearrange("a b -> b a"), [P, D])))
        weight("cb2", [P, 1], ((al, al), row(a["L0_gnn_cb2"], P)))
        weight("w_m1", [D, 2 * HM], ((al, s(0, HM)), a["L1_gnn_W_m1"][0:D, :]),
               ((al, s(HM, 2 * HM)), a["L1_gnn_W_m1"][D:2 * D, :]))
        weight("w_e", [DE, HM], ((al, al), a["L1_gnn_W_m1"][2 * D:2 * D + DE, :]))
        weight("w_m2", [HC, D], ((s(0, HM), al), a["L1_gnn_W_m2"]),
               ((s(HM, HM + 1), al), a["L1_gnn_b_m2"].rearrange("(a b) -> a b", a=1)))
        weight("row_m1", [P, 2 * HM], ((al, s(HM, 2 * HM)), row(a["L1_gnn_b_m1"], P)))
        weight("w_c1a", [D, HC], ((al, al), a["L1_gnn_W_c1"][0:D, :]))
        weight("w_c1b", [D, HC], ((al, al), a["L1_gnn_W_c1"][D:2 * D, :]))
        weight("b_c1", [HC, 1], ((al, al), col(a["L1_gnn_b_c1"])))
        weight("w_c2", [HC, D], ((al, al), a["L1_gnn_W_c2"]))
        weight("row_bc2", [P, D], ((al, al), row(a["L1_gnn_b_c2"], P)))
        for k in range(2):
            weight(f"w_g{k}", [D, D], ((al, al), a[f"L2_gnn_W{k + 1}"]))
            weight(f"b_g{k}", [D, 1], ((al, al), col(a[f"L2_gnn_b{k + 1}"])))
            weight(f"gamma{k}", [D, 1], ((al, al), col(a[f"L2_gnn_gamma{k + 1}"])))
            weight(f"beta{k}", [D, 1], ((al, al), col(a[f"L2_gnn_beta{k + 1}"])))
            weight(f"w_n1{k}", [D, D], ((al, al), a[f"L3_gnn_W1_{k + 1}"]))
            weight(f"w_n2{k}", [D, D], ((al, al), a[f"L3_gnn_W2_{k + 1}"]))

        dr = {name: nc.dram_tensor(name, shape, dt, kind="Internal").ap() for name, shape, dt in (
            ("tab0", [NP, 3 * D], F32), ("tgt0", [NW, D], F32), ("tab1", [NP, HM], F32), ("tgt1", [NW, HM], F32),
            ("tab2", [NP, D], F32), ("base_f", [1, NG], F32), ("base_i", [1, NG], I32), ("reach", [1, NG], F32),
            ("degout", [1, NP], F32))}
        ins = dict(a, loads=loads)

        st = Stage(nc, "zero")
        dve = st.sem("dve")
        with nc.Block() as block:
            @block.vector
            def _(v):
                step = Chain(v, dve)
                step(nc.vector.memset(w["row_ab"][:], 0.0))
                step(nc.vector.memset(w["row_m1"][:], 0.0))
                step(nc.vector.memset(w["w_m2"][:], 0.0))
        st.close()

        rounds = setup(nc, m, w, ins, dr)

        st = Stage(nc, "turns")
        dve = st.sem("dve")
        with nc.Block() as block:
            @block.vector
            def _(v):
                step = Chain(v, dve)
                step(nc.vector.tensor_scalar(w["b_ph"][0:D, :], w["b_ph"][0:D, :], PI / 2, None, ALU.add))
                step(nc.vector.tensor_scalar(w["b_ph"][D:P, :], w["b_ph"][D:P, :], PI, None, ALU.add))
                step(nc.vector.tensor_scalar(w["row_ph"][:, D:P], w["row_ph"][:, D:P], PI / 2, None, ALU.add))
        st.close()

        def stopped(k):
            if stop != k:
                return False
            st = Stage(nc, "stop")
            o = st.sem("out")
            with nc.Block() as block:
                @block.sync
                def _(sp):
                    store_x(m, sp, out, o)
            st.close()
            return True

        layer0_nodes(nc, m, w, dr)
        first_windows(nc, m, ins, dr, "l0", [m.E])
        layer0_edges(nc, m, w, ins, dr, rounds)
        layer0_out(nc, m, w)
        if stopped(0):
            return
        layer1_nodes(nc, m, w, dr)
        first_windows(nc, m, ins, dr, "l1", [m.E, m.B])
        split_sources(nc, m)
        layer1_edges(nc, m, w, ins, dr, rounds)
        layer1_out(nc, m, w, dr)
        if stopped(1):
            return
        for conv in range(2):
            layer2_in(nc, m, w, dr, conv)
            first_windows(nc, m, ins, dr, f"l2{conv}", [m.E])
            sum_sources(nc, m, dr, rounds, f"l2e{conv}", True)
            layer2_out(nc, m, w, conv)
        if stopped(2):
            return
        for conv in range(2):
            layer3_in(nc, m, w, dr, conv)
            first_windows(nc, m, ins, dr, f"l3{conv}", [m.E])
            sum_sources(nc, m, dr, rounds, f"l3e{conv}", False)
            layer3_out(nc, m, w, conv, out)




STOP = None


def kernel(**inputs):
    import numpy as np
    import concourse.bacc as bacc
    from concourse.bass_utils import run_bass_kernel_spmd

    a = {k: np.ascontiguousarray(v) for k, v in inputs.items()}
    pad = EP - E
    tiles = lambda v: np.ascontiguousarray(v.reshape(NG * J, P).T)
    src = np.pad(a.pop("src"), (0, pad))
    dst = np.pad(a.pop("dst"), (0, pad), constant_values=NO_TARGET)
    ew = np.pad(a.pop("edge_weight"), (0, pad))
    ea = np.pad(a.pop("edge_attr_32"), ((0, pad), (0, 0)))
    a["x"] = np.pad(a["x"], ((0, NP - N), (0, 0)))
    a["src_t"], a["dst_t"], a["ew_t"] = tiles(src), tiles(dst), tiles(ew)
    a["dst_rows"] = np.ascontiguousarray(dst.reshape(NG, GE))
    a["ea_T"] = np.ascontiguousarray(ea.T)

    nc = bacc.Bacc("TRN2", target_bir_lowering=False, num_devices=1)
    arrays, aps = {}, {}
    for name, v in a.items():
        arrays[f"in_{name}"] = v
        aps[name] = nc.dram_tensor(f"in_{name}", v.shape, mybir.dt.from_np(v.dtype), kind="ExternalInput").ap()
    out = nc.dram_tensor("out_x", (N, D), F32, kind="ExternalOutput").ap()
    gnn_kernel(nc, aps, out, STOP)
    r = run_bass_kernel_spmd(nc, [arrays], core_ids=[0])
    return r.results[0]["out_x"]
```

```python
from contextlib import ExitStack

import concourse.bass as bass
from concourse import mybir

F32 = mybir.dt.float32
I32 = mybir.dt.int32
BF16 = mybir.dt.bfloat16
ALU = mybir.AluOpType
ACT = mybir.ActivationFunctionType
AX = mybir.AxisListType.X

P = 128
N = 6250
E = 200000
D = 64
DE = 32
NT = -(-N // P)
NP = NT * P
WIN = 64
NW = NP + WIN
J = 4
GE = J * P
U = 4
NG = -(-E // (GE * U)) * U
EP = NG * GE
TURNS = NG // U
HM = 80
HC = 96
CH = 512
NCH = -(-NP // CH)
AHEAD = 4
EPS = 1e-5
PI = 3.141592653589793
TWO_PI_HI = 6.28125
TWO_PI_LO = 2.0 * PI - TWO_PI_HI
ROUND_MAGIC = 12582912.0
PI_BELOW = 3.1415925
NO_TARGET = 1 << 20


def chunk(c):
    return c * CH, min(CH, NP - c * CH)


def ds(start, size):
    return bass.ds(start, size)


def bc(ap, shape):
    return ap.to_broadcast(shape)


class Memory:

    def __init__(self, nc, ctx):
        def sb(name, shape, dt=F32):
            return ctx.enter_context(nc.sbuf_tensor(name, shape, dt))

        self.big = sb("node_arrays", [P, 6 * NW])
        r = [self.big[:, k * NW:(k + 1) * NW] for k in range(6)]
        self.A, self.B, self.C, self.D, self.E, self.F = r
        self.DE = self.big[:, 3 * NW:5 * NW]
        self.x = sb("x_nodes", [P, NT, D])
        self.src = sb("src_ids", [P, (NG + U) * J], I32)
        self.ew = sb("edge_weights", [P, NG * J])
        self.dstrel = sb("target_in_window", [P, NG, J])
        self.nodeid = sb("window_node_ids", [WIN, NG])
        self.base_i = sb("window_base", [1, NG], I32)
        self.onehot = sb("onehot", [P, 2, J, WIN])
        self.hi1 = sb("onehot_src_tile", [P, 2, J, WIN], BF16)
        self.lo1 = sb("onehot_src_row", [P, 2, J, P], BF16)
        self.idx = sb("gather_ids", [P, U, J], I32)
        self.ident = sb("identity", [P, P])
        self.iota = sb("iota_free", [P, P])
        self.iotap = sb("iota_partition", [P, 1])
        self.stat = sb("node_stats", [P, 4, NT])
        self.col = sb("channel_stats", [P, 16])
        self.kgate = sb("gates", [P, 2, J])
        self.zsum = sb("gate_inputs", [P, 2, J])
        self.ps = [ctx.enter_context(nc.psum_tensor(f"bank{k}", [P, CH], F32)) for k in range(8)]

        self.H = self.F[:, 0:NT * D].rearrange("p (t f) -> p t f", f=D)
        self.TAB = self.F[:, NW // 2:NW // 2 + NT * D].rearrange("p (t f) -> p t f", f=D)
        self.hilo = self.F[:, NW // 2:NW // 2 + NG * J * 2 // 2]

    def carve(self, region, sizes):
        out, at = [], 0
        for parts, *shape in sizes:
            n = 1
            for s in shape:
                n *= s
            piece = region[0:parts, at:at + n]
            if len(shape) == 2:
                piece = piece.rearrange("p (a b) -> p a b", b=shape[1])
            elif len(shape) == 3:
                piece = piece.rearrange("p (a b c) -> p a b c", b=shape[1], c=shape[2])
            out.append(piece)
            at += n
        assert at <= NW, at
        return out


class Chain:

    def __init__(self, eng, sem):
        self.eng, self.sem, self.n = eng, sem, 0

    def __call__(self, ins):
        self.n += 1
        ins.then_inc(self.sem, 1)
        self.eng.wait_ge(self.sem, self.n)


class Stage:

    def __init__(self, nc, name):
        self.nc, self.name, self.all, self.kept = nc, name, [], []
        self.ctx = ExitStack()

    def sem(self, name):
        s = self.ctx.enter_context(self.nc.semaphore(f"{self.name}_{name}"))
        self.all.append(s)
        return s

    def keep(self, sems):
        self.all += sems
        self.kept = sems
        return sems

    def close(self):
        kept = sorted(s.num for s in self.kept)
        if kept:
            self.nc.gpsimd.dma_reset(range(kept[0], kept[-1] + 1))
        for s in self.all:
            self.nc.gpsimd.sem_clear(s)
        self.nc.all_engine_barrier()
        self.ctx.close()


def rows_of(table, cols):
    return table[0:NP, cols[0]:cols[1]].rearrange("(t p) f -> p t f", p=P)




def setup(nc, m, w, ins, dr):
    st = Stage(nc, "setup")
    loads, consts, idz, mins, sent, back, dve, loaded_bases, rounds_ready = (
        st.sem(n) for n in ("loads", "consts", "ident_zero", "mins", "sent", "back", "dve", "bases", "rounds"))
    rows_in, zero_out = st.sem("rows_in"), st.sem("zero_out")
    per = NG // 98
    rows = m.A[0:98, 0:per * GE].bitcast(I32).rearrange("p (c e) -> p c e", e=GE)
    inside = m.B[0:98, 0:per * GE].rearrange("p (c e) -> p c e", e=GE)
    least, most, reach = m.C[0:98, 0:per], m.C[0:98, 8:8 + per], m.C[0:98, 16:16 + per]
    least_i = m.C[0:98, 24:24 + per].bitcast(I32)
    reach_row = m.C[0:1, 512:512 + NG]
    far = m.C[0:1, 1024:1028]
    far_i = m.C[0:1, 1032:1034].bitcast(I32)
    n_loads = len(ins["loads"]) + 3
    with nc.Block() as block:
        @block.sync
        def _(sp):
            sp.dma_start(rows, ins["dst_rows"].rearrange("(p c) e -> p c e", c=per)).then_inc(rows_in, 16)
            sp.dma_start(m.x[:], ins["x"].rearrange("(t p) f -> p t f", p=P)).then_inc(loads, 16)
            sp.dma_start(m.src[:, 0:NG * J], ins["src_t"]).then_inc(loads, 16)
            sp.dma_start(m.ew[:], ins["ew_t"]).then_inc(loads, 16)
            for to, what in ins["loads"]:
                sp.dma_start(to, what).then_inc(loads, 16)
            sp.wait_ge(mins, 1)
            sp.dma_start(dr["base_f"].rearrange("a (p c) -> (a p) c", c=per), least).then_inc(sent, 16)
            sp.dma_start(dr["base_i"].rearrange("a (p c) -> (a p) c", c=per), least_i).then_inc(sent, 16)
            sp.dma_start(dr["reach"].rearrange("a (p c) -> (a p) c", c=per), reach).then_inc(sent, 16)
            sp.wait_ge(sent, 48)
            sp.dma_start(reach_row, dr["reach"]).then_inc(back, 16)
            sp.wait_ge(consts, 3)
            for t, width in ((dr["tgt0"], D), (dr["tgt1"], HM)):
                sp.dma_start(t[NP:NW, :], m.E[0:WIN, 0:width]).then_inc(zero_out, 16)
            sp.wait_ge(zero_out, 32)
            sp.wait_ge(loads, 16 * n_loads)

        @block.gpsimd
        def _(pool):
            nc.gpsimd.memset(m.ident[:], 0.0).then_inc(idz, 1)
            nc.gpsimd.iota(m.iota[:], [[1, P]], base=0, channel_multiplier=0,
                           allow_small_or_imprecise_dtypes=True).then_inc(consts, 1)
            nc.gpsimd.iota(m.iotap[:], [[1, 1]], base=0, channel_multiplier=1,
                           allow_small_or_imprecise_dtypes=True).then_inc(consts, 1)
            pool.wait_ge(idz, 1)
            nc.gpsimd.affine_select(out=m.ident[:], in_=m.ident[:], compare_op=ALU.not_equal, fill=1.0,
                                    base=0, pattern=[[-1, P]], channel_multiplier=1).then_inc(idz, 1)
            pool.wait_ge(idz, 2)

        @block.vector
        def _(v):
            step = Chain(v, dve)
            nc.vector.memset(m.E[0:WIN, 0:P], 0.0).then_inc(consts, 1)
            step(nc.vector.memset(m.src[:, NG * J:], 0))
            v.wait_ge(rows_in, 16)
            step(nc.vector.tensor_reduce(out=least, in_=rows, axis=AX, op=ALU.min))
            step(nc.vector.scalar_tensor_tensor(out=inside, in0=rows, scalar=float(N), in1=rows,
                                                op0=ALU.is_lt, op1=ALU.mult))
            step(nc.vector.tensor_reduce(out=most, in_=inside, axis=AX, op=ALU.max))
            step(nc.vector.tensor_scalar(least, least, float(N), None, ALU.min))
            step(nc.vector.tensor_copy(least_i, least))
            nc.vector.scalar_tensor_tensor(out=reach, in0=least, scalar=-1.0, in1=most,
                                           op0=ALU.mult, op1=ALU.add).then_inc(mins, 1)
            v.wait_ge(back, 16)
            step(nc.vector.tensor_reduce(out=far[:, 0:1], in_=reach_row, axis=AX, op=ALU.max))
            step(nc.vector.tensor_scalar(far[:, 1:2], far[:, 0:1], 0.0, None, ALU.max))
            step(nc.vector.tensor_copy(far_i[:, 0:1], far[:, 1:2]))
            step(nc.vector.tensor_single_scalar(far_i[:, 1:2], far_i[:, 0:1], WIN.bit_length() - 1,
                                                op=ALU.arith_shift_right))
            step(nc.vector.tensor_copy(far[:, 2:3], far_i[:, 1:2]))
            step(nc.vector.tensor_scalar(far[:, 3:4], far[:, 2:3], 1.0, None, ALU.add))
            step(nc.vector.tensor_copy(m.rounds[:], far[:, 3:4]))
    st.close()
    with nc.Block() as block:
        @block.vector
        def _(v):
            pass
    return nc.values_load(m.rounds[0:1, 0:1], min_val=1, max_val=-(-N // WIN))




class Nodes:

    def __init__(self, nc, m, st, scratch):
        self.nc, self.m, self.scratch = nc, m, scratch
        self.chain, self.var, self.std, self.h = (st.sem(n) for n in ("ln_dve", "ln_var", "ln_std", "ln_h"))
        self.turned, self.stored = st.sem("h_turned"), st.sem("hT_stored")

    def vector(self, v):
        nc, m = self.nc, self.m
        step = Chain(v, self.chain)
        mean, var, std, rstd = (m.stat[:, k, :] for k in range(4))
        scr = self.scratch[:, 0:NT * D].rearrange("p (t f) -> p t f", f=D)
        wide = [P, NT, D]
        step(nc.vector.tensor_reduce(out=mean, in_=m.x[:], axis=AX, op=ALU.add))
        step(nc.vector.tensor_scalar(mean, mean, 1.0 / D, None, ALU.mult))
        step(nc.vector.tensor_tensor(m.H, m.x[:], bc(mean.unsqueeze(2), wide), ALU.subtract))
        step(nc.vector.tensor_tensor(scr, m.H, m.H, ALU.mult))
        step(nc.vector.tensor_reduce(out=var, in_=scr, axis=AX, op=ALU.add))
        nc.vector.tensor_scalar(var, var, 1.0 / D, EPS, ALU.mult, ALU.add).then_inc(self.var, 1)
        v.wait_ge(self.std, 1)
        step(nc.vector.reciprocal(rstd, std))
        nc.vector.scalar_tensor_tensor(out=m.H, in0=m.H, scalar=0.0, in1=bc(rstd.unsqueeze(2), wide),
                                       op0=ALU.max, op1=ALU.mult).then_inc(self.h, 1)

    def scalar(self, act):
        nc, m = self.nc, self.m
        act.wait_ge(self.var, 1)
        nc.scalar.activation(m.stat[:, 2, :], m.stat[:, 1, :], ACT.Sqrt).then_inc(self.std, 1)
        for c in range(NCH):
            lo, n = chunk(c)
            act.wait_ge(self.turned, c + 1)
            nc.scalar.copy(m.A[0:D, lo:lo + n], m.ps[c % 2][0:D, 0:n]).then_inc(self.stored, 1)

    def tensor(self, pe):
        nc, m = self.nc, self.m
        pe.wait_ge(self.h, 1)
        for c in range(NCH):
            lo, n = chunk(c)
            if c >= 2:
                pe.wait_ge(self.stored, c - 1)
            for j in range(n // P):
                last = nc.tensor.transpose(m.ps[c % 2][0:D, j * P:(j + 1) * P], m.H[:, lo // P + j, :], m.ident[:])
            last.then_inc(self.turned, 1)


def reduced_sine(nc, step, x, k):
    step(nc.vector.tensor_scalar(k, x, 1.0 / (2.0 * PI), ROUND_MAGIC, ALU.mult, ALU.add))
    step(nc.vector.tensor_scalar(k, k, -ROUND_MAGIC, None, ALU.add))
    step(nc.vector.scalar_tensor_tensor(out=x, in0=k, scalar=-TWO_PI_HI, in1=x, op0=ALU.mult, op1=ALU.add))
    step(nc.vector.scalar_tensor_tensor(out=x, in0=k, scalar=-TWO_PI_LO, in1=x, op0=ALU.mult, op1=ALU.add))
    return nc.vector.tensor_scalar(x, x, PI_BELOW, -PI_BELOW, ALU.min, ALU.max)


def load_windows(nc, m, sp, ins, dr, sem, n_sem):
    sp.dma_start(m.dstrel[:].bitcast(I32), ins["dst_t"].rearrange("p (g j) -> p g j", j=J)).then_inc(sem, 16)
    sp.dma_start(m.D[:, 0:NG], bc(dr["base_f"], [P, NG])).then_inc(sem, 16)
    sp.dma_start(m.base_i[:], dr["base_i"]).then_inc(sem, 16)


def finish_windows(nc, m, v, step, sem):
    v.wait_ge(sem, 48)
    step(nc.vector.tensor_copy(m.dstrel[:], m.dstrel[:].bitcast(I32)))
    step(nc.vector.tensor_tensor(m.dstrel[:], m.dstrel[:], bc(m.D[:, 0:NG].unsqueeze(2), [P, NG, J]), ALU.subtract))
    step(nc.vector.tensor_scalar(m.nodeid[:], m.D[0:WIN, 0:NG], m.iotap[0:WIN, :], None, ALU.add))


def first_windows(nc, m, ins, dr, name, zero):
    st = Stage(nc, name + "_win")
    landed, dve = st.sem("landed"), st.sem("dve")
    with nc.Block() as block:
        @block.sync
        def _(sp):
            load_windows(nc, m, sp, ins, dr, landed, 3)
            sp.wait_ge(landed, 48)

        @block.vector
        def _(v):
            step = Chain(v, dve)
            for z in zero:
                step(nc.vector.memset(z, 0.0))
            finish_windows(nc, m, v, step, landed)
    st.close()


def edge_rounds(nc, m, rounds, name, one_round):
    with nc.Fori(0, rounds) as _r:
        st = Stage(nc, name)
        one_round(st)
        st.close()
        st = Stage(nc, name + "_shift")
        dve = st.sem("dve")
        with nc.Block() as block:
            @block.vector
            def _(v):
                step = Chain(v, dve)
                step(nc.vector.tensor_scalar(m.dstrel[:], m.dstrel[:], float(-WIN), None, ALU.add))
                step(nc.vector.tensor_scalar(m.nodeid[:], m.nodeid[:], float(WIN), None, ALU.add))
                step(nc.vector.tensor_scalar(m.base_i[:], m.base_i[:], float(WIN), float(N), ALU.add, ALU.min))
        st.close()


class Ring:

    def __init__(self, st, name):
        self.s = st.sem(name)

    def start(self, eng):
        eng.sem_inc(self.s, AHEAD)

    def done(self, eng, g, back=0):
        eng.wait_ge(self.s, g + (1 + AHEAD - back))

    def inc(self, ins):
        ins.then_inc(self.s, 1)


class Group:

    def __init__(self, i, u, back):
        self.u, self.b = (u - back) % U, (u - back) % 2
        self.g = i * U + (u - back)
        self.turn = i if u >= back else i - 1

    def gathered(self, eng, sems):
        eng.wait_ge(sems[self.u], self.turn * (16 * J) + 16 * J)

    def landed(self, eng, sems):
        eng.wait_ge(sems[self.b], self.turn * 32 + 16 * (self.u // 2 + 1))

    def tiles(self, first=0, n=J):
        return ds(self.turn * (U * J) + self.u * J + first, n)


def slots(eng, body):
    def peeled(i, u):
        return lambda k: Group(i, u, k) if 0 <= i * U + u - k < NG else None

    for u in range(U):
        body(peeled(0, u))
    with eng.Fori(1, TURNS) as i:
        for u in range(U):
            body(lambda k, u=u: Group(i, u, k))
    for u in range(U):
        body(peeled(TURNS, u))


def gather_program(nc, m, pool, rows, table, idx_set, used, gathered, turns):
    with pool.Fori(0, TURNS) as i:
        for u in range(U):
            g = i * U + u
            pool.wait_ge(idx_set, g + 1)
            used.done(pool, g, U)
            pool.sem_inc(turns, 1)
            for j in range(J):
                nc.gpsimd.indirect_dma_start(
                    rows[:, u * J + j, :], None, table,
                    bass.IndirectOffsetOnAxis(ap=m.idx[:, u, j:j + 1], axis=0)).then_inc(gathered[u], 16)


def first_ids(nc, m, act, idx_set):
    for u in range(U):
        nc.scalar.copy(m.idx[:, u, :], m.src[:, u * J:(u + 1) * J]).then_inc(idx_set, 1)


def next_ids(nc, m, act, g, gathered, idx_set):
    g.gathered(act, gathered)
    nc.scalar.copy(m.idx[:, g.u, :], m.src[:, g.tiles(U * J)]).then_inc(idx_set, 1)


def plain_onehot(nc, m, v, out, g):
    return nc.vector.tensor_tensor(out, bc(m.iota[:, 0:WIN].unsqueeze(1), [P, J, WIN]),
                                   bc(m.dstrel[:, ds(g.g, 1), :].rearrange("p a j -> p (a j)").unsqueeze(2),
                                      [P, J, WIN]), ALU.is_equal)


def window_base(m, eng, g):
    return eng.value_load(m.base_i[0:1, ds(g, 1)], min_val=0, max_val=NP)




def layer0_nodes(nc, m, w, dr):
    st = Stage(nc, "l0n")
    ln = Nodes(nc, m, st, m.D)
    up, upd, ph, phd, nm, nmd = (st.sem(n) for n in ("up", "up_read", "ph", "ph_read", "nm", "nm_read"))
    dve, args, trig, out, dved = (st.sem(n) for n in ("dve", "args", "trig", "out", "dve_done"))
    T1, PHT, PHN, AB = m.B, m.C, m.D, m.E
    phn3 = PHN[:, 0:NP].rearrange("p (t f) -> p t f", f=P)
    ab3 = AB[:, 0:NP].rearrange("p (t f) -> p t f", f=P)
    with nc.Block() as block:
        @block.vector
        def _(v):
            ln.vector(v)
            for c in range(NCH):
                lo, n = chunk(c)
                k = n // P
                v.wait_ge(ph, c + 1)
                nc.vector.tensor_scalar(PHT[:, lo:lo + n], m.ps[4 + c % 2][:, 0:n], w["b_ph"][:], None,
                                        ALU.add).then_inc(phd, 1)
                v.wait_ge(nm, 2 * c + 1)
                nc.vector.tensor_tensor(phn3[:, lo // P:lo // P + k, :],
                                        m.ps[6][:, 0:n].rearrange("p (t f) -> p t f", f=P),
                                        bc(w["row_ph"][:].unsqueeze(1), [P, k, P]), ALU.add).then_inc(nmd, 1)
                v.wait_ge(nm, 2 * c + 2)
                nc.vector.tensor_tensor(ab3[:, lo // P:lo // P + k, :],
                                        m.ps[7][:, 0:n].rearrange("p (t f) -> p t f", f=P),
                                        bc(w["row_ab"][:].unsqueeze(1), [P, k, P]), ALU.add).then_inc(nmd, 1)
            v.wait_ge(phd, NCH)
            v.wait_ge(nmd, 2 * NCH)
            step = Chain(v, dve)
            reduced_sine(nc, step, PHN[:, 0:NP], m.F[:, 0:NP]).then_inc(args, 1)
            v.wait_ge(args, 1)
            reduced_sine(nc, step, PHT[:, 0:NP], m.F[:, 0:NP]).then_inc(args, 1)

        @block.scalar
        def _(act):
            ln.scalar(act)
            for c in range(NCH):
                lo, n = chunk(c)
                act.wait_ge(up, c + 1)
                nc.scalar.activation(T1[0:D, lo:lo + n], m.ps[2 + c % 2][0:D, 0:n], ACT.Tanh,
                                     bias=w["b_pf"][0:D, :]).then_inc(upd, 1)
                nc.scalar.activation(T1[D:P, lo:lo + n], m.ps[2 + c % 2][D:P, 0:n], ACT.Relu,
                                     bias=w["b_pf"][D:P, :]).then_inc(upd, 1)
            act.wait_ge(args, 1)
            nc.scalar.activation(PHN[:, 0:NP], PHN[:, 0:NP], ACT.Sin).then_inc(trig, 1)
            act.wait_ge(args, 2)
            nc.scalar.activation(PHT[:, 0:NP], PHT[:, 0:NP], ACT.Sin).then_inc(trig, 1)

        @block.tensor
        def _(pe):
            ln.tensor(pe)
            for c in range(NCH):
                lo, n = chunk(c)
                pe.wait_ge(ln.stored, c + 1)
                if c >= 2:
                    pe.wait_ge(upd, 2 * (c - 1))
                nc.tensor.matmul(m.ps[2 + c % 2][:, 0:n], w["w_pf"][:], m.A[0:D, lo:lo + n],
                                 start=True, stop=True).then_inc(up, 1)
                pe.wait_ge(upd, 2 * (c + 1))
                if c >= 2:
                    pe.wait_ge(phd, c - 1)
                nc.tensor.matmul(m.ps[4 + c % 2][:, 0:n], w["w_pp"][:], T1[0:D, lo:lo + n],
                                 start=True, stop=True).then_inc(ph, 1)
                if c >= 1:
                    pe.wait_ge(nmd, 2 * c - 1)
                for j in range(n // P):
                    last = nc.tensor.matmul(m.ps[6][:, j * P:(j + 1) * P], T1[0:D, lo + j * P:lo + (j + 1) * P],
                                            w["w_pp"][:], start=True, stop=True)
                last.then_inc(nm, 1)
                if c >= 1:
                    pe.wait_ge(nmd, 2 * c)
                for j in range(n // P):
                    last = nc.tensor.matmul(m.ps[7][:, j * P:(j + 1) * P], m.A[0:D, lo + j * P:lo + (j + 1) * P],
                                            w["w_ba"][:], start=True, stop=True)
                last.then_inc(nm, 1)

        @block.sync
        def _(sp):
            sp.wait_ge(nmd, 2 * NCH)
            sp.dma_start(rows_of(dr["tab0"], (2 * D, 3 * D)), ab3[:, :, 0:D]).then_inc(out, 16)
            sp.dma_start(rows_of(dr["tgt0"], (0, D)), ab3[:, :, D:P]).then_inc(out, 16)
            sp.wait_ge(trig, 1)
            sp.dma_start(rows_of(dr["tab0"], (0, 2 * D)), phn3).then_inc(out, 16)
            sp.wait_ge(out, 48)
    st.close()


def degree_weights(nc, m):
    st = Stage(nc, "dw")
    dve = st.sem("dve")
    rest = m.D[:, 0:NG * J]
    with nc.Block() as block:
        @block.vector
        def _(v):
            step = Chain(v, dve)
            step(nc.vector.memset(m.dw[:, :, 3:4], 1.0))
            step(nc.vector.tensor_copy(rest, m.ew[:]))
            for k in range(3):
                step(nc.vector.tensor_copy(m.dw[:, :, k], rest))
                step(nc.vector.tensor_tensor(rest, rest, m.dw[:, :, k], ALU.subtract))
    st.close()


def layer0_edges(nc, m, w, ins, dr, rounds):
    RW = 3 * D
    rows, trow, ot, win, relu, oh1 = m.carve(m.D, [(P, U * J, RW), (WIN, 2, GE), (WIN, 2, GE), (WIN, 2, D),
                                                   (P, J, D), (P, J * WIN)])
    trow = trow.bitcast(I32)
    oh1 = oh1.bitcast(BF16).rearrange("p (b j w) -> p b j w", b=2, j=J)
    degs = m.A[0:4, :]

    def one_round(st):
        gathered = st.keep(m.gathered)
        trow_in = [st.sem(f"targets_in{b}") for b in range(2)]
        win_in = [st.sem(f"window_in{b}") for b in range(2)]
        idx_set, dve, turns = st.sem("ids_set"), st.sem("relu"), st.sem("gather_turns")
        ot_set, z_set, zs_set, k_set, ok_set, seg, added = (
            Ring(st, n) for n in ("expander", "gate_psum", "gate_sum", "gate", "onehot", "segments", "added"))

        with nc.Block() as block:
            @block.sync
            def _(sp):
                with sp.Fori(0, TURNS) as i:
                    for u in range(U):
                        g, b = i * U + u, u % 2
                        ot_set.done(sp, g, 2)
                        sp.dma_start(trow[:, b, :], bc(ins["dst_rows"][ds(g, 1), :], [WIN, GE])).then_inc(trow_in[b], 16)
                        z_set.done(sp, g, 2)
                        base = window_base(m, sp, g)
                        sp.dma_start(win[:, b, :], dr["tgt0"][ds(base, WIN), :]).then_inc(win_in[b], 16)

            @block.gpsimd
            def _(pool):
                gather_program(nc, m, pool, rows, dr["tab0"], idx_set, seg, gathered, turns)

            @block.scalar
            def _(act):
                k_set.start(act)
                first_ids(nc, m, act, idx_set)

                def share(at):
                    if g := at(1):
                        zs_set.done(act, g.g)
                        k_set.inc(nc.scalar.activation(m.kgate[:, g.b, :], m.zsum[:, g.b, :], ACT.Sigmoid,
                                                       bias=w["cb2"][:]))
                        next_ids(nc, m, act, g, gathered, idx_set)

                slots(act, share)

            @block.tensor
            def _(pe):
                z_set.start(pe)
                seg.start(pe)

                def share(at):
                    if g := at(1):
                        z = m.ps[g.b]
                        ot_set.done(pe, g.g)
                        g.landed(pe, win_in)
                        zs_set.done(pe, g.g, 2)
                        g.gathered(pe, gathered)
                        for j in range(J):
                            nc.tensor.matmul(z[:, j * D:(j + 1) * D], ot[:, g.b, j * P:(j + 1) * P], win[:, g.b, :],
                                             start=True, stop=False)
                            last = nc.tensor.matmul(z[:, j * D:(j + 1) * D], m.ident[:],
                                                    rows[:, g.u * J + j, 2 * D:3 * D], start=False, stop=True)
                        z_set.inc(last)
                    if g := at(2):
                        ok_set.done(pe, g.g)
                        added.done(pe, g.g, 2)
                        for j in range(J):
                            nc.tensor.matmul(m.ps[4 + g.b][0:4, 0:WIN], m.dw[:, g.tiles(j, 1), :].rearrange("p a k -> p (a k)"),
                                             oh1[:, g.b, j, :], start=(j == 0), stop=(j == J - 1))
                        for j in range(J):
                            last = nc.tensor.matmul(m.ps[2 + g.b][:, 0:WIN], rows[:, g.u * J + j, 0:2 * D],
                                                    m.onehot[:, g.b, j, :], start=(j == 0), stop=(j == J - 1))
                        seg.inc(last)

                slots(pe, share)

            @block.vector
            def _(v):
                for r in (ot_set, zs_set, ok_set, added):
                    r.start(v)

                def share(at):
                    if g := at(0):
                        g.landed(v, trow_in)
                        z_set.done(v, g.g, 2)
                        ot_set.inc(nc.vector.tensor_scalar(ot[:, g.b, :], trow[:, g.b, :], m.nodeid[:, ds(g.g, 1)],
                                                           None, ALU.is_equal))
                    if g := at(2):
                        k_set.done(v, g.g)
                        seg.done(v, g.g, 2)
                        plain_onehot(nc, m, v, oh1[:, g.b], g)
                        for j in range(J):
                            last = nc.vector.tensor_scalar(m.onehot[:, g.b, j, :], m.iota[:, 0:WIN],
                                                           m.dstrel[:, ds(g.g, 1), j], m.kgate[:, g.b, j:j + 1],
                                                           ALU.is_equal, ALU.mult)
                        ok_set.inc(last)
                    if g := at(3):
                        base = window_base(m, v, g.g)
                        seg.done(v, g.g)
                        added.done(v, g.g, 1)
                        nc.vector.tensor_tensor(degs[:, ds(base, WIN)], degs[:, ds(base, WIN)],
                                                m.ps[4 + g.b][0:4, 0:WIN], ALU.add)
                        added.inc(nc.vector.tensor_tensor(m.E[:, ds(base, WIN)], m.E[:, ds(base, WIN)],
                                                          m.ps[2 + g.b][:, 0:WIN], ALU.add))
                    if g := at(1):
                        z_set.done(v, g.g)
                        zs_set.done(v, g.g, 1)
                        nc.vector.scalar_tensor_tensor(
                            out=relu, in0=m.ps[g.b][:, 0:J * D].rearrange("p (j f) -> p j f", f=D), scalar=0.0,
                            in1=bc(w["row_cw2"][:].unsqueeze(1), [P, J, D]), op0=ALU.max, op1=ALU.mult).then_inc(dve, 1)
                        v.wait_ge(dve, g.g + 1)
                        zs_set.inc(nc.vector.tensor_reduce(out=m.zsum[:, g.b, :], in_=relu, axis=AX, op=ALU.add))

                slots(v, share)

    edge_rounds(nc, m, rounds, "l0e", one_round)


def spread_degrees(nc, m, w):
    st = Stage(nc, "deg")
    pr, prd = st.sem("product"), st.sem("product_read")
    with nc.Block() as block:
        @block.tensor
        def _(pe):
            for c in range(NCH):
                lo, n = chunk(c)
                if c >= 2:
                    pe.wait_ge(prd, c - 1)
                nc.tensor.matmul(m.ps[c % 2][:, 0:n], w["spread"][:], m.A[0:4, lo:lo + n],
                                 start=True, stop=True).then_inc(pr, 1)

        @block.scalar
        def _(act):
            for c in range(NCH):
                lo, n = chunk(c)
                act.wait_ge(pr, c + 1)
                nc.scalar.copy(m.B[:, lo:lo + n], m.ps[c % 2][:, 0:n]).then_inc(prd, 1)
    st.close()


def layer0_out(nc, m, w):
    st = Stage(nc, "l0o")
    mul, fr, frd, o1, o1d, o2, o2d, dve = (
        st.sem(n) for n in ("mul", "freq", "freq_read", "o1", "o1_read", "o2", "o2_read", "dve"))
    O1 = m.D
    with nc.Block() as block:
        @block.vector
        def _(v):
            nc.vector.tensor_tensor(m.E[:, 0:NP], m.E[:, 0:NP], m.C[:, 0:NP], ALU.mult).then_inc(mul, 1)
            for c in range(NCH):
                lo, n = chunk(c)
                t, k = lo // P, n // P
                v.wait_ge(o2, c + 1)
                nc.vector.tensor_tensor(m.H[:, t:t + k, :], m.ps[4 + c % 2][:, 0:k * D].rearrange("p (t f) -> p t f", f=D),
                                        bc(w["row_ob2"][:].unsqueeze(1), [P, k, D]), ALU.add).then_inc(o2d, 1)
            v.wait_ge(o2d, NCH)
            nc.vector.tensor_tensor(m.x[:], m.x[:], m.H, ALU.add).then_inc(dve, 1)
            v.wait_ge(dve, 1)

        @block.scalar
        def _(act):
            for c in range(NCH):
                lo, n = chunk(c)
                act.wait_ge(fr, c + 1)
                nc.scalar.activation(m.A[D:P, lo:lo + n], m.ps[c % 2][D:P, 0:n], ACT.Identity,
                                     bias=w["fb2"][D:P, :]).then_inc(frd, 1)
                act.wait_ge(o1, c + 1)
                nc.scalar.activation(O1[0:D, lo:lo + n], m.ps[2 + c % 2][0:D, 0:n], ACT.Relu,
                                     bias=w["ob1"][:]).then_inc(o1d, 1)

        @block.tensor
        def _(pe):
            for c in range(NCH):
                lo, n = chunk(c)
                if c >= 2:
                    pe.wait_ge(frd, c - 1)
                nc.tensor.matmul(m.ps[c % 2][D:P, 0:n], w["fw2"][D:P, :], m.B[D:P, lo:lo + n],
                                 start=True, stop=True).then_inc(fr, 1)
                pe.wait_ge(mul, 1)
                if c >= 2:
                    pe.wait_ge(o1d, c - 1)
                nc.tensor.matmul(m.ps[2 + c % 2][0:D, 0:n], w["ow1s"][:], m.E[:, lo:lo + n], start=True, stop=False)
                pe.wait_ge(frd, c + 1)
                nc.tensor.matmul(m.ps[2 + c % 2][0:D, 0:n], w["ow1s"][D:P, :], m.A[D:P, lo:lo + n],
                                 start=False, stop=True).then_inc(o1, 1)
                pe.wait_ge(o1d, c + 1)
                if c >= 2:
                    pe.wait_ge(o2d, c - 1)
                for j in range(n // P):
                    last = nc.tensor.matmul(m.ps[4 + c % 2][:, j * D:(j + 1) * D], O1[0:D, lo + j * P:lo + (j + 1) * P],
                                            w["ow2"][:], start=True, stop=True)
                last.then_inc(o2, 1)
    st.close()




def layer1_nodes(nc, m, w, dr):
    st = Stage(nc, "l1n")
    ln = Nodes(nc, m, st, m.D)
    tb, tbd, out, dve = (st.sem(n) for n in ("tab", "tab_read", "out", "dve"))
    tab = m.DE[:, 0:NT * 2 * HM].rearrange("p (t f) -> p t f", f=2 * HM)
    per = 3
    cuts = [(t, min(per, NT - t)) for t in range(0, NT, per)]
    with nc.Block() as block:
        @block.vector
        def _(v):
            ln.vector(v)
            for c, (t, k) in enumerate(cuts):
                v.wait_ge(tb, c + 1)
                nc.vector.tensor_tensor(tab[:, t:t + k, :],
                                        m.ps[2 + c % 2][:, 0:k * 2 * HM].rearrange("p (t f) -> p t f", f=2 * HM),
                                        bc(w["row_m1"][:].unsqueeze(1), [P, k, 2 * HM]), ALU.add).then_inc(tbd, 1)

        @block.scalar
        def _(act):
            ln.scalar(act)

        @block.tensor
        def _(pe):
            ln.tensor(pe)
            pe.wait_ge(ln.stored, NCH)
            for c, (t, k) in enumerate(cuts):
                if c >= 2:
                    pe.wait_ge(tbd, c - 1)
                for j in range(k):
                    last = nc.tensor.matmul(m.ps[2 + c % 2][:, j * 2 * HM:(j + 1) * 2 * HM],
                                            m.A[0:D, (t + j) * P:(t + j + 1) * P], w["w_m1"][:], start=True, stop=True)
                last.then_inc(tb, 1)

        @block.sync
        def _(sp):
            sp.wait_ge(tbd, len(cuts))
            sp.dma_start(rows_of(dr["tab1"], (0, HM)), tab[:, :, 0:HM]).then_inc(out, 16)
            sp.dma_start(rows_of(dr["tgt1"], (0, HM)), tab[:, :, HM:2 * HM]).then_inc(out, 16)
            sp.wait_ge(out, 32)
    st.close()


def layer1_edges(nc, m, w, ins, dr, rounds):
    K = WIN + DE
    rows, trow, left, right, m1, msg = m.carve(m.D, [
        (P, U * J, HM), (WIN, 2, GE), (K, 2, HM), (K, 2, GE), (HC, 2, GE), (P, 2, J, D)])
    trow = trow.bitcast(I32)

    st = Stage(nc, "l1s")
    dve = st.sem("dve")
    with nc.Block() as block:
        @block.vector
        def _(v):
            step = Chain(v, dve)
            step(nc.vector.memset(m1, 1.0))
            for b in range(2):
                step(nc.vector.tensor_copy(left[WIN:K, b, :], w["w_e"][WIN:K, :]))
    st.close()

    def one_round(st):
        gathered = st.keep(m.gathered)
        trow_in = [st.sem(f"targets_in{b}") for b in range(2)]
        win_in = [st.sem(f"window_in{b}") for b in range(2)]
        ea_in = [st.sem(f"edge_features_in{b}") for b in range(2)]
        idx_set, turns = st.sem("ids_set"), st.sem("gather_turns")
        ot_set, pre, g1, msgp, g2, oh, seg, added = (
            Ring(st, n) for n in ("expander", "pre", "gelu1", "msg_psum", "gelu2", "onehot", "segments", "added"))

        with nc.Block() as block:
            @block.sync
            def _(sp):
                with sp.Fori(0, TURNS) as i:
                    for u in range(U):
                        g, b = i * U + u, u % 2
                        ot_set.done(sp, g, 2)
                        sp.dma_start(trow[:, b, :], bc(ins["dst_rows"][ds(g, 1), :], [WIN, GE])).then_inc(trow_in[b], 16)
                        pre.done(sp, g, 2)
                        base = window_base(m, sp, g)
                        sp.dma_start(left[0:WIN, b, :], dr["tgt1"][ds(base, WIN), :]).then_inc(win_in[b], 16)
                        sp.dma_start(right[WIN:K, b, :], ins["ea_T"][:, ds(i * (U * GE) + u * GE, GE)]).then_inc(ea_in[b], 16)

            @block.gpsimd
            def _(pool):
                gather_program(nc, m, pool, rows, dr["tab1"], idx_set, pre, gathered, turns)

            @block.scalar
            def _(act):
                g1.start(act)
                g2.start(act)
                first_ids(nc, m, act, idx_set)

                def share(at):
                    if g := at(2):
                        msgp.done(act, g.g)
                        seg.done(act, g.g, 2)
                        g2.inc(nc.scalar.activation(msg[:, g.b, :, :], m.ps[2 + g.b][:, 0:J * D].rearrange(
                            "p (j f) -> p j f", f=D), ACT.Gelu))
                    if g := at(1):
                        next_ids(nc, m, act, g, gathered, idx_set)
                        pre.done(act, g.g)
                        msgp.done(act, g.g, 2)
                        g1.inc(nc.scalar.activation(m1[0:HM, g.b, :], m.ps[g.b][0:HM, :], ACT.Gelu))

                slots(act, share)

            @block.tensor
            def _(pe):
                for r in (pre, msgp, seg):
                    r.start(pe)

                def share(at):
                    if g := at(3):
                        oh.done(pe, g.g)
                        g2.done(pe, g.g)
                        added.done(pe, g.g, 2)
                        for j in range(J):
                            last = nc.tensor.matmul(m.ps[4 + g.b][0:D, 0:WIN], msg[:, g.b, j, :],
                                                    m.onehot[:, g.b, j, :], start=(j == 0), stop=(j == J - 1))
                        seg.inc(last)
                    if g := at(2):
                        g1.done(pe, g.g)
                        g2.done(pe, g.g, 2)
                        for j in range(J):
                            last = nc.tensor.matmul(m.ps[2 + g.b][:, j * D:(j + 1) * D],
                                                    m1[:, g.b, j * P:(j + 1) * P], w["w_m2"][:], start=True, stop=True)
                        msgp.inc(last)
                    if g := at(1):
                        z = m.ps[g.b][0:HM, :]
                        g1.done(pe, g.g, 2)
                        g.landed(pe, ea_in)
                        g.landed(pe, win_in)
                        ot_set.done(pe, g.g)
                        nc.tensor.matmul(z, left[:, g.b, :], right[:, g.b, :], start=True, stop=False)
                        g.gathered(pe, gathered)
                        for j in range(J):
                            last = nc.tensor.matmul(z[:, j * P:(j + 1) * P], rows[:, g.u * J + j, :], m.ident[:],
                                                    start=False, stop=(j == J - 1))
                        pre.inc(last)

                slots(pe, share)

            @block.vector
            def _(v):
                for r in (ot_set, oh, added):
                    r.start(v)

                def share(at):
                    if g := at(0):
                        g.landed(v, trow_in)
                        pre.done(v, g.g, 2)
                        ot_set.inc(nc.vector.tensor_scalar(right[0:WIN, g.b, :], trow[:, g.b, :],
                                                           m.nodeid[:, ds(g.g, 1)], None, ALU.is_equal))
                    if g := at(2):
                        seg.done(v, g.g, 2)
                        oh.inc(plain_onehot(nc, m, v, m.onehot[:, g.b], g))
                    if g := at(4):
                        base = window_base(m, v, g.g)
                        seg.done(v, g.g)
                        added.done(v, g.g, 1)
                        added.inc(nc.vector.tensor_tensor(m.E[0:D, ds(base, WIN)], m.E[0:D, ds(base, WIN)],
                                                          m.ps[4 + g.b][0:D, 0:WIN], ALU.add))

                slots(v, share)

    edge_rounds(nc, m, rounds, "l1e", one_round)


def layer1_out(nc, m, w, dr):
    st = Stage(nc, "l1o")
    c1, c1d, c2, c2d, g, dve = (st.sem(n) for n in ("c1", "c1_read", "c2", "c2_read", "gelu", "dve"))
    comb = m.D[:, 0:NT * D].rearrange("p (t f) -> p t f", f=D)
    with nc.Block() as block:
        @block.vector
        def _(v):
            step = Chain(v, dve)
            step(nc.vector.tensor_tensor(m.x[:], m.x[:], m.H, ALU.add))
            for c in range(NCH):
                lo, n = chunk(c)
                t, k = lo // P, n // P
                v.wait_ge(c2, c + 1)
                nc.vector.tensor_tensor(comb[:, t:t + k, :], m.ps[2 + c % 2][:, 0:k * D].rearrange("p (t f) -> p t f", f=D),
                                        bc(w["row_bc2"][:].unsqueeze(1), [P, k, D]), ALU.add).then_inc(c2d, 1)
            v.wait_ge(g, 1)
            step(nc.vector.tensor_tensor(m.x[:], m.x[:], comb, ALU.add))

        @block.scalar
        def _(act):
            for c in range(NCH):
                lo, n = chunk(c)
                act.wait_ge(c1, c + 1)
                nc.scalar.activation(m.C[0:HC, lo:lo + n], m.ps[c % 2][0:HC, 0:n], ACT.Gelu,
                                     bias=w["b_c1"][:]).then_inc(c1d, 1)
            act.wait_ge(c2d, NCH)
            nc.scalar.activation(comb, comb, ACT.Gelu).then_inc(g, 1)

        @block.tensor
        def _(pe):
            for c in range(NCH):
                lo, n = chunk(c)
                if c >= 2:
                    pe.wait_ge(c1d, c - 1)
                nc.tensor.matmul(m.ps[c % 2][0:HC, 0:n], w["w_c1a"][:], m.A[0:D, lo:lo + n], start=True, stop=False)
                nc.tensor.matmul(m.ps[c % 2][0:HC, 0:n], w["w_c1b"][:], m.E[0:D, lo:lo + n],
                                 start=False, stop=True).then_inc(c1, 1)
                pe.wait_ge(c1d, c + 1)
                if c >= 2:
                    pe.wait_ge(c2d, c - 1)
                for j in range(n // P):
                    last = nc.tensor.matmul(m.ps[2 + c % 2][:, j * D:(j + 1) * D], m.C[0:HC, lo + j * P:lo + (j + 1) * P],
                                            w["w_c2"][:], start=True, stop=True)
                last.then_inc(c2, 1)
    st.close()




def split_sources(nc, m):
    st = Stage(nc, "split")
    dve = st.sem("dve")
    n = NG * J
    hi_i, lo_i = m.onehot_scr(n)
    with nc.Block() as block:
        @block.vector
        def _(v):
            step = Chain(v, dve)
            step(nc.vector.tensor_single_scalar(hi_i, m.src[:, 0:n], P.bit_length() - 1, op=ALU.arith_shift_right))
            step(nc.vector.tensor_copy(m.hi, hi_i))
            step(nc.vector.tensor_single_scalar(lo_i, m.src[:, 0:n], P - 1, op=ALU.bitwise_and))
            step(nc.vector.tensor_copy(m.lo, lo_i))
    st.close()


def sum_sources(nc, m, dr, rounds, name, weighted, count):
    rows, = m.carve(m.D, [(P, U * J, D)])

    def one_round(st):
        gathered = st.keep(m.gathered)
        idx_set, dve, turns = st.sem("ids_set"), st.sem("dve"), st.sem("gather_turns")
        oh, seg, added = (Ring(st, n) for n in ("onehot", "segments", "added"))
        with nc.Block() as block:
            @block.gpsimd
            def _(pool):
                gather_program(nc, m, pool, rows, dr["tab2"], idx_set, seg, gathered, turns)

            @block.scalar
            def _(act):
                first_ids(nc, m, act, idx_set)

                def share(at):
                    if g := at(0):
                        next_ids(nc, m, act, g, gathered, idx_set)

                slots(act, share)

            @block.tensor
            def _(pe):
                seg.start(pe)

                def share(at):
                    if g := at(1):
                        oh.done(pe, g.g)
                        added.done(pe, g.g, 2)
                        if count:
                            for j in range(J):
                                nc.tensor.matmul(m.ps[2 + g.b][0:WIN, 0:P], m.hi1[:, g.b, j, :], m.lo1[:, g.b, j, :],
                                                 start=(j == 0), stop=(j == J - 1))
                        g.gathered(pe, gathered)
                        for j in range(J):
                            last = nc.tensor.matmul(m.ps[g.b][0:D, 0:WIN], rows[:, g.u * J + j, :],
                                                    m.onehot[:, g.b, j, :], start=(j == 0), stop=(j == J - 1))
                        seg.inc(last)

                slots(pe, share)

            @block.vector
            def _(v):
                oh.start(v)
                added.start(v)
                if count:
                    nc.vector.memset(m.hist, 0.0).then_inc(dve, 1)
                    v.wait_ge(dve, 1)

                def share(at):
                    if g := at(0):
                        seg.done(v, g.g, 2)
                        if count:
                            nc.vector.tensor_tensor(m.hi1[:, g.b], bc(m.iota[:, 0:WIN].unsqueeze(1), [P, J, WIN]),
                                                    bc(m.hi[:, g.tiles()].unsqueeze(2), [P, J, WIN]), ALU.is_equal)
                            nc.vector.tensor_tensor(m.lo1[:, g.b], bc(m.iota[:].unsqueeze(1), [P, J, P]),
                                                    bc(m.lo[:, g.tiles()].unsqueeze(2), [P, J, P]), ALU.is_equal)
                        if weighted:
                            for j in range(J):
                                last = nc.vector.tensor_scalar(
                                    m.onehot[:, g.b, j, :], m.iota[:, 0:WIN], m.dstrel[:, ds(g.g, 1), j],
                                    m.ew[:, g.tiles(j, 1)], ALU.is_equal, ALU.mult)
                        else:
                            last = plain_onehot(nc, m, v, m.onehot[:, g.b], g)
                        oh.inc(last)
                    if g := at(2):
                        base = window_base(m, v, g.g)
                        seg.done(v, g.g)
                        added.done(v, g.g, 1)
                        if count:
                            nc.vector.tensor_tensor(m.hist, m.hist, m.ps[2 + g.b][0:WIN, 0:P], ALU.add)
                        added.inc(nc.vector.tensor_tensor(m.E[0:D, ds(base, WIN)], m.E[0:D, ds(base, WIN)],
                                                          m.ps[g.b][0:D, 0:WIN], ALU.add))

                slots(v, share)

    edge_rounds(nc, m, rounds, name, one_round)


def turn_to_nodes(nc, m, pe, src_region, bank0, turned, stored):
    for c in range(NCH):
        lo, n = chunk(c)
        if c >= 2:
            pe.wait_ge(stored, c - 1)
        for j in range(n // P):
            last = nc.tensor.transpose(m.ps[bank0 + c % 2][:, j * D:(j + 1) * D],
                                       src_region[0:D, lo + j * P:lo + (j + 1) * P], m.ident[0:D, 0:D])
        last.then_inc(turned, 1)




def layer2_in(nc, m, w, dr, conv):
    st = Stage(nc, f"l2n{conv}")
    first = conv == 0
    ln = Nodes(nc, m, st, m.D) if first else None
    dve, rt, dg, us, zt, ztd, zn, znd, out = (
        st.sem(n) for n in ("dve", "root", "deg", "u_set", "zt", "zt_read", "zn", "zn_read", "out"))
    dinv, deg = m.B[0:D, 0:NP], m.B[0:D, 0:NP]
    U_, Z = m.D[0:D, 0:NP], m.C[0:D, 0:NP]
    W_ = w[f"w_g{conv}"]
    with nc.Block() as block:
        @block.vector
        def _(v):
            step = Chain(v, dve)
            if first:
                ln.vector(v)
                nc.vector.tensor_scalar(deg, deg, 1.0, None, ALU.add).then_inc(dg, 1)
                v.wait_ge(rt, 1)
                step(nc.vector.reciprocal(dinv, dinv))
                v.wait_ge(ln.stored, NCH)
            nc.vector.tensor_tensor(U_, m.A[0:D, 0:NP], dinv, ALU.mult).then_inc(us, 1)
            for c in range(NCH):
                lo, n = chunk(c)
                t, k = lo // P, n // P
                v.wait_ge(zn, c + 1)
                nc.vector.tensor_copy(m.TAB[:, t:t + k, :], m.ps[4 + c % 2][:, 0:k * D].rearrange(
                    "p (t f) -> p t f", f=D)).then_inc(znd, 1)

        @block.scalar
        def _(act):
            if first:
                ln.scalar(act)
                act.wait_ge(dg, 1)
                nc.scalar.activation(dinv, deg, ACT.Sqrt).then_inc(rt, 1)
            for c in range(NCH):
                lo, n = chunk(c)
                act.wait_ge(zt, c + 1)
                nc.scalar.copy(Z[:, lo:lo + n], m.ps[2 + c % 2][0:D, 0:n]).then_inc(ztd, 1)

        @block.tensor
        def _(pe):
            if first:
                ln.tensor(pe)
            pe.wait_ge(us, 1)
            for c in range(NCH):
                lo, n = chunk(c)
                if c >= 2:
                    pe.wait_ge(ztd, c - 1)
                nc.tensor.matmul(m.ps[2 + c % 2][0:D, 0:n], W_[:], U_[:, lo:lo + n], start=True, stop=True).then_inc(zt, 1)
                if c >= 2:
                    pe.wait_ge(znd, c - 1)
                for j in range(n // P):
                    last = nc.tensor.matmul(m.ps[4 + c % 2][:, j * D:(j + 1) * D], U_[:, lo + j * P:lo + (j + 1) * P],
                                            W_[:], start=True, stop=True)
                last.then_inc(zn, 1)

        @block.sync
        def _(sp):
            sp.wait_ge(znd, NCH)
            sp.dma_start(rows_of(dr["tab2"], (0, D)), m.TAB).then_inc(out, 16)
            sp.wait_ge(out, 16)
    st.close()


def layer2_out(nc, m, w, dr, conv):
    st = Stage(nc, f"l2o{conv}")
    dve, var, std, done, turned, stored, out = (
        st.sem(n) for n in ("dve", "var", "std", "done", "turned", "stored", "out"))
    col = m.col
    Eo = m.E[0:D, 0:NP]
    sq = m.D[0:D, 0:NP]
    mean, v_, sd, scale = (col[0:D, k:k + 1] for k in range(4))
    parts = m.F[0:D, NW // 2:NW // 2 + N // 50]
    in_parts = lambda ap: ap[:, 0:N].rearrange("p (a b) -> p a b", b=50)
    b, gamma, beta = w[f"b_g{conv}"], w[f"gamma{conv}"], w[f"beta{conv}"]
    with nc.Block() as block:
        @block.vector
        def _(v):
            step = Chain(v, dve)
            step(nc.vector.tensor_tensor(Eo, Eo, m.C[0:D, 0:NP], ALU.add))
            step(nc.vector.tensor_tensor(Eo, Eo, m.B[0:D, 0:NP], ALU.mult))
            step(nc.vector.tensor_scalar(Eo, Eo, b[:], None, ALU.add))
            step(nc.vector.tensor_reduce(out=parts, in_=in_parts(Eo), axis=AX, op=ALU.add))
            step(nc.vector.tensor_reduce(out=mean, in_=parts, axis=AX, op=ALU.add))
            step(nc.vector.tensor_scalar(mean, mean, 1.0 / N, None, ALU.mult))
            step(nc.vector.tensor_scalar(Eo, Eo, mean, None, ALU.subtract))
            step(nc.vector.tensor_tensor(sq, Eo, Eo, ALU.mult))
            step(nc.vector.tensor_reduce(out=parts, in_=in_parts(sq), axis=AX, op=ALU.add))
            step(nc.vector.tensor_reduce(out=v_, in_=parts, axis=AX, op=ALU.add))
            nc.vector.tensor_scalar(v_, v_, 1.0 / N, EPS, ALU.mult, ALU.add).then_inc(var, 1)
            v.wait_ge(std, 1)
            step(nc.vector.reciprocal(scale, sd))
            step(nc.vector.tensor_tensor(scale, scale, gamma[:], ALU.mult))
            step(nc.vector.tensor_scalar(m.A[0:D, 0:NP], Eo, scale, beta[:], ALU.mult, ALU.add))
            if conv == 0:
                step(nc.vector.tensor_scalar(m.A[0:D, 0:NP], m.A[0:D, 0:NP], 0.0, None, ALU.max))
            else:
                v.sem_inc(done, 1)
                for c in range(NCH):
                    lo, n = chunk(c)
                    t, k = lo // P, n // P
                    v.wait_ge(turned, c + 1)
                    nc.vector.tensor_tensor(m.H[:, t:t + k, :], m.H[:, t:t + k, :],
                                            m.ps[c % 2][:, 0:k * D].rearrange("p (t f) -> p t f", f=D),
                                            ALU.add).then_inc(stored, 1)
                v.wait_ge(stored, NCH)
                step(nc.vector.scalar_tensor_tensor(out=m.x[:], in0=m.H, scalar=0.0, in1=m.x[:],
                                                    op0=ALU.max, op1=ALU.add))

        @block.scalar
        def _(act):
            act.wait_ge(var, 1)
            nc.scalar.activation(sd, v_, ACT.Sqrt).then_inc(std, 1)

        @block.tensor
        def _(pe):
            if conv == 1:
                pe.wait_ge(done, 1)
                turn_to_nodes(nc, m, pe, m.A, 0, turned, stored)

        @block.sync
        def _(sp):
            if conv == 0:
                sp.dma_start(dr["degout"].rearrange("a (t p) -> (a t) p", p=P), m.hist[0:NT, :]).then_inc(out, 16)
                sp.wait_ge(out, 16)
    st.close()




def layer3_in(nc, m, w, dr, conv):
    st = Stage(nc, f"l3n{conv}")
    first = conv == 0
    ln = Nodes(nc, m, st, m.D) if first else None
    dve, rt, dg, us, turned, stored, out, degs = (
        st.sem(n) for n in ("dve", "root", "deg", "u_set", "turned", "stored", "out", "degs_in"))
    U_ = m.D[0:D, 0:NP]
    both = (m.B[0:D, 0:NP], m.C[0:D, 0:NP])
    with nc.Block() as block:
        @block.vector
        def _(v):
            step = Chain(v, dve)
            if first:
                ln.vector(v)
                v.wait_ge(degs, 32)
                for r in both:
                    nc.vector.tensor_scalar(r, r, 1.0, None, ALU.max).then_inc(dg, 1)
                v.wait_ge(rt, 2)
                for r in both:
                    step(nc.vector.reciprocal(r, r))
                v.wait_ge(ln.stored, NCH)
            nc.vector.tensor_tensor(U_, m.A[0:D, 0:NP], m.B[0:D, 0:NP], ALU.mult).then_inc(us, 1)
            for c in range(NCH):
                lo, n = chunk(c)
                t, k = lo // P, n // P
                v.wait_ge(turned, c + 1)
                nc.vector.tensor_copy(m.TAB[:, t:t + k, :], m.ps[4 + c % 2][:, 0:k * D].rearrange(
                    "p (t f) -> p t f", f=D)).then_inc(stored, 1)

        @block.scalar
        def _(act):
            if first:
                ln.scalar(act)
                act.wait_ge(dg, 2)
                for r in both:
                    nc.scalar.activation(r, r, ACT.Sqrt).then_inc(rt, 1)

        @block.tensor
        def _(pe):
            if first:
                ln.tensor(pe)
            pe.wait_ge(us, 1)
            turn_to_nodes(nc, m, pe, m.D, 4, turned, stored)

        @block.sync
        def _(sp):
            if first:
                sp.dma_start(m.C[0:D, 0:NP], m.B[D:P, 0:NP]).then_inc(degs, 16)
                sp.dma_start(m.B[0:D, 0:NP], bc(dr["degout"], [D, NP])).then_inc(degs, 16)
            sp.wait_ge(stored, NCH)
            sp.dma_start(rows_of(dr["tab2"], (0, D)), m.TAB).then_inc(out, 16)
            sp.wait_ge(out, 16)
    st.close()


def layer3_out(nc, m, w, conv, out_dram):
    st = Stage(nc, f"l3o{conv}")
    dve, ready, pr, prd, out = (st.sem(n) for n in ("dve", "ready", "product", "product_read", "out"))
    A, Eo, M = m.A[0:D, 0:NP], m.E[0:D, 0:NP], m.D[0:D, 0:NP]
    w1, w2 = w[f"w_n1{conv}"], w[f"w_n2{conv}"]
    full = N // P
    with nc.Block() as block:
        @block.vector
        def _(v):
            step = Chain(v, dve)
            step(nc.vector.tensor_tensor(Eo, Eo, m.C[0:D, 0:NP], ALU.mult))
            step(nc.vector.tensor_tensor(M, Eo, A, ALU.mult))
            nc.vector.tensor_tensor(Eo, Eo, A, ALU.add).then_inc(ready, 1)
            if conv == 1:
                for c in range(NCH):
                    lo, n = chunk(c)
                    t, k = lo // P, n // P
                    v.wait_ge(pr, c + 1)
                    nc.vector.tensor_tensor(m.x[:, t:t + k, :], m.x[:, t:t + k, :],
                                            m.ps[c % 2][:, 0:k * D].rearrange("p (t f) -> p t f", f=D),
                                            ALU.add).then_inc(prd, 1)

        @block.scalar
        def _(act):
            if conv == 0:
                for c in range(NCH):
                    lo, n = chunk(c)
                    act.wait_ge(pr, c + 1)
                    nc.scalar.activation(m.A[0:D, lo:lo + n], m.ps[c % 2][0:D, 0:n], ACT.Relu).then_inc(prd, 1)

        @block.tensor
        def _(pe):
            pe.wait_ge(ready, 1)
            for c in range(NCH):
                lo, n = chunk(c)
                if c >= 2:
                    pe.wait_ge(prd, c - 1)
                if conv == 0:
                    nc.tensor.matmul(m.ps[c % 2][0:D, 0:n], w1[:], Eo[:, lo:lo + n], start=True, stop=False)
                    last = nc.tensor.matmul(m.ps[c % 2][0:D, 0:n], w2[:], M[:, lo:lo + n], start=False, stop=True)
                else:
                    for j in range(n // P):
                        at, to = slice(lo + j * P, lo + (j + 1) * P), m.ps[c % 2][:, j * D:(j + 1) * D]
                        nc.tensor.matmul(to, Eo[:, at], w1[:], start=True, stop=False)
                        last = nc.tensor.matmul(to, M[:, at], w2[:], start=False, stop=True)
                last.then_inc(pr, 1)

        @block.sync
        def _(sp):
            if conv == 1:
                sp.wait_ge(prd, NCH)
                store_x(m, sp, out_dram, out)
    st.close()


def store_x(m, sp, out_dram, out):
    full = N // P
    sp.dma_start(out_dram[0:full * P, :].rearrange("(t p) f -> p t f", p=P), m.x[:, 0:full, :]).then_inc(out, 16)
    sp.dma_start(out_dram[full * P:N, :], m.x[0:N - full * P, full, :]).then_inc(out, 16)
    sp.wait_ge(out, 32)




def gnn_kernel(nc, a, out, stop=None):
    with ExitStack() as ctx:
        m = Memory(nc, ctx)
        m.gathered = [ctx.enter_context(nc.semaphore(f"gathered{u}")) for u in range(U)]
        m.rounds = ctx.enter_context(nc.sbuf_tensor("rounds", [1, 1], I32))
        m.hist = ctx.enter_context(nc.sbuf_tensor("source_counts", [WIN, P], F32))[:]
        n = NG * J
        m.dw = m.F[:, 0:2 * n].bitcast(BF16).rearrange("p (t k) -> p t k", k=4)
        m.hi, m.lo = m.D[:, U * J * D:U * J * D + n], m.D[:, U * J * D + n:U * J * D + 2 * n]
        m.onehot_scr = lambda n: [m.D[:, U * J * D + 2 * n:U * J * D + 3 * n].bitcast(I32)] * 2

        w, loads = {}, []

        def weight(name, shape, *parts):
            t = ctx.enter_context(nc.sbuf_tensor("w_" + name, shape, F32))
            w[name] = t
            for where, what in parts:
                loads.append((t[where], what))

        def col(ap):
            return ap.rearrange("(a b) -> a b", b=1)

        def row(ap, parts):
            return bc(ap.rearrange("(a b) -> a b", a=1), [parts, ap.shape[0]])

        s = slice
        al, top, bot = s(None), s(0, D), s(D, P)
        left, right = (al, s(0, D)), (al, s(D, P))
        weight("w_pf", [D, P], (left, a["L0_gnn_pw1"]), (right, a["L0_gnn_fw1"]))
        weight("w_pp", [D, P], (left, a["L0_gnn_pw2"]), (right, a["L0_gnn_pw2"]))
        weight("w_ba", [D, P], (left, a["L0_gnn_cw1"][D:2 * D, :]), (right, a["L0_gnn_cw1"][0:D, :]))
        weight("fw2", [P, D], ((bot, al), a["L0_gnn_fw2"]))
        weight("ow1s", [P, D], ((top, al), a["L0_gnn_ow1"]), ((bot, al), a["L0_gnn_ow1"]))
        weight("ow2", [D, D], ((al, al), a["L0_gnn_ow2"]))
        weight("b_pf", [P, 1], ((top, al), col(a["L0_gnn_pb1"])), ((bot, al), col(a["L0_gnn_fb1"])))
        weight("b_ph", [P, 1], ((top, al), col(a["L0_gnn_pb2"])), ((bot, al), col(a["L0_gnn_pb2"])))
        weight("row_ph", [P, P], (left, row(a["L0_gnn_pb2"], P)), (right, row(a["L0_gnn_pb2"], P)))
        weight("row_ab", [P, P], (right, row(a["L0_gnn_cb1"], P)))
        weight("fb2", [P, 1], ((bot, al), col(a["L0_gnn_fb2"])))
        weight("ob1", [D, 1], ((al, al), col(a["L0_gnn_ob1"])))
        weight("row_ob2", [P, D], ((al, al), row(a["L0_gnn_ob2"], P)))
        weight("row_cw2", [P, D], ((al, al), bc(a["L0_gnn_cw2"].rearrange("a b -> b a"), [P, D])))
        weight("cb2", [P, 1], ((al, al), row(a["L0_gnn_cb2"], P)))
        weight("w_m1", [D, 2 * HM], ((al, s(0, HM)), a["L1_gnn_W_m1"][0:D, :]),
               ((al, s(HM, 2 * HM)), a["L1_gnn_W_m1"][D:2 * D, :]))
        weight("w_e", [WIN + DE, HM], ((s(WIN, WIN + DE), al), a["L1_gnn_W_m1"][2 * D:2 * D + DE, :]))
        weight("w_m2", [HC, D], ((s(0, HM), al), a["L1_gnn_W_m2"]),
               ((s(HM, HM + 1), al), a["L1_gnn_b_m2"].rearrange("(a b) -> a b", a=1)))
        weight("row_m1", [P, 2 * HM], ((al, s(HM, 2 * HM)), row(a["L1_gnn_b_m1"], P)))
        weight("w_c1a", [D, HC], ((al, al), a["L1_gnn_W_c1"][0:D, :]))
        weight("w_c1b", [D, HC], ((al, al), a["L1_gnn_W_c1"][D:2 * D, :]))
        weight("b_c1", [HC, 1], ((al, al), col(a["L1_gnn_b_c1"])))
        weight("w_c2", [HC, D], ((al, al), a["L1_gnn_W_c2"]))
        weight("row_bc2", [P, D], ((al, al), row(a["L1_gnn_b_c2"], P)))
        weight("spread", [4, P], ((al, al), a["spread"]))
        for k in range(2):
            weight(f"w_g{k}", [D, D], ((al, al), a[f"L2_gnn_W{k + 1}"]))
            weight(f"b_g{k}", [D, 1], ((al, al), col(a[f"L2_gnn_b{k + 1}"])))
            weight(f"gamma{k}", [D, 1], ((al, al), col(a[f"L2_gnn_gamma{k + 1}"])))
            weight(f"beta{k}", [D, 1], ((al, al), col(a[f"L2_gnn_beta{k + 1}"])))
            weight(f"w_n1{k}", [D, D], ((al, al), a[f"L3_gnn_W1_{k + 1}"]))
            weight(f"w_n2{k}", [D, D], ((al, al), a[f"L3_gnn_W2_{k + 1}"]))

        dr = {name: nc.dram_tensor(name, shape, dt, kind="Internal").ap() for name, shape, dt in (
            ("tab0", [NP, 3 * D], F32), ("tgt0", [NW, D], F32), ("tab1", [NP, HM], F32), ("tgt1", [NW, HM], F32),
            ("tab2", [NP, D], F32), ("base_f", [1, NG], F32), ("base_i", [1, NG], I32), ("reach", [1, NG], F32),
            ("degout", [1, NP], F32))}
        ins = dict(a, loads=loads)

        st = Stage(nc, "zero")
        dve = st.sem("dve")
        with nc.Block() as block:
            @block.vector
            def _(v):
                step = Chain(v, dve)
                step(nc.vector.memset(w["row_ab"][:], 0.0))
                step(nc.vector.memset(w["row_m1"][:], 0.0))
                step(nc.vector.memset(w["w_m2"][:], 0.0))
        st.close()

        rounds = setup(nc, m, w, ins, dr)

        st = Stage(nc, "turns")
        dve = st.sem("dve")
        with nc.Block() as block:
            @block.vector
            def _(v):
                step = Chain(v, dve)
                step(nc.vector.tensor_scalar(w["b_ph"][0:D, :], w["b_ph"][0:D, :], PI / 2, None, ALU.add))
                step(nc.vector.tensor_scalar(w["b_ph"][D:P, :], w["b_ph"][D:P, :], PI, None, ALU.add))
                step(nc.vector.tensor_scalar(w["row_ph"][:, D:P], w["row_ph"][:, D:P], PI / 2, None, ALU.add))
        st.close()

        def stopped(k):
            if stop != k:
                return False
            st = Stage(nc, "stop")
            o = st.sem("out")
            with nc.Block() as block:
                @block.sync
                def _(sp):
                    store_x(m, sp, out, o)
            st.close()
            return True

        layer0_nodes(nc, m, w, dr)
        first_windows(nc, m, ins, dr, "l0", [m.E, m.A[0:4, :]])
        degree_weights(nc, m)
        layer0_edges(nc, m, w, ins, dr, rounds)
        layer0_out(nc, m, w)
        spread_degrees(nc, m, w)
        if stopped(0):
            return
        layer1_nodes(nc, m, w, dr)
        first_windows(nc, m, ins, dr, "l1", [m.E])
        layer1_edges(nc, m, w, ins, dr, rounds)
        layer1_out(nc, m, w, dr)
        if stopped(1):
            return
        for conv in range(2):
            layer2_in(nc, m, w, dr, conv)
            first_windows(nc, m, ins, dr, f"l2{conv}", [m.E])
            if conv == 0:
                split_sources(nc, m)
            sum_sources(nc, m, dr, rounds, f"l2e{conv}", True, count=(conv == 0))
            layer2_out(nc, m, w, dr, conv)
        if stopped(2):
            return
        for conv in range(2):
            layer3_in(nc, m, w, dr, conv)
            first_windows(nc, m, ins, dr, f"l3{conv}", [m.E])
            sum_sources(nc, m, dr, rounds, f"l3e{conv}", False, count=False)
            layer3_out(nc, m, w, conv, out)




STOP = None


def kernel(**inputs):
    import numpy as np
    import concourse.bacc as bacc
    from concourse.bass_utils import run_bass_kernel_spmd

    a = {k: np.ascontiguousarray(v) for k, v in inputs.items()}
    pad = EP - E
    tiles = lambda v: np.ascontiguousarray(v.reshape(NG * J, P).T)
    src = np.pad(a.pop("src"), (0, pad), constant_values=N)
    dst = np.pad(a.pop("dst"), (0, pad), constant_values=NO_TARGET)
    ew = np.pad(a.pop("edge_weight"), (0, pad))
    ea = np.pad(a.pop("edge_attr_32"), ((0, pad), (0, 0)))
    a["x"] = np.pad(a["x"], ((0, NP - N), (0, 0)))
    a["src_t"], a["dst_t"], a["ew_t"] = tiles(src), tiles(dst), tiles(ew)
    a["dst_rows"] = np.ascontiguousarray(dst.reshape(NG, GE))
    a["spread"] = np.repeat(np.array([[1, 0], [1, 0], [1, 0], [0, 1]], np.float32), D, axis=1)
    a["ea_T"] = np.ascontiguousarray(ea.T)

    nc = bacc.Bacc("TRN2", target_bir_lowering=False, num_devices=1)
    arrays, aps = {}, {}
    for name, v in a.items():
        arrays[f"in_{name}"] = v
        aps[name] = nc.dram_tensor(f"in_{name}", v.shape, mybir.dt.from_np(v.dtype), kind="ExternalInput").ap()
    out = nc.dram_tensor("out_x", (N, D), F32, kind="ExternalOutput").ap()
    gnn_kernel(nc, aps, out, STOP)
    r = run_bass_kernel_spmd(nc, [arrays], core_ids=[0])
    return r.results[0]["out_x"]
```

```python
from contextlib import ExitStack

import concourse.bass as bass
from concourse import mybir

F32 = mybir.dt.float32
I32 = mybir.dt.int32
BF16 = mybir.dt.bfloat16
F16 = mybir.dt.float16
ALU = mybir.AluOpType
ACT = mybir.ActivationFunctionType
AX = mybir.AxisListType.X

P = 128
N = 6250
E = 200000
D = 64
DE = 32
NT = -(-N // P)
NP = NT * P
WIN = 64
NW = NP + WIN
J = 4
GE = J * P
U = 4
NG = -(-E // (GE * U)) * U
EP = NG * GE
TURNS = NG // U
HM = 80
HC = 96
CH = 512
NCH = -(-NP // CH)
AHEAD = 4
EPS = 1e-5
PI = 3.141592653589793
TWO_PI_HI = 6.28125
TWO_PI_LO = 2.0 * PI - TWO_PI_HI
ROUND_MAGIC = 12582912.0
PI_BELOW = 3.1415925
NO_TARGET = 1 << 20


class Plan:

    def __init__(self, dense, win, exact, tiles):
        self.dense, self.win, self.exact, self.tiles = dense, win, exact, tiles
        self.quarters = tiles // dense
        self.batch = 4 * dense
        self.width = NT * win
        self.depth = dense if exact else 2 * dense
        self.first = tiles // J
        self.groups = -(-E // GE) - self.first
        assert tiles % self.batch == 0 and tiles % J == 0 and self.width <= CH


L2_PLAN = Plan(dense=4, win=6, exact=True, tiles=768)
L3_PLAN = Plan(dense=7, win=7, exact=False, tiles=980)


def chunk(c):
    return c * CH, min(CH, NP - c * CH)


HALVES = ((NCH // 2, slice(0, NCH // 2 * (CH // P))), (NCH, slice(NCH // 2 * (CH // P), NT)))


def ds(start, size):
    return bass.ds(start, size)


def bc(ap, shape):
    return ap.to_broadcast(shape)


class Memory:

    def __init__(self, nc, ctx):
        def sb(name, shape, dt=F32):
            return ctx.enter_context(nc.sbuf_tensor(name, shape, dt))

        self.big = sb("node_arrays", [P, 6 * NW])
        self.C, self.E, self.A, self.D, self.B, self.F = (self.big[:, k * NW:(k + 1) * NW] for k in range(6))
        self.CE, self.AD, self.DBF = self.big[:, 0:2 * NW], self.big[:, 2 * NW:4 * NW], self.big[:, 3 * NW:6 * NW]
        self.x = sb("x_nodes", [P, NT, D])
        self.src = sb("src_ids", [P, (NG + U) * J], I32)
        self.ew = sb("edge_weights", [P, NG * J])
        self.dstrel = sb("target_in_window", [P, NG, J])
        self.nodeid = sb("window_node_ids", [WIN, NG])
        self.base_i = sb("window_base", [1, NG], I32)
        self.tile_i = sb("tile_window_base", [1, max(L2_PLAN.tiles, L3_PLAN.tiles)], I32)
        self.onehot = sb("onehot", [P, 2, J, WIN])
        self.marks = sb("onehot_src", [P, max(2 * J * (WIN + P), L3_PLAN.depth * P)], BF16)
        split = 2 * J * WIN
        self.hi1 = self.marks[:, 0:split].rearrange("p (b j w) -> p b j w", b=2, j=J)
        self.lo1 = self.marks[:, split:split + 2 * J * P].rearrange("p (b j w) -> p b j w", b=2, j=J)
        self.bases = self.marks[:].bitcast(F32)[:, 0:NG]
        self.idx = sb("gather_ids", [P, U, J], I32)
        self.ident = sb("identity", [P, P])
        self.iota = sb("iota_free", [P, L3_PLAN.width])
        self.iota16 = sb("iota_free_16", [P, L3_PLAN.width], F16)
        self.iotap = sb("iota_partition", [P, 1])
        self.stat = sb("node_stats", [P, 4, NT])
        self.col = sb("channel_stats", [P, 16])
        self.kgate = sb("gates", [P, 2, J])
        self.zsum = sb("gate_inputs", [P, 2, J])
        self.near = sb("near_columns", [P, 2, U * J])
        self.near_tiles = sb("near_tile_columns", [P, 3, max(L2_PLAN.batch, L3_PLAN.batch)])
        self.ps = [ctx.enter_context(nc.psum_tensor(f"bank{k}", [P, CH], F32)) for k in range(8)]

        self.H = self.F[:, 0:NT * D].rearrange("p (t f) -> p t f", f=D)
        self.TAB = self.F[:, NW // 2:NW // 2 + NT * D].rearrange("p (t f) -> p t f", f=D)

    def carve(self, region, sizes):
        out, at = [], 0
        for parts, *shape in sizes:
            n = 1
            for s in shape:
                n *= s
            piece = region[0:parts, at:at + n]
            if len(shape) == 2:
                piece = piece.rearrange("p (a b) -> p a b", b=shape[1])
            elif len(shape) == 3:
                piece = piece.rearrange("p (a b c) -> p a b c", b=shape[1], c=shape[2])
            out.append(piece)
            at += n
        assert at <= region.shape[1], at
        return out


class Chain:

    def __init__(self, eng, sem):
        self.eng, self.sem, self.n = eng, sem, 0

    def __call__(self, ins):
        self.n += 1
        ins.then_inc(self.sem, 1)
        self.eng.wait_ge(self.sem, self.n)


class Stage:

    def __init__(self, nc, name):
        self.nc, self.name, self.all, self.kept = nc, name, [], []
        self.ctx = ExitStack()

    def sem(self, name):
        s = self.ctx.enter_context(self.nc.semaphore(f"{self.name}_{name}"))
        self.all.append(s)
        return s

    def keep(self, sems):
        self.all += sems
        self.kept = sems
        return sems

    def close(self):
        kept = sorted(s.num for s in self.kept)
        if kept:
            self.nc.gpsimd.dma_reset(range(kept[0], kept[-1] + 1))
        for s in self.all:
            self.nc.gpsimd.sem_clear(s)
        self.nc.all_engine_barrier()
        self.ctx.close()


def rows_of(table, cols):
    return table[0:NP, cols[0]:cols[1]].rearrange("(t p) f -> p t f", p=P)




def setup(nc, m, w, ins, dr):
    st = Stage(nc, "setup")
    loads, consts, idz, mins, sent, back, dve = (
        st.sem(n) for n in ("loads", "consts", "ident_zero", "mins", "sent", "back", "dve"))
    rows_in, zero_out = st.sem("rows_in"), st.sem("zero_out")
    per = NG // 98
    rows = m.A[0:98, 0:per * GE].bitcast(I32).rearrange("p (c e) -> p c e", e=GE)
    inside = m.B[0:98, 0:per * GE].rearrange("p (c e) -> p c e", e=GE)
    least, most, reach = m.C[0:98, 0:per], m.C[0:98, 8:8 + per], m.C[0:98, 16:16 + per]
    least_i = m.C[0:98, 24:24 + per].bitcast(I32)
    T = NG * J // 98
    tleast, tmost, treach = (m.C[0:98, 64 * k:64 * k + T] for k in (1, 2, 3))
    tleast_i = m.C[0:98, 256:256 + T].bitcast(I32)
    by_tile = lambda ap: ap.rearrange("p c (j e) -> p (c j) e", e=P)
    reach_row = m.C[0:1, 512:512 + NG]
    treach_row = m.C[0:1, 1024:1024 + NG * J]
    far = m.C[0:1, 4096:4099]
    n_loads = ins["early"] + 2
    x_in = st.sem("x_in")
    ln = Nodes(nc, m, st, m.D)
    with nc.Block() as block:
        @block.sync
        def _(sp):
            sp.dma_start(rows, ins["dst_rows"].rearrange("(p c) e -> p c e", c=per)).then_inc(rows_in, 16)
            sp.dma_start(m.x[:], ins["x"].rearrange("(t p) f -> p t f", p=P)).then_inc(x_in, 16)
            sp.dma_start(m.src[:, 0:NG * J], ins["src_t"]).then_inc(loads, 16)
            sp.dma_start(m.ew[:], ins["ew_t"]).then_inc(loads, 16)
            for to, what in ins["loads"][:ins["early"]]:
                sp.dma_start(to, what).then_inc(loads, 16)
            sp.wait_ge(mins, 1)
            sp.dma_start(dr["base_f"].rearrange("a (p c) -> (a p) c", c=per), least).then_inc(sent, 16)
            sp.dma_start(dr["base_i"].rearrange("a (p c) -> (a p) c", c=per), least_i).then_inc(sent, 16)
            sp.dma_start(dr["reach"].rearrange("a (p c) -> (a p) c", c=per), reach).then_inc(sent, 16)
            for to, what in (("tbase_f", tleast), ("tbase_i", tleast_i), ("treach", treach)):
                sp.dma_start(dr[to].rearrange("a (p c) -> (a p) c", c=T), what).then_inc(sent, 16)
            sp.wait_ge(sent, 96)
            sp.dma_start(reach_row, dr["reach"]).then_inc(back, 16)
            sp.dma_start(treach_row, dr["treach"]).then_inc(back, 16)
            sp.wait_ge(consts, 3)
            for t, width in ((dr["tgt0"], D), (dr["tgt1"], HM)):
                sp.dma_start(t[NP:NW, :], m.E[0:WIN, 0:width]).then_inc(zero_out, 16)
            sp.wait_ge(zero_out, 32)
            sp.wait_ge(loads, 16 * n_loads)

        @block.scalar
        def _(act):
            ln.root(act)

        @block.gpsimd
        def _(pool):
            nc.gpsimd.memset(m.ident[:], 0.0).then_inc(idz, 1)
            nc.gpsimd.iota(m.iota[:], [[1, L3_PLAN.width]], base=0, channel_multiplier=0,
                           allow_small_or_imprecise_dtypes=True).then_inc(consts, 1)
            nc.gpsimd.iota(m.iotap[:], [[1, 1]], base=0, channel_multiplier=1,
                           allow_small_or_imprecise_dtypes=True).then_inc(consts, 1)
            pool.wait_ge(idz, 1)
            nc.gpsimd.affine_select(out=m.ident[:], in_=m.ident[:], compare_op=ALU.not_equal, fill=1.0,
                                    base=0, pattern=[[-1, P]], channel_multiplier=1).then_inc(idz, 1)
            pool.wait_ge(idz, 2)

        @block.vector
        def _(v):
            step = Chain(v, dve)
            nc.vector.memset(m.E[0:WIN, 0:P], 0.0).then_inc(consts, 1)
            step(nc.vector.memset(m.src[:, NG * J:], 0))
            v.wait_ge(rows_in, 16)
            step(nc.vector.tensor_reduce(out=least, in_=rows, axis=AX, op=ALU.min))
            step(nc.vector.tensor_reduce(out=tleast, in_=by_tile(rows), axis=AX, op=ALU.min))
            step(nc.vector.scalar_tensor_tensor(out=inside, in0=rows, scalar=float(N), in1=rows,
                                                op0=ALU.is_lt, op1=ALU.mult))
            step(nc.vector.tensor_reduce(out=most, in_=inside, axis=AX, op=ALU.max))
            step(nc.vector.tensor_reduce(out=tmost, in_=by_tile(inside), axis=AX, op=ALU.max))
            for lo_, hi_, i_, r_ in ((least, most, least_i, reach), (tleast, tmost, tleast_i, treach)):
                step(nc.vector.tensor_scalar(lo_, lo_, float(N), None, ALU.min))
                step(nc.vector.tensor_copy(i_, lo_))
                step(nc.vector.scalar_tensor_tensor(out=r_, in0=lo_, scalar=-1.0, in1=hi_,
                                                    op0=ALU.mult, op1=ALU.add))
            v.sem_inc(mins, 1)
            v.wait_ge(consts, 3)
            step(nc.vector.tensor_copy(m.iota16[:], m.iota[:]))
            v.wait_ge(x_in, 16)
            ln.vector(v)
            v.wait_ge(back, 32)
            for k, (row, win) in enumerate(((reach_row, WIN), (treach_row[:, 0:L2_PLAN.tiles], L2_PLAN.win),
                                            (treach_row[:, 0:L3_PLAN.tiles], L3_PLAN.win))):
                f = far[:, k:k + 1]
                step(nc.vector.tensor_reduce(out=f, in_=row, axis=AX, op=ALU.max))
                step(nc.vector.tensor_scalar(f, f, 0.0, 0.5, ALU.max, ALU.add))
                step(nc.vector.tensor_scalar(f, f, 1.0 / win, -0.5, ALU.mult, ALU.add))
                step(nc.vector.tensor_scalar(f, f, ROUND_MAGIC, None, ALU.add))
                step(nc.vector.tensor_scalar(f, f, 1.0 - ROUND_MAGIC, None, ALU.add))
                if k:
                    step(nc.vector.tensor_tensor(f, f, far[:, 0:1], ALU.max))
            step(nc.vector.tensor_copy(m.rounds[:], far))
    st.close()
    return [nc.values_load(m.rounds[0:1, k:k + 1], min_val=1, max_val=-(-N // win))
            for k, win in enumerate((WIN, L2_PLAN.win, L3_PLAN.win))]




class Nodes:

    def __init__(self, nc, m, st, scratch, normed=False):
        self.normed = normed
        self.nc, self.m, self.scratch = nc, m, scratch
        self.chain, self.var, self.std, self.h = (st.sem(n) for n in ("ln_dve", "ln_var", "ln_std", "ln_h"))
        self.turned, self.stored = st.sem("h_turned"), st.sem("hT_stored")

    def vector(self, v):
        nc, m = self.nc, self.m
        step = Chain(v, self.chain)
        mean, var, std, rstd = (m.stat[:, k, :] for k in range(4))
        scr = self.scratch[:, 0:NT * D].rearrange("p (t f) -> p t f", f=D)
        wide = [P, NT, D]
        step(nc.vector.tensor_reduce(out=mean, in_=m.x[:], axis=AX, op=ALU.add))
        step(nc.vector.tensor_scalar(mean, mean, 1.0 / D, None, ALU.mult))
        step(nc.vector.tensor_tensor(m.H, m.x[:], bc(mean.unsqueeze(2), wide), ALU.subtract))
        step(nc.vector.tensor_tensor(scr, m.H, m.H, ALU.mult))
        step(nc.vector.tensor_reduce(out=var, in_=scr, axis=AX, op=ALU.add))
        nc.vector.tensor_scalar(var, var, 1.0 / D, EPS, ALU.mult, ALU.add).then_inc(self.var, 1)
        v.wait_ge(self.std, 1)
        step(nc.vector.reciprocal(rstd, std))
        nc.vector.scalar_tensor_tensor(out=m.H, in0=m.H, scalar=0.0, in1=bc(rstd.unsqueeze(2), wide),
                                       op0=ALU.max, op1=ALU.mult).then_inc(self.h, 1)

    def root(self, act):
        act.wait_ge(self.var, 1)
        self.nc.scalar.activation(self.m.stat[:, 2, :], self.m.stat[:, 1, :], ACT.Sqrt).then_inc(self.std, 1)

    def store(self, act, c):
        lo, n = chunk(c)
        act.wait_ge(self.turned, c + 1)
        self.nc.scalar.copy(self.m.A[0:D, lo:lo + n], self.m.ps[c % 2][0:D, 0:n]).then_inc(self.stored, 1)

    def scalar(self, act):
        self.root(act)
        for c in range(NCH):
            self.store(act, c)

    def turn(self, pe, c):
        nc, m = self.nc, self.m
        lo, n = chunk(c)
        if c == 0 and not self.normed:
            pe.wait_ge(self.h, 1)
        if c >= 2:
            pe.wait_ge(self.stored, c - 1)
        for j in range(n // P):
            last = nc.tensor.transpose(m.ps[c % 2][0:D, j * P:(j + 1) * P], m.H[:, lo // P + j, :], m.ident[:])
        last.then_inc(self.turned, 1)

    def tensor(self, pe):
        for c in range(NCH):
            self.turn(pe, c)


def reduced_sine(nc, step, x, k):
    step(nc.vector.tensor_scalar(k, x, 1.0 / (2.0 * PI), ROUND_MAGIC, ALU.mult, ALU.add))
    step(nc.vector.tensor_scalar(k, k, -ROUND_MAGIC, None, ALU.add))
    step(nc.vector.scalar_tensor_tensor(out=x, in0=k, scalar=-TWO_PI_HI, in1=x, op0=ALU.mult, op1=ALU.add))
    step(nc.vector.scalar_tensor_tensor(out=x, in0=k, scalar=-TWO_PI_LO, in1=x, op0=ALU.mult, op1=ALU.add))
    return nc.vector.tensor_scalar(x, x, PI_BELOW, -PI_BELOW, ALU.min, ALU.max)


def load_windows(nc, m, sp, ins, dr, sem):
    sp.dma_start(m.dstrel[:].bitcast(I32), ins["dst_t"].rearrange("p (g j) -> p g j", j=J)).then_inc(sem, 16)
    sp.dma_start(m.bases, bc(dr["base_f"], [P, NG])).then_inc(sem, 16)
    sp.dma_start(m.base_i[:], dr["base_i"]).then_inc(sem, 16)


def finish_windows(nc, m, v, step, sem):
    v.wait_ge(sem, 48)
    step(nc.vector.tensor_copy(m.dstrel[:], m.dstrel[:].bitcast(I32)))
    step(nc.vector.tensor_tensor(m.dstrel[:], m.dstrel[:], bc(m.bases.unsqueeze(2), [P, NG, J]), ALU.subtract))
    step(nc.vector.tensor_scalar(m.nodeid[:], m.bases[0:WIN, :], m.iotap[0:WIN, :], None, ALU.add))


def edge_rounds(nc, m, rounds, name, one_round, shift=None):
    with nc.Fori(0, rounds) as _r:
        st = Stage(nc, name)
        moved = st.sem("windows_moved")

        def next_windows(v):
            step = Chain(v, moved)
            if shift:
                shift(step)
                return
            step(nc.vector.tensor_scalar(m.dstrel[:], m.dstrel[:], float(-WIN), None, ALU.add))
            step(nc.vector.tensor_scalar(m.nodeid[:], m.nodeid[:], float(WIN), None, ALU.add))
            step(nc.vector.tensor_scalar(m.base_i[:], m.base_i[:], float(WIN), float(N), ALU.add, ALU.min))

        one_round(st, next_windows)
        st.close()


class Ring:

    def __init__(self, st, name):
        self.s = st.sem(name)

    def start(self, eng):
        eng.sem_inc(self.s, AHEAD)

    def done(self, eng, g, back=0):
        if not isinstance(g, int) or g >= back:
            eng.wait_ge(self.s, g + (1 + AHEAD - back))

    def inc(self, ins):
        ins.then_inc(self.s, 1)


class Group:

    def __init__(self, i, u, back, per=U, first=0):
        k = u - back
        self.q = i * per + k
        self.g = self.q + first if first else self.q
        self.u, self.b = k % U, k % 2
        self.turn = i * (per // U) + k // U
        self.first = first

    def gathered(self, eng, sems):
        eng.wait_ge(sems[self.u], self.turn * (16 * J) + 16 * J)

    def landed(self, eng, sems):
        eng.wait_ge(sems[self.b], self.turn * 32 + 16 * (self.u // 2 + 1))

    def tiles(self, first=0, n=J):
        return ds(self.turn * (U * J) + (self.first + self.u) * J + first, n)


def slots(eng, body, per=U, count=NG, lags=U):
    def peeled(i, u):
        return lambda k, make=Group, n=count: make(i, u, k) if 0 <= i * per + u - k < n else None

    turns = count // per
    for u in range(per):
        body(peeled(0, u))
    with eng.Fori(1, turns) as i:
        for u in range(per):
            body(lambda k, make=Group, n=count, u=u: make(i, u, k))
    for s in range(turns * per, count + lags):
        body(peeled(s // per, s % per))


def gather_program(nc, m, pool, rows, table, idx_set, used, gathered, turns, groups=NG):
    def group(i, u):
        g = i * U + u
        pool.wait_ge(idx_set, g + 1)
        used.done(pool, g, U)
        pool.sem_inc(turns, 1)
        for j in range(J):
            nc.gpsimd.indirect_dma_start(
                rows[:, u * J + j, :], None, table,
                bass.IndirectOffsetOnAxis(ap=m.idx[:, u, j:j + 1], axis=0)).then_inc(gathered[u], 16)

    with pool.Fori(0, groups // U) as i:
        for u in range(U):
            group(i, u)
    for u in range(groups % U):
        group(groups // U, u)


def first_ids(nc, m, act, idx_set, first=0):
    for u in range(U):
        nc.scalar.copy(m.idx[:, u, :], m.src[:, (first + u) * J:(first + u + 1) * J]).then_inc(idx_set, 1)


def next_ids(nc, m, act, g, gathered, idx_set):
    g.gathered(act, gathered)
    nc.scalar.copy(m.idx[:, g.u, :], m.src[:, g.tiles(U * J)]).then_inc(idx_set, 1)


def plain_onehot(nc, m, v, out, g):
    return nc.vector.tensor_tensor(out, bc(m.iota[:, 0:WIN].unsqueeze(1), [P, J, WIN]),
                                   bc(m.dstrel[:, ds(g.g, 1), :].rearrange("p a j -> p (a j)").unsqueeze(2),
                                      [P, J, WIN]), ALU.is_equal)


def near_columns(nc, m, v, g, used, sem, *sources):
    if g.u:
        return
    used.done(v, g.q, 1)
    for k, source in enumerate(sources):
        last = nc.vector.tensor_copy(m.near[:, k, :], source[:, g.tiles(0, U * J)])
    last.then_inc(sem, 1)
    v.wait_ge(sem, g.turn + 1)


IN_BOUNDS = "bases are clamped to 0..N where they are made and moved on"


def window_bases(nc, eng, row, first, n):
    _, values = nc.values_load_multi_w_load_instructions(
        row[0:1, ds(first, n)], engines=[eng.engine], min_val=0, max_val=N,
        skip_runtime_bounds_check_because=IN_BOUNDS)
    return values


def window_base(nc, m, eng, g):
    return window_bases(nc, eng, m.base_i, g, 1)[0]




def degree_weights(nc, m, step):
    rest = m.F[:, 0:NG * J]
    step(nc.vector.memset(m.dw[:, :, 3:4], 1.0))
    step(nc.vector.tensor_copy(rest, m.ew[:]))
    for k in range(3):
        step(nc.vector.tensor_copy(m.dw[:, :, k], rest))
        step(nc.vector.tensor_tensor(rest, rest, m.dw[:, :, k], ALU.subtract))


def layer0_nodes(nc, m, w, ins, dr):
    st = Stage(nc, "l0n")
    ln = Nodes(nc, m, st, m.D, normed=True)
    up, upd, ph, phd, ab, abd = (st.sem(n) for n in ("up", "up_read", "ph", "ph_read", "ab", "ab_read"))
    dve, sine, args, trig, tn, tnd, ab_out, out, loads, landed, zeroed = (st.sem(n) for n in (
        "dve", "sine", "args", "trig", "trig_nodes", "trig_nodes_read", "gate_products_out", "out", "loads", "landed", "zeroed"))
    T1, Q, QN, AB = m.B, m.C, m.D, m.E
    qn3 = QN[:, 0:NP].rearrange("p (t f) -> p t f", f=P)
    ab3 = AB[:, 0:NP].rearrange("p (t f) -> p t f", f=P)
    late = ins["loads"][ins["early"]:]
    turns = m.onehot[:].rearrange("p b j w -> p (b j w)")
    with nc.Block() as block:
        @block.vector
        def _(v):
            step = Chain(v, dve)
            step(nc.vector.tensor_scalar(w["b_ph"][0:D, :], w["b_ph"][0:D, :], PI / 2, None, ALU.add))
            finish_windows(nc, m, v, step, landed)
            sine_step = Chain(v, sine)
            for c in range(NCH):
                lo, n = chunk(c)
                k = n // P
                v.wait_ge(ab, c + 1)
                nc.vector.tensor_tensor(ab3[:, lo // P:lo // P + k, :],
                                        m.ps[6 + c % 2][:, 0:n].rearrange("p (t f) -> p t f", f=P),
                                        bc(w["row_ab"][:].unsqueeze(1), [P, k, P]), ALU.add).then_inc(abd, 1)
                v.wait_ge(ph, c + 1)
                nc.vector.tensor_scalar(Q[:, lo:lo + n], m.ps[4 + c % 2][:, 0:n], w["b_ph"][:], None,
                                        ALU.add).then_inc(phd, 1)
                v.wait_ge(phd, c + 1)
                reduced_sine(nc, sine_step, Q[:, lo:lo + n], turns[:, 0:n]).then_inc(args, 1)
                v.wait_ge(args, c + 1)
            v.wait_ge(ln.stored, NCH)
            degree_weights(nc, m, step)

        @block.gpsimd
        def _(pool):
            pool.wait_ge(ab, NCH)
            nc.gpsimd.memset(m.A[0:4, :], 0.0).then_inc(zeroed, 1)
            pool.wait_ge(ab_out, 64)
            nc.gpsimd.memset(m.E, 0.0).then_inc(zeroed, 1)
            pool.wait_ge(zeroed, 2)

        @block.scalar
        def _(act):
            ln.store(act, 0)
            for c in range(NCH):
                if c + 1 < NCH:
                    ln.store(act, c + 1)
                lo, n = chunk(c)
                act.wait_ge(up, c + 1)
                nc.scalar.activation(T1[0:D, lo:lo + n], m.ps[2 + c % 2][0:D, 0:n], ACT.Tanh,
                                     bias=w["b_pf"][0:D, :]).then_inc(upd, 1)
                nc.scalar.activation(T1[D:P, lo:lo + n], m.ps[2 + c % 2][D:P, 0:n], ACT.Relu,
                                     bias=w["b_pf"][D:P, :]).then_inc(upd, 1)
            for c in range(NCH + 1):
                if c < NCH:
                    lo, n = chunk(c)
                    act.wait_ge(args, c + 1)
                    nc.scalar.activation(Q[:, lo:lo + n], Q[:, lo:lo + n], ACT.Sin).then_inc(trig, 1)
                if c >= 1:
                    lo, n = chunk(c - 1)
                    t, k = lo // P, n // P
                    act.wait_ge(tn, c)
                    turned = m.ps[6 + (c - 1) % 2][:, 0:n].rearrange("p (t f) -> p t f", f=P)
                    nc.scalar.copy(qn3[:, t:t + k, 0:D], turned[:, :, D:P])
                    nc.scalar.activation(qn3[:, t:t + k, D:P], turned[:, :, 0:D], ACT.Identity,
                                         scale=-1.0).then_inc(tnd, 1)

        @block.tensor
        def _(pe):
            def hidden(c):
                lo, n = chunk(c)
                pe.wait_ge(ln.stored, c + 1)
                if c >= 2:
                    pe.wait_ge(upd, 2 * (c - 1))
                nc.tensor.matmul(m.ps[2 + c % 2][:, 0:n], w["w_pf"][:], m.A[0:D, lo:lo + n],
                                 start=True, stop=True).then_inc(up, 1)
                if c >= 2:
                    pe.wait_ge(abd, c - 1)
                for j in range(n // P):
                    last = nc.tensor.matmul(m.ps[6 + c % 2][:, j * P:(j + 1) * P], m.A[0:D, lo + j * P:lo + (j + 1) * P],
                                            w["w_ba"][:], start=True, stop=True)
                last.then_inc(ab, 1)

            ln.turn(pe, 0)
            ln.turn(pe, 1)
            hidden(0)
            for c in range(NCH):
                lo, n = chunk(c)
                if c + 2 < NCH:
                    ln.turn(pe, c + 2)
                if c + 1 < NCH:
                    hidden(c + 1)
                pe.wait_ge(upd, 2 * (c + 1))
                if c >= 2:
                    pe.wait_ge(phd, c - 1)
                nc.tensor.matmul(m.ps[4 + c % 2][:, 0:n], w["w_pp"][:], T1[0:D, lo:lo + n],
                                 start=True, stop=True).then_inc(ph, 1)
            for c in range(NCH):
                lo, n = chunk(c)
                pe.wait_ge(trig, c + 1)
                if c == 0:
                    pe.wait_ge(abd, NCH)
                if c >= 2:
                    pe.wait_ge(tnd, c - 1)
                for j in range(n // P):
                    last = nc.tensor.transpose(m.ps[6 + c % 2][:, j * P:(j + 1) * P],
                                               Q[:, lo + j * P:lo + (j + 1) * P], m.ident[:])
                last.then_inc(tn, 1)

        @block.sync
        def _(sp):
            load_windows(nc, m, sp, ins, dr, landed)
            for to, what in late:
                sp.dma_start(to, what).then_inc(loads, 16)
            for chunks, tiles in HALVES:
                sp.wait_ge(abd, chunks)
                sp.dma_start(rows_of(dr["tab0"], (2 * D, 3 * D))[:, tiles, :], ab3[:, tiles, 0:D]).then_inc(ab_out, 16)
                sp.dma_start(rows_of(dr["tgt0"], (0, D))[:, tiles, :], ab3[:, tiles, D:P]).then_inc(ab_out, 16)
            for chunks, tiles in HALVES:
                sp.wait_ge(tnd, chunks)
                sp.dma_start(rows_of(dr["tab0"], (0, 2 * D))[:, tiles, :], qn3[:, tiles, :]).then_inc(out, 16)
            sp.wait_ge(ab_out, 64)
            sp.wait_ge(out, 32)
            sp.wait_ge(loads, 16 * len(late))
    st.close()


def layer0_edges(nc, m, w, ins, dr, rounds):
    RW = 3 * D
    rows, trow, ot, win, relu, oh1 = m.carve(m.D, [(P, U * J, RW), (WIN, 2, GE), (WIN, 2, GE), (WIN, 2, D),
                                                   (P, J, D), (P, J * WIN)])
    trow = trow.bitcast(I32)
    oh1 = oh1.bitcast(BF16).rearrange("p (b j w) -> p b j w", b=2, j=J)
    degs = m.A[0:4, :]

    def one_round(st, next_windows):
        gathered = st.keep(m.gathered)
        trow_in = [st.sem(f"targets_in{b}") for b in range(2)]
        win_in = [st.sem(f"window_in{b}") for b in range(2)]
        idx_set, dve, turns, near = st.sem("ids_set"), st.sem("relu"), st.sem("gather_turns"), st.sem("near")
        ot_set, z_set, zs_set, k_set, ok_set, seg, added = (
            Ring(st, n) for n in ("expander", "gate_psum", "gate_sum", "gate", "onehot", "segments", "added"))

        with nc.Block() as block:
            @block.sync
            def _(sp):
                with sp.Fori(0, TURNS) as i:
                    for u in range(U):
                        g, b = i * U + u, u % 2
                        ot_set.done(sp, g, 2)
                        sp.dma_start(trow[:, b, :], bc(ins["dst_rows"][ds(g, 1), :], [WIN, GE])).then_inc(trow_in[b], 16)
                        z_set.done(sp, g, 2)
                        base = window_base(nc, m, sp, g)
                        sp.dma_start(win[:, b, :], dr["tgt0"][ds(base, WIN), :]).then_inc(win_in[b], 16)

            @block.gpsimd
            def _(pool):
                gather_program(nc, m, pool, rows, dr["tab0"], idx_set, seg, gathered, turns)

            @block.scalar
            def _(act):
                k_set.start(act)
                first_ids(nc, m, act, idx_set)

                def share(at):
                    if g := at(1):
                        zs_set.done(act, g.g)
                        k_set.inc(nc.scalar.activation(m.kgate[:, g.b, :], m.zsum[:, g.b, :], ACT.Sigmoid,
                                                       bias=w["cb2"][:]))
                        next_ids(nc, m, act, g, gathered, idx_set)

                slots(act, share)

            @block.tensor
            def _(pe):
                z_set.start(pe)
                seg.start(pe)

                def share(at):
                    if g := at(1):
                        z = m.ps[g.b]
                        ot_set.done(pe, g.g)
                        g.landed(pe, win_in)
                        zs_set.done(pe, g.g, 2)
                        for j in range(J):
                            last = nc.tensor.matmul(z[:, j * D:(j + 1) * D], ot[:, g.b, j * P:(j + 1) * P],
                                                    win[:, g.b, :], start=True, stop=True)
                        z_set.inc(last)
                    if g := at(2):
                        ok_set.done(pe, g.g)
                        added.done(pe, g.g, 2)
                        g.gathered(pe, gathered)
                        for j in range(J):
                            nc.tensor.matmul(m.ps[4 + g.b][0:4, 0:WIN], m.dw[:, g.tiles(j, 1), :].rearrange("p a k -> p (a k)"),
                                             oh1[:, g.b, j, :], start=(j == 0), stop=(j == J - 1))
                        for j in range(J):
                            last = nc.tensor.matmul(m.ps[2 + g.b][:, 0:WIN], rows[:, g.u * J + j, 0:2 * D],
                                                    m.onehot[:, g.b, j, :], start=(j == 0), stop=(j == J - 1))
                        seg.inc(last)

                slots(pe, share)

            @block.vector
            def _(v):
                for r in (ot_set, zs_set, ok_set, added):
                    r.start(v)

                def share(at):
                    if g := at(0):
                        g.landed(v, trow_in)
                        z_set.done(v, g.g, 2)
                        ot_set.inc(nc.vector.tensor_scalar(ot[:, g.b, :], trow[:, g.b, :], m.nodeid[:, ds(g.g, 1)],
                                                           None, ALU.is_equal))
                    if g := at(2):
                        k_set.done(v, g.g)
                        seg.done(v, g.g, 2)
                        near_columns(nc, m, v, g, ok_set, near, m.dstrel[:].rearrange("p g j -> p (g j)"))
                        nc.vector.tensor_tensor(oh1[:, g.b], bc(m.iota[:, 0:WIN].unsqueeze(1), [P, J, WIN]),
                                                bc(m.near[:, 0, g.u * J:(g.u + 1) * J].unsqueeze(2), [P, J, WIN]),
                                                ALU.is_equal)
                        for j in range(J):
                            at_j = g.u * J + j
                            last = nc.vector.tensor_scalar(m.onehot[:, g.b, j, :], m.iota[:, 0:WIN],
                                                           m.near[:, 0, at_j:at_j + 1], m.kgate[:, g.b, j:j + 1],
                                                           ALU.is_equal, ALU.mult)
                        ok_set.inc(last)
                    if g := at(3):
                        base = window_base(nc, m, v, g.g)
                        seg.done(v, g.g)
                        added.done(v, g.g, 1)
                        nc.vector.tensor_tensor(degs[:, ds(base, WIN)], degs[:, ds(base, WIN)],
                                                m.ps[4 + g.b][0:4, 0:WIN], ALU.add)
                        added.inc(nc.vector.tensor_tensor(m.E[:, ds(base, WIN)], m.E[:, ds(base, WIN)],
                                                          m.ps[2 + g.b][:, 0:WIN], ALU.add))
                    if g := at(1):
                        z_set.done(v, g.g)
                        g.gathered(v, gathered)
                        zs_set.done(v, g.g, 1)
                        nc.vector.tensor_tensor(relu, m.ps[g.b][:, 0:J * D].rearrange("p (j f) -> p j f", f=D),
                                                rows[:, g.u * J:(g.u + 1) * J, 2 * D:3 * D], ALU.add).then_inc(dve, 1)
                        v.wait_ge(dve, 2 * g.g + 1)
                        nc.vector.scalar_tensor_tensor(
                            out=relu, in0=relu, scalar=0.0, in1=bc(w["row_cw2"][:].unsqueeze(1), [P, J, D]),
                            op0=ALU.max, op1=ALU.mult).then_inc(dve, 1)
                        v.wait_ge(dve, 2 * g.g + 2)
                        zs_set.inc(nc.vector.tensor_reduce(out=m.zsum[:, g.b, :], in_=relu, axis=AX, op=ALU.add))

                slots(v, share)
                next_windows(v)

    edge_rounds(nc, m, rounds, "l0e", one_round)


class Roots:

    def __init__(self, nc, m, st, dr, parts):
        self.nc, self.m, self.dr, self.parts = nc, m, dr, parts
        self.moved, self.chain, self.degree, self.root, self.inverse = (
            st.sem("deg_" + n) for n in ("moved", "dve", "degree", "root", "inverse"))
        self.d = m.onehot[0:NT].rearrange("t b j w -> t (b j w)").rearrange("t (k p) -> t k p", k=4)
        self.values = self.d[:, 2:4, :] if parts else m.hist[0:NT, :]
        self.rows = self.dr["roots"][0:2, :] if parts else self.dr["roots"][2:3, :]

    def sync_in(self, sp):
        sp.dma_start(self.dr["degs"], self.m.A[0:4, 0:NP]).then_inc(self.moved, 16)
        sp.wait_ge(self.moved, 16)
        sp.dma_start(self.d, self.dr["degs"].rearrange("k (t p) -> t k p", p=P)).then_inc(self.moved, 16)

    def vector(self, v):
        nc, step = self.nc, Chain(v, self.chain)
        if self.parts:
            v.wait_ge(self.moved, 32)
            d = self.d
            step(nc.vector.tensor_tensor(d[:, 0, :], d[:, 0, :], d[:, 1, :], ALU.add))
            step(nc.vector.tensor_tensor(d[:, 2, :], d[:, 0, :], d[:, 2, :], ALU.add))
            step(nc.vector.tensor_scalar(d[:, 2, :], d[:, 2, :], 1.0, None, ALU.add))
            nc.vector.tensor_scalar(d[:, 3, :], d[:, 3, :], 1.0, None, ALU.max).then_inc(self.degree, 1)
        else:
            nc.vector.tensor_scalar(self.values, self.values, 1.0, None, ALU.max).then_inc(self.degree, 1)
        v.wait_ge(self.root, 1)
        nc.vector.reciprocal(self.values, self.values).then_inc(self.inverse, 1)

    def scalar(self, act):
        act.wait_ge(self.degree, 1)
        self.nc.scalar.activation(self.values, self.values, ACT.Sqrt).then_inc(self.root, 1)

    def sync_out(self, sp):
        sp.wait_ge(self.inverse, 1)
        so_far = 32 if self.parts else 0
        to = self.rows.rearrange("k (t p) -> t k p", p=P)
        sp.dma_start(to, self.values if self.parts else self.values.unsqueeze(1)).then_inc(self.moved, 16)
        sp.wait_ge(self.moved, so_far + 16)


def layer0_out(nc, m, w, dr):
    st = Stage(nc, "l0o")
    mul, fr, frd, o1, o1d, o2, o2d, dve = (
        st.sem(n) for n in ("mul", "freqs", "joined", "o1", "o1_read", "o2", "o2_read", "dve"))
    O1 = m.D
    roots = Roots(nc, m, st, dr, parts=True)
    with nc.Block() as block:
        @block.sync
        def _(sp):
            roots.sync_in(sp)
            roots.sync_out(sp)

        @block.vector
        def _(v):
            def joined(c):
                lo, n = chunk(c)
                nc.vector.tensor_tensor(m.E[:, lo:lo + n], m.E[:, lo:lo + n], m.C[:, lo:lo + n], ALU.mult).then_inc(mul, 1)
                v.wait_ge(mul, c + 1)
                v.wait_ge(fr, c + 1)
                nc.vector.scalar_tensor_tensor(
                    out=m.E[D:P, lo:lo + n], in0=m.ps[c % 2][D:P, 0:n], scalar=w["fb2"][D:P, :], in1=m.E[D:P, lo:lo + n],
                    op0=ALU.add, op1=ALU.add).then_inc(frd, 1)

            step = Chain(v, dve)
            step(nc.vector.tensor_tensor(m.x[:], m.x[:], bc(w["row_ob2"][:].unsqueeze(1), [P, NT, D]), ALU.add))
            for c in range(NCH + 2):
                if c < NCH:
                    joined(c)
                if c >= 2:
                    lo, n = chunk(c - 2)
                    t, k = lo // P, n // P
                    v.wait_ge(o2, c - 1)
                    nc.vector.tensor_tensor(m.x[:, t:t + k, :], m.x[:, t:t + k, :], m.ps[4 + c % 2][:, 0:k * D].rearrange(
                        "p (t f) -> p t f", f=D), ALU.add).then_inc(o2d, 1)
                if c == NCH // 2:
                    roots.vector(v)

        @block.scalar
        def _(act):
            for c in range(NCH):
                lo, n = chunk(c)
                act.wait_ge(o1, c + 1)
                nc.scalar.activation(O1[0:D, lo:lo + n], m.ps[2 + c % 2][0:D, 0:n], ACT.Relu,
                                     bias=w["ob1"][:]).then_inc(o1d, 1)
                if c == NCH // 2 - 2:
                    roots.scalar(act)

        @block.tensor
        def _(pe):
            def freqs(c):
                lo, n = chunk(c)
                if c >= 2:
                    pe.wait_ge(frd, c - 1)
                nc.tensor.matmul(m.ps[c % 2][D:P, 0:n], w["fw2"][D:P, :], m.B[D:P, lo:lo + n],
                                 start=True, stop=True).then_inc(fr, 1)

            def hidden(c):
                lo, n = chunk(c)
                pe.wait_ge(frd, c + 1)
                if c >= 2:
                    pe.wait_ge(o1d, c - 1)
                nc.tensor.matmul(m.ps[2 + c % 2][0:D, 0:n], w["ow1s"][:], m.E[:, lo:lo + n],
                                 start=True, stop=True).then_inc(o1, 1)

            freqs(0)
            freqs(1)
            hidden(0)
            for c in range(NCH):
                lo, n = chunk(c)
                if c + 2 < NCH:
                    freqs(c + 2)
                if c + 1 < NCH:
                    hidden(c + 1)
                pe.wait_ge(o1d, c + 1)
                if c >= 2:
                    pe.wait_ge(o2d, c - 1)
                for j in range(n // P):
                    last = nc.tensor.matmul(m.ps[4 + c % 2][:, j * D:(j + 1) * D], O1[0:D, lo + j * P:lo + (j + 1) * P],
                                            w["ow2"][:], start=True, stop=True)
                last.then_inc(o2, 1)
    st.close()




def layer1_nodes(nc, m, w, ins, dr):
    st = Stage(nc, "l1n")
    ln = Nodes(nc, m, st, m.D)
    tb, tbd, out, dve, landed, zeroed = (st.sem(n) for n in ("tab", "tab_read", "out", "dve", "landed", "zeroed"))
    tab = m.DBF[:, 0:NT * 2 * HM].rearrange("p (t f) -> p t f", f=2 * HM)
    per = 3
    cuts = [(t, min(per, NT - t)) for t in range(0, NT, per)]
    hi, lo, digit = digit_columns(m)
    stores = [(0, 8), (8, len(cuts))]
    with nc.Block() as block:
        @block.vector
        def _(v):
            step = Chain(v, dve)
            ln.vector(v)
            source_digits(nc, m, step, NG * J, hi, lo, digit)
            for c, (t, k) in enumerate(cuts):
                v.wait_ge(tb, c + 1)
                nc.vector.tensor_tensor(tab[:, t:t + k, :], m.ps[2 + c % 2][:, 0:k * 2 * HM].rearrange(
                    "p (t f) -> p t f", f=2 * HM), bc(w["row_m1"][:].unsqueeze(1), [P, k, 2 * HM]), ALU.add).then_inc(tbd, 1)
            finish_windows(nc, m, v, step, landed)

        @block.gpsimd
        def _(pool):
            nc.gpsimd.memset(m.E, 0.0).then_inc(zeroed, 1)
            pool.wait_ge(zeroed, 1)

        @block.scalar
        def _(act):
            ln.scalar(act)

        @block.tensor
        def _(pe):
            ln.tensor(pe)
            pe.wait_ge(ln.stored, NCH)
            for c, (t, k) in enumerate(cuts):
                if c >= 2:
                    pe.wait_ge(tbd, c - 1)
                for j in range(k):
                    last = nc.tensor.matmul(m.ps[2 + c % 2][:, j * 2 * HM:(j + 1) * 2 * HM],
                                            m.A[0:D, (t + j) * P:(t + j + 1) * P], w["w_m1"][:], start=True, stop=True)
                last.then_inc(tb, 1)

        @block.sync
        def _(sp):
            load_windows(nc, m, sp, ins, dr, landed)
            for first, last in stores:
                sp.wait_ge(tbd, last)
                tiles = slice(first * per, min(last * per, NT))
                sp.dma_start(rows_of(dr["tab1"], (0, HM))[:, tiles, :], tab[:, tiles, 0:HM]).then_inc(out, 16)
                sp.dma_start(rows_of(dr["tgt1"], (0, HM))[:, tiles, :], tab[:, tiles, HM:2 * HM]).then_inc(out, 16)
            sp.wait_ge(ln.stored, NCH)
            sp.wait_ge(zeroed, 1)
            sp.dma_start(m.E[D:P, 0:NP], m.A[0:D, 0:NP]).then_inc(out, 16)
            sp.wait_ge(out, 80)
    st.close()


def digit_columns(m):
    n = NG * J
    return m.C[:, 0:n], m.C[:, n:2 * n], m.C[:, 2 * n:3 * n].bitcast(I32)


def source_digits(nc, m, step, n, hi, lo, digit):
    step(nc.vector.tensor_single_scalar(digit, m.src[:, 0:n], P.bit_length() - 1, op=ALU.arith_shift_right))
    step(nc.vector.tensor_copy(hi, digit))
    step(nc.vector.tensor_single_scalar(digit, m.src[:, 0:n], P - 1, op=ALU.bitwise_and))
    step(nc.vector.tensor_copy(lo, digit))


def layer1_edges(nc, m, w, ins, dr, rounds):
    K = WIN + DE
    rows, trow, left, right, m1, msg = m.carve(m.D, [
        (P, U * J, HM), (WIN, 2, GE), (K, 2, HM), (K, 2, GE), (HC, 2, GE), (P, 2, J, D)])
    trow = trow.bitcast(I32)
    hi, lo, _digit = digit_columns(m)

    st = Stage(nc, "l1s")
    dve = st.sem("dve")
    with nc.Block() as block:
        @block.vector
        def _(v):
            step = Chain(v, dve)
            step(nc.vector.memset(m1, 1.0))
            for b in range(2):
                step(nc.vector.tensor_copy(left[WIN:K, b, :], w["w_e"][WIN:K, :]))
    st.close()

    def one_round(st, next_windows):
        gathered = st.keep(m.gathered)
        trow_in = [st.sem(f"targets_in{b}") for b in range(2)]
        win_in = [st.sem(f"window_in{b}") for b in range(2)]
        ea_in = [st.sem(f"edge_features_in{b}") for b in range(2)]
        idx_set, turns, zeroed = st.sem("ids_set"), st.sem("gather_turns"), st.sem("count_zeroed")
        ot_set, pre, g1, msgp, g2, oh, seg, added = (
            Ring(st, n) for n in ("expander", "pre", "gelu1", "msg_psum", "gelu2", "onehot", "segments", "added"))

        with nc.Block() as block:
            @block.sync
            def _(sp):
                with sp.Fori(0, TURNS) as i:
                    for u in range(U):
                        g, b = i * U + u, u % 2
                        ot_set.done(sp, g, 2)
                        sp.dma_start(trow[:, b, :], bc(ins["dst_rows"][ds(g, 1), :], [WIN, GE])).then_inc(trow_in[b], 16)
                        pre.done(sp, g, 2)
                        base = window_base(nc, m, sp, g)
                        sp.dma_start(left[0:WIN, b, :], dr["tgt1"][ds(base, WIN), :]).then_inc(win_in[b], 16)
                        sp.dma_start(right[WIN:K, b, :], ins["ea_T"][:, ds(i * (U * GE) + u * GE, GE)]).then_inc(ea_in[b], 16)

            @block.gpsimd
            def _(pool):
                gather_program(nc, m, pool, rows, dr["tab1"], idx_set, pre, gathered, turns)

            @block.scalar
            def _(act):
                g1.start(act)
                g2.start(act)
                first_ids(nc, m, act, idx_set)

                def share(at):
                    if g := at(2):
                        msgp.done(act, g.g)
                        seg.done(act, g.g, 2)
                        g2.inc(nc.scalar.activation(msg[:, g.b, :, :], m.ps[2 + g.b][:, 0:J * D].rearrange(
                            "p (j f) -> p j f", f=D), ACT.Gelu))
                    if g := at(1):
                        next_ids(nc, m, act, g, gathered, idx_set)
                        pre.done(act, g.g)
                        msgp.done(act, g.g, 2)
                        g1.inc(nc.scalar.activation(m1[0:HM, g.b, :], m.ps[g.b][0:HM, :], ACT.Gelu))

                slots(act, share)

            @block.tensor
            def _(pe):
                for r in (pre, msgp, seg):
                    r.start(pe)

                def share(at):
                    if g := at(3):
                        oh.done(pe, g.g)
                        g2.done(pe, g.g)
                        added.done(pe, g.g, 2)
                        for j in range(J):
                            nc.tensor.matmul(m.ps[6 + g.b][0:WIN, 0:P], m.hi1[:, g.b, j, :], m.lo1[:, g.b, j, :],
                                             start=(j == 0), stop=(j == J - 1))
                        for j in range(J):
                            last = nc.tensor.matmul(m.ps[4 + g.b][0:D, 0:WIN], msg[:, g.b, j, :],
                                                    m.onehot[:, g.b, j, :], start=(j == 0), stop=(j == J - 1))
                        seg.inc(last)
                    if g := at(2):
                        g1.done(pe, g.g)
                        g2.done(pe, g.g, 2)
                        for j in range(J):
                            last = nc.tensor.matmul(m.ps[2 + g.b][:, j * D:(j + 1) * D],
                                                    m1[:, g.b, j * P:(j + 1) * P], w["w_m2"][:], start=True, stop=True)
                        msgp.inc(last)
                    if g := at(1):
                        z = m.ps[g.b][0:HM, :]
                        g1.done(pe, g.g, 2)
                        g.landed(pe, ea_in)
                        g.landed(pe, win_in)
                        ot_set.done(pe, g.g)
                        nc.tensor.matmul(z, left[:, g.b, :], right[:, g.b, :], start=True, stop=False)
                        g.gathered(pe, gathered)
                        for j in range(J):
                            last = nc.tensor.matmul(z[:, j * P:(j + 1) * P], rows[:, g.u * J + j, :], m.ident[:],
                                                    start=False, stop=(j == J - 1))
                        pre.inc(last)

                slots(pe, share)

            @block.vector
            def _(v):
                nc.vector.memset(m.hist, 0.0).then_inc(zeroed, 1)
                for r in (ot_set, oh, added):
                    r.start(v)
                v.wait_ge(zeroed, 1)

                def share(at):
                    if g := at(0):
                        g.landed(v, trow_in)
                        pre.done(v, g.g, 2)
                        ot_set.inc(nc.vector.tensor_scalar(right[0:WIN, g.b, :], trow[:, g.b, :],
                                                           m.nodeid[:, ds(g.g, 1)], None, ALU.is_equal))
                    if g := at(2):
                        seg.done(v, g.g, 2)
                        plain_onehot(nc, m, v, m.onehot[:, g.b], g)
                        nc.vector.tensor_tensor(m.hi1[:, g.b], bc(m.iota[:, 0:WIN].unsqueeze(1), [P, J, WIN]),
                                                bc(hi[:, g.tiles()].unsqueeze(2), [P, J, WIN]), ALU.is_equal)
                        oh.inc(nc.vector.tensor_tensor(m.lo1[:, g.b], bc(m.iota[:, 0:P].unsqueeze(1), [P, J, P]),
                                                       bc(lo[:, g.tiles()].unsqueeze(2), [P, J, P]), ALU.is_equal))
                    if g := at(4):
                        base = window_base(nc, m, v, g.g)
                        seg.done(v, g.g)
                        added.done(v, g.g, 1)
                        nc.vector.tensor_tensor(m.hist, m.hist, m.ps[6 + g.b][0:WIN, 0:P], ALU.add)
                        added.inc(nc.vector.tensor_tensor(m.E[0:D, ds(base, WIN)], m.E[0:D, ds(base, WIN)],
                                                          m.ps[4 + g.b][0:D, 0:WIN], ALU.add))

                slots(v, share)
                next_windows(v)

    edge_rounds(nc, m, rounds, "l1e", one_round)


def layer1_out(nc, m, w, dr):
    st = Stage(nc, "l1o")
    c1, c1d, c2, c2d, g, dve = (st.sem(n) for n in ("c1", "c1_read", "c2", "c2_read", "gelu", "dve"))
    comb = m.D[:, 0:NT * D].rearrange("p (t f) -> p t f", f=D)
    roots, ahead = Roots(nc, m, st, dr, parts=False), st.sem("ahead")
    with nc.Block() as block:
        @block.sync
        def _(sp):
            sp.dma_start(m.B[0:D, 0:NP], bc(dr["roots"][0:1, :], [D, NP])).then_inc(ahead, 16)
            roots.sync_out(sp)
            sp.wait_ge(ahead, 16)

        @block.vector
        def _(v):
            step = Chain(v, dve)
            roots.vector(v)
            step(nc.vector.tensor_tensor(m.x[:], m.x[:], m.H, ALU.add))
            for c in range(NCH):
                lo, n = chunk(c)
                t, k = lo // P, n // P
                v.wait_ge(c2, c + 1)
                nc.vector.tensor_tensor(comb[:, t:t + k, :], m.ps[2 + c % 2][:, 0:k * D].rearrange("p (t f) -> p t f", f=D),
                                        bc(w["row_bc2"][:].unsqueeze(1), [P, k, D]), ALU.add).then_inc(c2d, 1)
            v.wait_ge(g, 1)
            step(nc.vector.tensor_tensor(m.x[:], m.x[:], comb, ALU.add))

        @block.scalar
        def _(act):
            roots.scalar(act)
            for c in range(NCH):
                lo, n = chunk(c)
                act.wait_ge(c1, c + 1)
                nc.scalar.activation(m.C[0:HC, lo:lo + n], m.ps[c % 2][0:HC, 0:n], ACT.Gelu,
                                     bias=w["b_c1"][:]).then_inc(c1d, 1)
            act.wait_ge(c2d, NCH)
            nc.scalar.activation(comb, comb, ACT.Gelu).then_inc(g, 1)

        @block.tensor
        def _(pe):
            def first(c):
                lo, n = chunk(c)
                if c >= 2:
                    pe.wait_ge(c1d, c - 1)
                nc.tensor.matmul(m.ps[c % 2][0:HC, 0:n], w["w_c1"][:], m.E[:, lo:lo + n],
                                 start=True, stop=True).then_inc(c1, 1)

            first(0)
            for c in range(NCH):
                lo, n = chunk(c)
                if c + 1 < NCH:
                    first(c + 1)
                pe.wait_ge(c1d, c + 1)
                if c >= 2:
                    pe.wait_ge(c2d, c - 1)
                for j in range(n // P):
                    last = nc.tensor.matmul(m.ps[2 + c % 2][:, j * D:(j + 1) * D], m.C[0:HC, lo + j * P:lo + (j + 1) * P],
                                            w["w_c2"][:], start=True, stop=True)
                last.then_inc(c2, 1)
    st.close()




class DenseQuarter:

    def __init__(self, plan, i, u, back):
        k = u - back
        self.plan, self.k = plan, k
        self.q = i * (2 * U) + k
        self.batch = i * 2 + k // U
        self.half, self.r = (k // U) % 2, k % U
        self.i = i

    def tile(self, j):
        return self.i * (2 * U * self.plan.dense) + (self.k * self.plan.dense + j)

    def mod(self, j, depth):
        return (self.k * self.plan.dense + j) % depth

    def last_of_batch(self):
        return self.tile(self.plan.dense * (U - self.r) - 1)


class SumBuffers:

    def __init__(self, m, plan):
        n, cols = plan.tiles, plan.batch * plan.win
        if plan.exact:
            self.inc, self.rows, self.mark, self.row1 = m.carve(m.AD, [
                (P, 2, NT, cols), (P, U * J, D), (P, plan.depth, plan.width), (P, plan.depth, P)])
            self.combo, self.hi, self.lo = m.carve(m.C[:, 3072:], [(P, n), (P, n), (P, n)])
            self.table = m.TAB
            self.iota = m.iota
        else:
            self.combo = m.F[:, NW - n:]
            self.table, self.inc, self.rows, mark = m.carve(m.DBF[:, 0:3 * NW - n], [
                (P, NT, 3 * D // 2), (P, NT, cols), (P, U * J, D), (P, plan.width * plan.dense)])
            self.table = self.table.bitcast(BF16)
            self.inc = self.inc.bitcast(BF16).rearrange("p t (b c) -> p b t c", b=2)
            self.mark = mark.bitcast(BF16).rearrange("p (b c) -> p b c", b=plan.depth)
            self.row1 = m.marks[:, 0:plan.depth * P].rearrange("p (b c) -> p b c", b=plan.depth)
            self.lo = m.ew[:, 0:n]
            self.hi = m.ew[:, n:n + n // 2].bitcast(F16)
            self.iota = m.iota16
        self.scratch = self.combo
        self.far = m.C if plan.exact else m.E
        self.tmp = self.far[:, 2048:2048 + n]
        self.rel = m.dstrel[:].rearrange("p g j -> p (g j)")


def tile_combinations(nc, m, plan, buf, step, tmp):
    rel = buf.rel[:, 0:plan.tiles]
    step(nc.vector.tensor_scalar(tmp, rel, 0.0, None, ALU.is_ge))
    step(nc.vector.scalar_tensor_tensor(out=tmp, in0=rel, scalar=float(plan.win), in1=tmp, op0=ALU.is_lt, op1=ALU.mult))
    step(nc.vector.scalar_tensor_tensor(out=buf.combo, in0=rel, scalar=1.0, in1=buf.hi, op0=ALU.add, op1=ALU.add))
    step(nc.vector.tensor_tensor(buf.combo, buf.combo, tmp, ALU.mult))
    step(nc.vector.tensor_scalar(buf.combo, buf.combo, -1.0, None, ALU.add))


class SumWindows:

    def __init__(self, nc, m, st, ins, dr, plan):
        self.nc, self.m, self.ins, self.dr, self.plan = nc, m, ins, dr, plan
        self.landed = st.sem("windows_landed")
        self.buf = SumBuffers(m, plan)
        self.group_base, self.tile_base = self.buf.far[:, 0:NG], self.buf.far[:, 1024:1024 + plan.tiles]

    def sync(self, sp):
        m, dr, n = self.m, self.dr, self.plan.tiles
        for to, what in ((m.dstrel[:].bitcast(I32), self.ins["dst_t"].rearrange("p (g j) -> p g j", j=J)),
                         (self.group_base, bc(dr["base_f"], [P, NG])), (m.base_i[:], dr["base_i"]),
                         (self.tile_base, bc(dr["tbase_f"][:, 0:n], [P, n])), (m.tile_i[:, 0:n], dr["tbase_i"][:, 0:n])):
            sp.dma_start(to, what).then_inc(self.landed, 16)

    def vector(self, v, step):
        nc, m, buf, plan, n = self.nc, self.m, self.buf, self.plan, self.plan.tiles
        source_digits(nc, m, step, n, buf.hi, buf.lo, buf.scratch.bitcast(I32))
        step(nc.vector.tensor_scalar(buf.hi, buf.hi, float(plan.win), None, ALU.mult))
        v.wait_ge(self.landed, 80)
        step(nc.vector.tensor_copy(m.dstrel[:], m.dstrel[:].bitcast(I32)))
        late = m.dstrel[:, plan.first:NG, :]
        step(nc.vector.tensor_tensor(late, late, bc(self.group_base[:, plan.first:NG].unsqueeze(2),
                                                    [P, NG - plan.first, J]), ALU.subtract))
        step(nc.vector.tensor_tensor(buf.rel[:, 0:n], buf.rel[:, 0:n], self.tile_base, ALU.subtract))
        tile_combinations(nc, m, plan, buf, step, buf.tmp)


def sum_sources(nc, m, dr, rounds, name, plan):
    buf = SumBuffers(m, plan)
    weighted, win, dense, width = plan.exact, plan.win, plan.dense, plan.width
    out_rows = D if plan.exact else P

    def one_round(st, next_windows):
        gathered = st.keep(m.gathered)
        idx_set, turns, near, near_tiles = (st.sem(n) for n in ("ids_set", "gather_turns", "near", "near_tiles"))
        inc_banks = [m.ps[k] for k in (0, 1, 6, 7)]
        oh, seg, added, marks, made, kept, product, summed = (Ring(st, n) for n in (
            "onehot", "segments", "added", "marks", "incidence_psum", "incidence", "product", "summed"))

        def items(at):
            return (lambda k: at(k, lambda i, u, back: Group(i, u, back, 2 * U, plan.first), plan.groups),
                    lambda k: at(k, lambda i, u, back: DenseQuarter(plan, i, u, back), plan.quarters))

        def run(eng, share):
            slots(eng, lambda at: share(*items(at)), 2 * U, min(plan.groups, plan.quarters) // (2 * U) * (2 * U),
                  max(plan.groups, plan.quarters) - min(plan.groups, plan.quarters) // (2 * U) * (2 * U) + 2 * U)

        with nc.Block() as block:
            @block.gpsimd
            def _(pool):
                gather_program(nc, m, pool, buf.rows, dr["tab2"], idx_set, seg, gathered, turns, plan.groups)

            @block.scalar
            def _(act):
                kept.start(act)
                first_ids(nc, m, act, idx_set, plan.first)

                def share(gather, tiles):
                    if g := gather(1):
                        next_ids(nc, m, act, g, gathered, idx_set)
                    if d := tiles(0):
                        for j in range(dense):
                            n, k = d.tile(j), d.r * dense + j
                            if k == 0:
                                product.done(act, d.batch, 2)
                            made.done(act, n)
                            kept.inc(nc.scalar.copy(
                                buf.inc[:, d.half, :, k * win:(k + 1) * win],
                                inc_banks[d.mod(j, 4)][:, 0:width].rearrange("p (t c) -> p t c", c=win)))

                run(act, share)

            @block.tensor
            def _(pe):
                for r in (seg, made, product):
                    r.start(pe)

                def share(gather, tiles):
                    new, old = tiles(0), tiles(U)
                    for j in range(dense):
                        if new:
                            n, b = new.tile(j), new.mod(j, plan.depth)
                            marks.done(pe, n)
                            kept.done(pe, n, 4)
                            made.inc(nc.tensor.matmul(inc_banks[new.mod(j, 4)][:, 0:width], buf.row1[:, b, :], buf.mark[:, b, :],
                                                      start=True, stop=True))
                        if old:
                            k = old.r * dense + j
                            out = m.ps[2 + old.half]
                            cols = plan.batch * win
                            if k == 0:
                                kept.done(pe, old.last_of_batch())
                                summed.done(pe, old.last_of_batch(), 2 * plan.batch)
                            for t in range(k * NT // plan.batch, (k + 1) * NT // plan.batch):
                                right = buf.inc[:, old.half, t, :]
                                if plan.exact:
                                    last = nc.tensor.matmul(out[0:D, 0:cols], buf.table[:, t, :], right,
                                                            start=(t == 0), stop=(t == NT - 1))
                                else:
                                    nc.tensor.matmul(out[:, 0:cols], buf.table[:, t, 0:2 * D], right,
                                                     start=(t == 0), stop=(t == NT - 1), skip_group_check=True)
                                    last = nc.tensor.matmul(out[0:D, 0:cols], buf.table[:, t, 2 * D:3 * D], right,
                                                            start=False, stop=(t == NT - 1), skip_group_check=True)
                            if k == plan.batch - 1:
                                product.inc(last)
                    if g := gather(1):
                        oh.done(pe, g.q)
                        added.done(pe, g.q, 2)
                        g.gathered(pe, gathered)
                        for j in range(J):
                            last = nc.tensor.matmul(m.ps[4 + g.b][0:D, 0:WIN], buf.rows[:, g.u * J + j, :],
                                                    m.onehot[:, g.b, j, :], start=(j == 0), stop=(j == J - 1))
                        seg.inc(last)

                run(pe, share)

            @block.vector
            def _(v):
                for r in (oh, added, marks, summed):
                    r.start(v)

                def share(gather, tiles):
                    new, old, last_group = tiles(0), tiles(2 * U), gather(2)
                    group_base = None
                    if new and new.r == 0:
                        marks.done(v, new.tile(0), 1)
                        for k, source in enumerate((buf.lo, buf.combo, m.ew)[:3 if weighted else 2]):
                            last = nc.vector.tensor_copy(m.near_tiles[:, k, 0:plan.batch],
                                                         source[:, ds(new.tile(0), plan.batch)])
                        last.then_inc(near_tiles, 1)
                        v.wait_ge(near_tiles, new.batch + 1)
                    for j in range(dense):
                        if new:
                            n, b, k = new.tile(j), new.mod(j, plan.depth), new.r * dense + j
                            lo, combo, weight = (m.near_tiles[:, a, k:k + 1] for a in range(3))
                            if plan.depth == dense:
                                made.done(v, n, dense)
                                nc.vector.tensor_scalar(buf.row1[:, b, :], buf.iota[:, 0:P], lo, None, ALU.is_equal)
                            elif j == 0:
                                made.done(v, new.tile(dense - 1), 2 * dense)
                                nc.vector.tensor_tensor(
                                    buf.row1[:, b:b + dense, :], bc(buf.iota[:, 0:P].unsqueeze(1), [P, dense, P]),
                                    bc(m.near_tiles[:, 0, k:k + dense].unsqueeze(2), [P, dense, P]), ALU.is_equal)
                            if weighted:
                                marks.inc(nc.vector.tensor_scalar(
                                    buf.mark[:, b, :], buf.iota[:, 0:width], combo, weight, ALU.is_equal, ALU.mult))
                            else:
                                marks.inc(nc.vector.tensor_scalar(
                                    buf.mark[:, b, :], buf.iota[:, 0:width], combo, None, ALU.is_equal))
                        if last_group and group_base is None:
                            group_base = window_base(nc, m, v, last_group.g)
                        if old:
                            n, k = old.tile(j), old.r * dense + j
                            if k == 0:
                                product.done(v, old.batch)
                            if j == 0:
                                bases = window_bases(nc, v, m.tile_i, n, dense)
                            base = bases[j]
                            summed.done(v, n, 1)
                            if j == 0 and (g := gather(3)):
                                added.done(v, g.q)
                            summed.inc(nc.vector.tensor_tensor(
                                m.E[0:out_rows, ds(base, win)], m.E[0:out_rows, ds(base, win)],
                                m.ps[2 + old.half][0:out_rows, k * win:(k + 1) * win], ALU.add))
                    if g := gather(0):
                        seg.done(v, g.q, 2)
                        if weighted:
                            near_columns(nc, m, v, g, oh, near, m.dstrel[:].rearrange("p g j -> p (g j)"), m.ew)
                            for j in range(J):
                                target, weight = (m.near[:, a, g.u * J + j:g.u * J + j + 1] for a in range(2))
                                last = nc.vector.tensor_scalar(m.onehot[:, g.b, j, :], m.iota[:, 0:WIN],
                                                               target, weight, ALU.is_equal, ALU.mult)
                        else:
                            last = plain_onehot(nc, m, v, m.onehot[:, g.b], g)
                        oh.inc(last)
                    if g := last_group:
                        seg.done(v, g.q)
                        added.done(v, g.q, 1)
                        if old:
                            summed.done(v, old.tile(dense - 1))
                        added.inc(nc.vector.tensor_tensor(m.E[0:D, ds(group_base, WIN)], m.E[0:D, ds(group_base, WIN)],
                                                          m.ps[4 + g.b][0:D, 0:WIN], ALU.add))

                run(v, share)
                next_windows(v)

    def shift(step):
        n = plan.tiles
        late = m.dstrel[:, plan.first:NG, :]
        step(nc.vector.tensor_scalar(late, late, float(-WIN), None, ALU.add))
        step(nc.vector.tensor_scalar(buf.rel[:, 0:n], buf.rel[:, 0:n], float(-plan.win), None, ALU.add))
        step(nc.vector.tensor_scalar(m.base_i[:], m.base_i[:], float(WIN), float(N), ALU.add, ALU.min))
        step(nc.vector.tensor_scalar(m.tile_i[:, 0:n], m.tile_i[:, 0:n], float(plan.win), float(N), ALU.add, ALU.min))
        rows = buf.rows.rearrange("p a b -> p (a b)")
        tile_combinations(nc, m, plan, buf, step, rows[:, 0:n])

    edge_rounds(nc, m, rounds, name, one_round, shift)


def turn_chunk(nc, m, pe, source, bank0, c, ready, turned, stored, reads=1):
    lo, n = chunk(c)
    if ready:
        pe.wait_ge(ready, c + 1)
    if c >= 2:
        pe.wait_ge(stored, reads * (c - 1))
    for j in range(n // P):
        last = nc.tensor.transpose(m.ps[bank0 + c % 2][:, j * D:(j + 1) * D],
                                   source[0:D, lo + j * P:lo + (j + 1) * P], m.ident[0:D, 0:D])
    last.then_inc(turned, 1)


def turn_to_nodes(nc, m, pe, source, bank0, turned, stored, reads=1):
    for c in range(NCH):
        turn_chunk(nc, m, pe, source, bank0, c, None, turned, stored, reads)




def layer2_in(nc, m, w, ins, dr, conv):
    st = Stage(nc, f"l2n{conv}")
    first = conv == 0
    ln = Nodes(nc, m, st, m.D) if first else None
    windows = SumWindows(nc, m, st, ins, dr, L2_PLAN)
    dve, us, zt, ztd, zn, znd, out = (
        st.sem(n) for n in ("dve", "u_set", "zt", "zt_read", "zn", "zn_read", "out"))
    dinv = m.B[0:D, 0:NP]
    U_ = m.A[0:D, 0:NP]
    W_ = w[f"w_g{conv}"]
    with nc.Block() as block:
        @block.vector
        def _(v):
            step = Chain(v, dve)
            if first:
                ln.vector(v)
            for c in range(NCH):
                lo, n = chunk(c)
                if first:
                    v.wait_ge(ln.stored, c + 1)
                nc.vector.tensor_tensor(U_[:, lo:lo + n], m.A[0:D, lo:lo + n], dinv[:, lo:lo + n],
                                        ALU.mult).then_inc(us, 1)
            step(nc.vector.memset(m.E[0:D, NP:NW], 0.0))
            windows.vector(v, step)

        @block.scalar
        def _(act):
            if first:
                ln.scalar(act)
            for c in range(NCH):
                lo, n = chunk(c)
                t, k = lo // P, n // P
                act.wait_ge(zt, c + 1)
                nc.scalar.copy(m.E[0:D, lo:lo + n], m.ps[2 + c % 2][0:D, 0:n]).then_inc(ztd, 1)
                act.wait_ge(zn, c + 1)
                nc.scalar.copy(m.TAB[:, t:t + k, :], m.ps[4 + c % 2][:, 0:k * D].rearrange(
                    "p (t f) -> p t f", f=D)).then_inc(znd, 1)

        @block.tensor
        def _(pe):
            def product(c):
                lo, n = chunk(c)
                pe.wait_ge(us, c + 1)
                if c >= 2:
                    pe.wait_ge(ztd, c - 1)
                nc.tensor.matmul(m.ps[2 + c % 2][0:D, 0:n], W_[:], U_[:, lo:lo + n], start=True, stop=True).then_inc(zt, 1)

            if first:
                ln.tensor(pe)
            product(0)
            for c in range(NCH):
                if c + 1 < NCH:
                    product(c + 1)
                turn_chunk(nc, m, pe, m.E, 4, c, ztd, zn, znd)

        @block.sync
        def _(sp):
            windows.sync(sp)
            for chunks, tiles in HALVES:
                sp.wait_ge(znd, chunks)
                sp.dma_start(rows_of(dr["tab2"], (0, D))[:, tiles, :], m.TAB[:, tiles, :]).then_inc(out, 16)
            sp.wait_ge(out, 32)
    st.close()


def layer2_out(nc, m, w, dr, conv):
    st = Stage(nc, f"l2o{conv}")
    dve, scaled, var, std, done, turned, stored, ahead = (
        st.sem(n) for n in ("dve", "scaled", "var", "std", "done", "turned", "stored", "ahead"))
    col = m.col
    Eo = m.E[0:D, 0:NP]
    sq = m.D[0:D, 0:NP]
    mean, v_, sd, scale = (col[0:D, k:k + 1] for k in range(4))
    parts = m.F[0:D, NW // 2:NW // 2 + N // 50]
    in_parts = lambda ap: ap[:, 0:N].rearrange("p (a b) -> p a b", b=50)
    b, gamma, beta = w[f"b_g{conv}"], w[f"gamma{conv}"], w[f"beta{conv}"]
    with nc.Block() as block:
        @block.vector
        def _(v):
            step = Chain(v, dve)
            nc.vector.tensor_tensor(Eo, Eo, m.B[0:D, 0:NP], ALU.mult).then_inc(scaled, 1)
            v.wait_ge(scaled, 1)
            step(nc.vector.tensor_scalar(Eo, Eo, b[:], None, ALU.add))
            step(nc.vector.tensor_reduce(out=parts, in_=in_parts(Eo), axis=AX, op=ALU.add))
            step(nc.vector.tensor_reduce(out=mean, in_=parts, axis=AX, op=ALU.add))
            step(nc.vector.tensor_scalar(mean, mean, 1.0 / N, None, ALU.mult))
            step(nc.vector.tensor_scalar(Eo, Eo, mean, None, ALU.subtract))
            step(nc.vector.tensor_tensor(sq, Eo, Eo, ALU.mult))
            step(nc.vector.tensor_reduce(out=parts, in_=in_parts(sq), axis=AX, op=ALU.add))
            step(nc.vector.tensor_reduce(out=v_, in_=parts, axis=AX, op=ALU.add))
            nc.vector.tensor_scalar(v_, v_, 1.0 / N, EPS, ALU.mult, ALU.add).then_inc(var, 1)
            v.wait_ge(std, 1)
            step(nc.vector.reciprocal(scale, sd))
            step(nc.vector.tensor_tensor(scale, scale, gamma[:], ALU.mult))
            step(nc.vector.tensor_scalar(m.A[0:D, 0:NP], Eo, scale, beta[:], ALU.mult, ALU.add))
            if conv == 0:
                step(nc.vector.tensor_scalar(m.A[0:D, 0:NP], m.A[0:D, 0:NP], 0.0, None, ALU.max))
            else:
                v.sem_inc(done, 1)
                for c in range(NCH):
                    lo, n = chunk(c)
                    t, k = lo // P, n // P
                    v.wait_ge(turned, c + 1)
                    nc.vector.tensor_tensor(m.H[:, t:t + k, :], m.H[:, t:t + k, :],
                                            m.ps[c % 2][:, 0:k * D].rearrange("p (t f) -> p t f", f=D),
                                            ALU.add).then_inc(stored, 1)
                v.wait_ge(stored, NCH)
                step(nc.vector.scalar_tensor_tensor(out=m.x[:], in0=m.H, scalar=0.0, in1=m.x[:],
                                                    op0=ALU.max, op1=ALU.add))

        @block.scalar
        def _(act):
            act.wait_ge(var, 1)
            nc.scalar.activation(sd, v_, ACT.Sqrt).then_inc(std, 1)

        @block.tensor
        def _(pe):
            if conv == 1:
                pe.wait_ge(done, 1)
                turn_to_nodes(nc, m, pe, m.A, 0, turned, stored)

        @block.sync
        def _(sp):
            if conv == 1:
                sp.dma_start(m.C[:, 0:NP], bc(dr["roots"][1:2, :], [P, NP])).then_inc(ahead, 16)
                sp.wait_ge(scaled, 1)
                sp.dma_start(m.B[0:D, 0:NP], bc(dr["roots"][2:3, :], [D, NP])).then_inc(ahead, 16)
                sp.wait_ge(ahead, 32)
    st.close()




def layer3_in(nc, m, w, ins, dr, conv):
    st = Stage(nc, f"l3n{conv}")
    first = conv == 0
    ln = Nodes(nc, m, st, m.D) if first else None
    windows = SumWindows(nc, m, st, ins, dr, L3_PLAN)
    dve, us, turned, stored, out, made, zeroed, left, third = (st.sem(n) for n in (
        "dve", "u_set", "turned", "stored", "out", "windows_made", "zeroed", "left", "third_part"))
    parts = [windows.buf.table[:, :, k * D:(k + 1) * D] for k in range(3)]
    U_, table, rest = m.B[0:D, 0:NP], m.H, m.B[:, 0:NT * D].rearrange("p (t f) -> p t f", f=D)
    with nc.Block() as block:
        @block.vector
        def _(v):
            step = Chain(v, dve)
            if first:
                ln.vector(v)
                v.wait_ge(ln.stored, NCH)
            nc.vector.tensor_tensor(U_, m.A[0:D, 0:NP], U_, ALU.mult).then_inc(us, 1)
            windows.vector(v, step)
            v.sem_inc(made, 1)
            v.wait_ge(stored, 2 * NCH)
            step(nc.vector.tensor_tensor(rest, table, parts[0], ALU.subtract))
            step(nc.vector.tensor_copy(parts[1], rest))
            nc.vector.tensor_tensor(rest, rest, parts[1], ALU.subtract).then_inc(left, 1)

        @block.gpsimd
        def _(pool):
            pool.wait_ge(made, 1)
            nc.gpsimd.memset(m.E, 0.0).then_inc(zeroed, 1)
            pool.wait_ge(zeroed, 1)

        @block.scalar
        def _(act):
            if first:
                ln.scalar(act)
            for c in range(NCH):
                lo, n = chunk(c)
                t, k = lo // P, n // P
                act.wait_ge(turned, c + 1)
                for to in (table, parts[0]):
                    nc.scalar.copy(to[:, t:t + k, :], m.ps[4 + c % 2][:, 0:k * D].rearrange(
                        "p (t f) -> p t f", f=D)).then_inc(stored, 1)
            act.wait_ge(left, 1)
            nc.scalar.copy(parts[2], rest).then_inc(third, 1)
            act.wait_ge(third, 1)

        @block.tensor
        def _(pe):
            if first:
                ln.tensor(pe)
            pe.wait_ge(us, 1)
            turn_to_nodes(nc, m, pe, m.B, 4, turned, stored, reads=2)

        @block.sync
        def _(sp):
            windows.sync(sp)
            if first:
                sp.wait_ge(ln.stored, NCH)
                sp.dma_start(m.A[D:P, 0:NP], m.A[0:D, 0:NP]).then_inc(out, 16)
            sp.wait_ge(stored, 2 * NCH)
            sp.dma_start(rows_of(dr["tab2"], (0, D)), table).then_inc(out, 16)
            sp.wait_ge(out, 32 if first else 16)
    st.close()


def layer3_out(nc, m, w, dr, conv, out_dram):
    st = Stage(nc, f"l3o{conv}")
    ready, pr, prd, out, fold, folded, ahead = (
        st.sem(n) for n in ("ready", "product", "product_read", "out", "fold", "folded", "ahead"))
    both = m.D
    w12 = w[f"w_n{conv}"]
    with nc.Block() as block:
        @block.vector
        def _(v):
            def left_and_right(c):
                lo, n = chunk(c)
                at = slice(lo, lo + n)
                v.wait_ge(fold, c + 1)
                nc.vector.tensor_tensor(m.E[:, at], m.ps[4 + c % 2][:, 0:n], m.C[:, at], ALU.mult).then_inc(folded, 1)
                v.wait_ge(folded, c + 1)
                nc.vector.tensor_tensor(both[0:D, at], m.E[0:D, at], m.A[0:D, at], ALU.add)
                nc.vector.tensor_tensor(both[D:P, at], m.E[D:P, at], m.A[D:P, at], ALU.mult).then_inc(ready, 1)

            def add_to_x(c):
                lo, n = chunk(c)
                t, k = lo // P, n // P
                v.wait_ge(pr, c + 1)
                nc.vector.tensor_tensor(m.x[:, t:t + k, :], m.x[:, t:t + k, :],
                                        m.ps[c % 2][:, 0:k * D].rearrange("p (t f) -> p t f", f=D),
                                        ALU.add).then_inc(prd, 1)

            left_and_right(0)
            for c in range(1, NCH + 1):
                if c < NCH:
                    left_and_right(c)
                if conv == 1:
                    add_to_x(c - 1)

        @block.scalar
        def _(act):
            if conv == 0:
                for c in range(NCH):
                    lo, n = chunk(c)
                    act.wait_ge(pr, c + 1)
                    nc.scalar.activation(m.A[:, lo:lo + n], m.ps[c % 2][:, 0:n], ACT.Relu).then_inc(prd, 1)

        @block.tensor
        def _(pe):
            def add_halves(c):
                lo, n = chunk(c)
                if c >= 2:
                    pe.wait_ge(folded, c - 1)
                nc.tensor.matmul(m.ps[4 + c % 2][:, 0:n], w["fold"][:], m.E[:, lo:lo + n],
                                 start=True, stop=True).then_inc(fold, 1)

            add_halves(0)
            add_halves(1)
            for c in range(NCH):
                lo, n = chunk(c)
                pe.wait_ge(ready, c + 1)
                if c >= 2:
                    pe.wait_ge(prd, c - 1)
                if conv == 0:
                    last = nc.tensor.matmul(m.ps[c % 2][:, 0:n], w12[:], both[:, lo:lo + n], start=True, stop=True)
                else:
                    for j in range(n // P):
                        last = nc.tensor.matmul(m.ps[c % 2][:, j * D:(j + 1) * D], both[:, lo + j * P:lo + (j + 1) * P],
                                                w12[:, 0:D], start=True, stop=True)
                last.then_inc(pr, 1)
                if c + 2 < NCH:
                    add_halves(c + 2)

        @block.sync
        def _(sp):
            if conv == 0:
                sp.dma_start(m.B[0:D, 0:NP], bc(dr["roots"][2:3, :], [D, NP])).then_inc(ahead, 16)
                sp.wait_ge(ahead, 16)
            else:
                sp.wait_ge(prd, NCH)
                store_x(m, sp, out_dram, out)
    st.close()


def store_x(m, sp, out_dram, out):
    full = N // P
    sp.dma_start(out_dram[0:full * P, :].rearrange("(t p) f -> p t f", p=P), m.x[:, 0:full, :]).then_inc(out, 16)
    sp.dma_start(out_dram[full * P:N, :], m.x[0:N - full * P, full, :]).then_inc(out, 16)
    sp.wait_ge(out, 32)




def gnn_kernel(nc, a, out):
    with ExitStack() as ctx:
        m = Memory(nc, ctx)
        m.gathered = [ctx.enter_context(nc.semaphore(f"gathered{u}")) for u in range(U)]
        m.rounds = ctx.enter_context(nc.sbuf_tensor("rounds", [1, 3], I32))
        m.hist = ctx.enter_context(nc.sbuf_tensor("source_counts", [WIN, P], F32))[:]
        m.dw = m.F[:, NW - 2 * NG * J:].bitcast(BF16).rearrange("p (t k) -> p t k", k=4)

        w, loads = {}, []

        def weight(name, shape, *parts):
            t = ctx.enter_context(nc.sbuf_tensor("w_" + name, shape, F32))
            w[name] = t
            for where, what in parts:
                loads.append((t[where], what))

        def col(ap):
            return ap.rearrange("(a b) -> a b", b=1)

        def row(ap, parts):
            return bc(ap.rearrange("(a b) -> a b", a=1), [parts, ap.shape[0]])

        s = slice
        al, top, bot = s(None), s(0, D), s(D, P)
        left, right = (al, s(0, D)), (al, s(D, P))
        weight("w_pf", [D, P], (left, a["L0_gnn_pw1"]), (right, a["L0_gnn_fw1"]))
        weight("w_pp", [D, P], (left, a["L0_gnn_pw2"]), (right, a["L0_gnn_pw2"]))
        weight("w_ba", [D, P], (left, a["L0_gnn_cw1"][D:2 * D, :]), (right, a["L0_gnn_cw1"][0:D, :]))
        weight("fw2", [P, D], ((bot, al), a["L0_gnn_fw2"]))
        weight("ow1s", [P, D], ((top, al), a["L0_gnn_ow1"]), ((bot, al), a["L0_gnn_ow1"]))
        weight("ow2", [D, D], ((al, al), a["L0_gnn_ow2"]))
        weight("b_pf", [P, 1], ((top, al), col(a["L0_gnn_pb1"])), ((bot, al), col(a["L0_gnn_fb1"])))
        weight("b_ph", [P, 1], ((top, al), col(a["L0_gnn_pb2"])), ((bot, al), col(a["L0_gnn_pb2"])))
        weight("row_ab", [P, P], (right, row(a["L0_gnn_cb1"], P)))
        weight("fb2", [P, 1], ((bot, al), col(a["L0_gnn_fb2"])))
        weight("ob1", [D, 1], ((al, al), col(a["L0_gnn_ob1"])))
        weight("row_ob2", [P, D], ((al, al), row(a["L0_gnn_ob2"], P)))
        weight("row_cw2", [P, D], ((al, al), bc(a["L0_gnn_cw2"].rearrange("a b -> b a"), [P, D])))
        weight("cb2", [P, 1], ((al, al), row(a["L0_gnn_cb2"], P)))
        early = len(loads)
        weight("w_m1", [D, 2 * HM], ((al, s(0, HM)), a["L1_gnn_W_m1"][0:D, :]),
               ((al, s(HM, 2 * HM)), a["L1_gnn_W_m1"][D:2 * D, :]))
        weight("w_e", [WIN + DE, HM], ((s(WIN, WIN + DE), al), a["L1_gnn_W_m1"][2 * D:2 * D + DE, :]))
        weight("w_m2", [HC, D], ((s(0, HM), al), a["L1_gnn_W_m2"]),
               ((s(HM, HM + 1), al), a["L1_gnn_b_m2"].rearrange("(a b) -> a b", a=1)))
        weight("row_m1", [P, 2 * HM], ((al, s(HM, 2 * HM)), row(a["L1_gnn_b_m1"], P)))
        weight("w_c1", [P, HC], ((bot, al), a["L1_gnn_W_c1"][0:D, :]), ((top, al), a["L1_gnn_W_c1"][D:2 * D, :]))
        weight("b_c1", [HC, 1], ((al, al), col(a["L1_gnn_b_c1"])))
        weight("w_c2", [HC, D], ((al, al), a["L1_gnn_W_c2"]))
        weight("row_bc2", [P, D], ((al, al), row(a["L1_gnn_b_c2"], P)))
        weight("fold", [P, P], ((al, al), a["fold"]))
        for k in range(2):
            weight(f"w_g{k}", [D, D], ((al, al), a[f"L2_gnn_W{k + 1}"]))
            weight(f"b_g{k}", [D, 1], ((al, al), col(a[f"L2_gnn_b{k + 1}"])))
            weight(f"gamma{k}", [D, 1], ((al, al), col(a[f"L2_gnn_gamma{k + 1}"])))
            weight(f"beta{k}", [D, 1], ((al, al), col(a[f"L2_gnn_beta{k + 1}"])))
            weight(f"w_n{k}", [P, P], *(((half, cols), a[f"L3_gnn_W{h}_{k + 1}"])
                                        for h, half in ((1, top), (2, bot)) for cols in (s(0, D), s(D, P))))

        dr = {name: nc.dram_tensor(name, shape, dt, kind="Internal").ap() for name, shape, dt in (
            ("tab0", [NP, 3 * D], F32), ("tgt0", [NW, D], F32), ("tab1", [NP, HM], F32), ("tgt1", [NW, HM], F32),
            ("tab2", [NP, D], F32), ("base_f", [1, NG], F32), ("base_i", [1, NG], I32), ("reach", [1, NG], F32),
            ("tbase_f", [1, NG * J], F32), ("tbase_i", [1, NG * J], I32), ("treach", [1, NG * J], F32),
            ("degs", [4, NP], F32), ("roots", [3, NP], F32))}
        ins = dict(a, loads=loads, early=early)

        st = Stage(nc, "zero")
        dve = st.sem("dve")
        with nc.Block() as block:
            @block.vector
            def _(v):
                step = Chain(v, dve)
                step(nc.vector.memset(w["row_ab"][:], 0.0))
                step(nc.vector.memset(w["row_m1"][:], 0.0))
                step(nc.vector.memset(w["w_m2"][:], 0.0))
        st.close()

        rounds, rounds2, rounds3 = setup(nc, m, w, ins, dr)

        layer0_nodes(nc, m, w, ins, dr)
        layer0_edges(nc, m, w, ins, dr, rounds)
        layer0_out(nc, m, w, dr)
        layer1_nodes(nc, m, w, ins, dr)
        layer1_edges(nc, m, w, ins, dr, rounds)
        layer1_out(nc, m, w, dr)
        for conv in range(2):
            layer2_in(nc, m, w, ins, dr, conv)
            sum_sources(nc, m, dr, rounds2, f"l2e{conv}", L2_PLAN)
            layer2_out(nc, m, w, dr, conv)
        for conv in range(2):
            layer3_in(nc, m, w, ins, dr, conv)
            sum_sources(nc, m, dr, rounds3, f"l3e{conv}", L3_PLAN)
            layer3_out(nc, m, w, dr, conv, out)




def kernel(**inputs):
    import numpy as np
    import concourse.bacc as bacc
    from concourse.bass_utils import run_bass_kernel_spmd

    a = {k: np.ascontiguousarray(v) for k, v in inputs.items()}
    pad = EP - E
    tiles = lambda v: np.ascontiguousarray(v.reshape(NG * J, P).T)
    src = np.pad(a.pop("src"), (0, pad), constant_values=N)
    dst = np.pad(a.pop("dst"), (0, pad), constant_values=NO_TARGET)
    ew = np.pad(a.pop("edge_weight"), (0, pad))
    ea = np.pad(a.pop("edge_attr_32"), ((0, pad), (0, 0)))
    a["x"] = np.pad(a["x"], ((0, NP - N), (0, 0)))
    a["src_t"], a["dst_t"], a["ew_t"] = tiles(src), tiles(dst), tiles(ew)
    a["dst_rows"] = np.ascontiguousarray(dst.reshape(NG, GE))
    a["fold"] = np.tile(np.eye(D, dtype=np.float32), (2, 2))
    a["ea_T"] = np.ascontiguousarray(ea.T)

    nc = bacc.Bacc("TRN2", target_bir_lowering=False, num_devices=1)
    arrays, aps = {}, {}
    for name, v in a.items():
        arrays[f"in_{name}"] = v
        aps[name] = nc.dram_tensor(f"in_{name}", v.shape, mybir.dt.from_np(v.dtype), kind="ExternalInput").ap()
    out = nc.dram_tensor("out_x", (N, D), F32, kind="ExternalOutput").ap()
    gnn_kernel(nc, aps, out)
    r = run_bass_kernel_spmd(nc, [arrays], core_ids=[0])
    return r.results[0]["out_x"]
```
